# Optimizing a Trainium2 kernel written in Bass

```python
import numpy as np
import jax
import jax.numpy as jnp

def _softmax(x, axis=-1):
    return jax.nn.softmax(x, axis=axis)

def _gelu(x):
    return jax.nn.gelu(x, approximate=True)

def _silu(x):
    return jax.nn.silu(x)

def _sigmoid(x):
    return jax.nn.sigmoid(x)

def _layernorm(x, axis=-1, eps=1e-05):
    m = jnp.mean(x, axis=axis, keepdims=True)
    v = jnp.var(x, axis=axis, keepdims=True)
    return (x - m) / jnp.sqrt(v + eps)

def _scatter_add(tgt, idx, src, axis=0):
    return tgt.at[idx].add(src)

def _segment_sum(src, seg, n):
    return jax.ops.segment_sum(src, seg, n)
kernel_name = 'mk_adaln_d1_jaxref_r8_e62d36'

def setup_inputs(seed: int=0):
    np.random.seed(seed)
    _w = jnp.asarray

    def _L0_attn_setup():
        import jax, jax.numpy as jnp
        import numpy as np
        D_MODEL = 128
        N_STATE = 128

        def _ssm_scan(A, B_x):
            a = jnp.broadcast_to(A, B_x.shape)

            def combine(c1, c2):
                a1, b1 = c1
                a2, b2 = c2
                return (a1 * a2, a2 * b1 + b2)
            _, h = jax.lax.associative_scan(combine, (a, B_x), axis=1)
            return h
        key = jax.random.key(seed)
        k_x, k_A, k_Bw, k_Bb, k_Cw, k_Cb = jax.random.split(key, 6)
        x = jax.random.normal(k_x, (8, 256, D_MODEL), dtype=jnp.float32)
        log_A = jax.random.normal(k_A, (N_STATE,), dtype=jnp.float32) * 0.1 - 1.0
        bnd_B = 1.0 / np.sqrt(D_MODEL)
        B_w = jax.random.uniform(k_Bw, (N_STATE, D_MODEL), minval=-bnd_B, maxval=bnd_B, dtype=jnp.float32)
        B_b = jax.random.uniform(k_Bb, (N_STATE,), minval=-bnd_B, maxval=bnd_B, dtype=jnp.float32)
        bnd_C = 1.0 / np.sqrt(N_STATE)
        C_w = jax.random.uniform(k_Cw, (D_MODEL, N_STATE), minval=-bnd_C, maxval=bnd_C, dtype=jnp.float32)
        C_b = jax.random.uniform(k_Cb, (D_MODEL,), minval=-bnd_C, maxval=bnd_C, dtype=jnp.float32)
        return {'x': x, 'log_A': log_A, 'B_w': B_w, 'B_b': B_b, 'C_w': C_w, 'C_b': C_b}
    _L0_attn_in = _L0_attn_setup()

    def _L0_ffn_setup():
        import jax, jax.numpy as jnp
        import numpy as np
        EMBED = 128
        HEADS = 16
        HEAD_DIM = EMBED // HEADS
        NUM_EXPERTS = 8
        TOP_K = 2
        HIDDEN = (int(2 * (4 * EMBED) / 3) + 63) // 64 * 64
        SEQ = 256
        BATCH = 2
        ROPE_BASE = 10000.0
        EPS = 1e-06

        def _rope_tables(seq_len, dim):
            inv_freq = 1.0 / ROPE_BASE ** (np.arange(0, dim, 2, dtype=np.float32) / dim)
            t = np.arange(seq_len, dtype=np.float32)
            freqs = np.einsum('i,j->ij', t, inv_freq)
            emb = np.concatenate([freqs, freqs], axis=-1)
            return (jnp.asarray(np.cos(emb)), jnp.asarray(np.sin(emb)))

        def _rotate_half(x):
            x1, x2 = jnp.split(x, 2, axis=-1)
            return jnp.concatenate([-x2, x1], axis=-1)

        def _rmsnorm(x, w):
            return x * jax.lax.rsqrt(jnp.mean(x * x, axis=-1, keepdims=True) + EPS) * w

        def _attention(x, wq, wk, wv, wo):
            B, S, _ = x.shape
            q = (x @ wq).reshape(B, S, HEADS, HEAD_DIM).transpose(0, 2, 1, 3)
            k = (x @ wk).reshape(B, S, HEADS, HEAD_DIM).transpose(0, 2, 1, 3)
            v = (x @ wv).reshape(B, S, HEADS, HEAD_DIM).transpose(0, 2, 1, 3)
            cos, sin = _rope_tables(S, HEAD_DIM)
            cos = cos[None, None]
            sin = sin[None, None]
            q = q * cos + _rotate_half(q) * sin
            k = k * cos + _rotate_half(k) * sin
            scale = HEAD_DIM ** (-0.5)
            scores = jnp.einsum('bhqd,bhkd->bhqk', q, k) * scale
            causal = jnp.triu(jnp.ones((S, S), bool), k=1)
            scores = jnp.where(causal, -jnp.inf, scores)
            attn = jax.nn.softmax(scores, axis=-1)
            out = jnp.einsum('bhqk,bhkd->bhqd', attn, v)
            out = out.transpose(0, 2, 1, 3).reshape(B, S, EMBED)
            return out @ wo

        def _moe(x, w_router, wg, wu, wd):
            B, S, E = x.shape
            xf = x.reshape(-1, E)
            logits = xf @ w_router
            probs = jax.nn.softmax(logits, axis=-1)
            topw, topi = jax.lax.top_k(probs, TOP_K)
            topw = topw / jnp.sum(topw, axis=-1, keepdims=True)
            combine = jnp.sum(jax.nn.one_hot(topi, NUM_EXPERTS, dtype=xf.dtype) * topw[..., None], axis=1)
            g = jax.nn.silu(jnp.einsum('td,xdh->txh', xf, wg))
            u = jnp.einsum('td,xdh->txh', xf, wu)
            eo = jnp.einsum('txh,xhd->txd', g * u, wd)
            out = jnp.einsum('txd,tx->td', eo, combine)
            return out.reshape(B, S, E)
        key = jax.random.key(seed)
        ks = jax.random.split(key, 12)
        s = 0.02
        return {'x': jax.random.normal(ks[0], (BATCH, SEQ, EMBED), jnp.float32), 'wq': jax.random.normal(ks[1], (EMBED, EMBED), jnp.float32) * s, 'wk': jax.random.normal(ks[2], (EMBED, EMBED), jnp.float32) * s, 'wv': jax.random.normal(ks[3], (EMBED, EMBED), jnp.float32) * s, 'wo': jax.random.normal(ks[4], (EMBED, EMBED), jnp.float32) * s, 'w_router': jax.random.normal(ks[5], (EMBED, NUM_EXPERTS), jnp.float32) * s, 'wg': jax.random.normal(ks[6], (NUM_EXPERTS, EMBED, HIDDEN), jnp.float32) * s, 'wu': jax.random.normal(ks[7], (NUM_EXPERTS, EMBED, HIDDEN), jnp.float32) * s, 'wd': jax.random.normal(ks[8], (NUM_EXPERTS, HIDDEN, EMBED), jnp.float32) * s, 'g1': jnp.ones((EMBED,), jnp.float32), 'g2': jnp.ones((EMBED,), jnp.float32)}
    _L0_ffn_in = _L0_ffn_setup()
    _L0_c = _w((lambda *s: np.random.randn(*s).astype(np.float32) * 0.05)(16, 128))
    _L0_wmod = _w((lambda *s: np.random.randn(*s).astype(np.float32) * 0.05)(128, 6 * 128) * 128 ** (-0.5))
    _d = {'L0_attn_x': _L0_attn_in['x'], 'L0_attn_log_A': _L0_attn_in['log_A'], 'L0_attn_B_w': _L0_attn_in['B_w'], 'L0_attn_B_b': _L0_attn_in['B_b'], 'L0_attn_C_w': _L0_attn_in['C_w'], 'L0_attn_C_b': _L0_attn_in['C_b'], 'L0_ffn_wq': _L0_ffn_in['wq'], 'L0_ffn_wk': _L0_ffn_in['wk'], 'L0_ffn_wv': _L0_ffn_in['wv'], 'L0_ffn_wo': _L0_ffn_in['wo'], 'L0_ffn_w_router': _L0_ffn_in['w_router'], 'L0_ffn_wg': _L0_ffn_in['wg'], 'L0_ffn_wu': _L0_ffn_in['wu'], 'L0_ffn_wd': _L0_ffn_in['wd'], 'L0_ffn_g1': _L0_ffn_in['g1'], 'L0_ffn_g2': _L0_ffn_in['g2'], 'L0_c': _L0_c, 'L0_wmod': _L0_wmod}
    _x0 = _d['L0_attn_x']
    _d['L0_attn_x'] = jax.random.normal(jax.random.fold_in(jax.random.key(seed), 1), (16, 256, 128), dtype=_x0.dtype)
    del _x0
    return _d

def reference(L0_attn_x, L0_attn_log_A, L0_attn_B_w, L0_attn_B_b, L0_attn_C_w, L0_attn_C_b, L0_ffn_wq, L0_ffn_wk, L0_ffn_wv, L0_ffn_wo, L0_ffn_w_router, L0_ffn_wg, L0_ffn_wu, L0_ffn_wd, L0_ffn_g1, L0_ffn_g2, L0_c, L0_wmod):

    def _L0_attn_ref(x, log_A, B_w, B_b, C_w, C_b):
        import jax, jax.numpy as jnp
        import numpy as np
        D_MODEL = 128
        N_STATE = 128

        def _ssm_scan(A, B_x):
            a = jnp.broadcast_to(A, B_x.shape)

            def combine(c1, c2):
                a1, b1 = c1
                a2, b2 = c2
                return (a1 * a2, a2 * b1 + b2)
            _, h = jax.lax.associative_scan(combine, (a, B_x), axis=1)
            return h
        A = jax.nn.sigmoid(log_A)
        B_x = jnp.einsum('btd,nd->btn', x, B_w) + B_b
        h = _ssm_scan(A, B_x)
        y = jnp.einsum('btn,dn->btd', h, C_w) + C_b
        return y

    def _L0_ffn_ref(x, wq, wk, wv, wo, w_router, wg, wu, wd, g1, g2):
        import jax, jax.numpy as jnp
        import numpy as np
        EMBED = 128
        HEADS = 16
        HEAD_DIM = EMBED // HEADS
        NUM_EXPERTS = 8
        TOP_K = 2
        HIDDEN = (int(2 * (4 * EMBED) / 3) + 63) // 64 * 64
        SEQ = 256
        BATCH = 2
        ROPE_BASE = 10000.0
        EPS = 1e-06

        def _rope_tables(seq_len, dim):
            inv_freq = 1.0 / ROPE_BASE ** (np.arange(0, dim, 2, dtype=np.float32) / dim)
            t = np.arange(seq_len, dtype=np.float32)
            freqs = np.einsum('i,j->ij', t, inv_freq)
            emb = np.concatenate([freqs, freqs], axis=-1)
            return (jnp.asarray(np.cos(emb)), jnp.asarray(np.sin(emb)))

        def _rotate_half(x):
            x1, x2 = jnp.split(x, 2, axis=-1)
            return jnp.concatenate([-x2, x1], axis=-1)

        def _rmsnorm(x, w):
            return x * jax.lax.rsqrt(jnp.mean(x * x, axis=-1, keepdims=True) + EPS) * w

        def _attention(x, wq, wk, wv, wo):
            B, S, _ = x.shape
            q = (x @ wq).reshape(B, S, HEADS, HEAD_DIM).transpose(0, 2, 1, 3)
            k = (x @ wk).reshape(B, S, HEADS, HEAD_DIM).transpose(0, 2, 1, 3)
            v = (x @ wv).reshape(B, S, HEADS, HEAD_DIM).transpose(0, 2, 1, 3)
            cos, sin = _rope_tables(S, HEAD_DIM)
            cos = cos[None, None]
            sin = sin[None, None]
            q = q * cos + _rotate_half(q) * sin
            k = k * cos + _rotate_half(k) * sin
            scale = HEAD_DIM ** (-0.5)
            scores = jnp.einsum('bhqd,bhkd->bhqk', q, k) * scale
            causal = jnp.triu(jnp.ones((S, S), bool), k=1)
            scores = jnp.where(causal, -jnp.inf, scores)
            attn = jax.nn.softmax(scores, axis=-1)
            out = jnp.einsum('bhqk,bhkd->bhqd', attn, v)
            out = out.transpose(0, 2, 1, 3).reshape(B, S, EMBED)
            return out @ wo

        def _moe(x, w_router, wg, wu, wd):
            B, S, E = x.shape
            xf = x.reshape(-1, E)
            logits = xf @ w_router
            probs = jax.nn.softmax(logits, axis=-1)
            topw, topi = jax.lax.top_k(probs, TOP_K)
            topw = topw / jnp.sum(topw, axis=-1, keepdims=True)
            combine = jnp.sum(jax.nn.one_hot(topi, NUM_EXPERTS, dtype=xf.dtype) * topw[..., None], axis=1)
            g = jax.nn.silu(jnp.einsum('td,xdh->txh', xf, wg))
            u = jnp.einsum('td,xdh->txh', xf, wu)
            eo = jnp.einsum('txh,xhd->txd', g * u, wd)
            out = jnp.einsum('txd,tx->td', eo, combine)
            return out.reshape(B, S, E)
        h = x + _attention(_rmsnorm(x, g1), wq, wk, wv, wo)
        y = h + _moe(_rmsnorm(h, g2), w_router, wg, wu, wd)
        return y
    x = L0_attn_x
    mod = (_silu(L0_c) @ L0_wmod).reshape(L0_c.shape[0], 6, 1, -1)
    sa, ca, ga, sb, cb, gb = (mod[:, 0], mod[:, 1], mod[:, 2], mod[:, 3], mod[:, 4], mod[:, 5])
    ga = (2 * (ga >= 0) - 1) * jnp.maximum(jnp.abs(ga), 0.25)
    gb = (2 * (gb >= 0) - 1) * jnp.maximum(jnp.abs(gb), 0.25)
    h = _layernorm(x, axis=-1) * (1 + ca) + sa
    x = x + ga * _L0_attn_ref(h, L0_attn_log_A, L0_attn_B_w, L0_attn_B_b, L0_attn_C_w, L0_attn_C_b)
    h = _layernorm(x, axis=-1) * (1 + cb) + sb
    x = x + gb * _L0_ffn_ref(h, L0_ffn_wq, L0_ffn_wk, L0_ffn_wv, L0_ffn_wo, L0_ffn_w_router, L0_ffn_wg, L0_ffn_wu, L0_ffn_wd, L0_ffn_g1, L0_ffn_g2)
    return x

_drawn_inputs = setup_inputs


def setup_inputs(seed=0):
    import zlib

    import numpy as np

    out = dict(_drawn_inputs(seed))
    spreads = {'L0_ffn_g1': (1.0, 0.6), 'L0_ffn_g2': (1.0, 0.6)}
    factors = {'L0_attn_log_A': 64.0,
     'L0_attn_B_b': 5.892,
     'L0_attn_C_b': 3.946,
     'L0_ffn_wq': 8.0,
     'L0_ffn_wk': 8.0,
     'L0_ffn_wv': 8.0,
     'L0_ffn_wo': 8.0,
     'L0_ffn_w_router': 8.0,
     'L0_ffn_wg': 8.0,
     'L0_ffn_wu': 8.0,
     'L0_ffn_wd': 8.0}
    for name, (base, spread) in spreads.items():
        noise = np.random.default_rng([zlib.crc32(name.encode()), seed]).standard_normal(out[name].shape)
        drawn = base * np.exp(spread * noise) if base else spread * noise
        out[name] = jnp.asarray(drawn.astype(out[name].dtype))
    for name, factor in factors.items():
        out[name] = (out[name] * factor).astype(out[name].dtype)
    return out
```

```python
from contextlib import ExitStack

import numpy as np

import concourse.bass as bass
from concourse import mybir

F32 = mybir.dt.float32
BF16 = mybir.dt.bfloat16
I32 = mybir.dt.int32
U32 = mybir.dt.uint32
ALU = mybir.AluOpType
ACT = mybir.ActivationFunctionType
AX_X = mybir.AxisListType.X

P = 128
NB = 16
S = 256
QB = S // P
TT = NB * QB
H = 16
DH = P // H
NE = 8
HID = 384
HC = HID // P
EW = 2 * HID + HC * P
REG = NB * S + P
NT = 2 * NB * S // P + NE
NROW = NE * REG + 4 * P
LN_EPS, RMS_EPS = 1e-5, 1e-6
SCALE = float(DH) ** -0.5
ROWS = 64
Q_SLOTS = ((0, 2, 1, 3), (1, 0, 5, 2), (2, 1, 1, 1))
K_SLOTS = ((0, 0, 1, 3), (1, 3, 2, 2), (2, 4, 1, 1))
AUG = 6
NEG = -1.0e30
N_W = 14
SLOTS = 12 + H

C_ID, C_COS, C_SIN, C_UP, C_MASK, C_IOTA, C_OFF, C_ROW = 0, 128, 384, 640, 768, 896, 904, 912
C_TILE, C_DUMMY, C_KAUG, C_N = 920, 992, 1064, 1080
M_GA, M_CBGA, M_CB1, M_SB, M_GB = range(5)


def constants():
    c = np.zeros((P, C_N), np.float32)
    c[:, C_ID:C_ID + P] = np.eye(P)
    inv = 1.0 / 10000.0 ** (np.arange(0, DH, 2, dtype=np.float32) / DH)
    f = np.einsum('i,j->ij', np.arange(S, dtype=np.float32), inv)
    emb = np.concatenate([f, f], axis=-1)
    c[:, C_COS:C_COS + S] = np.tile(np.cos(emb).T, (H, 1))
    c[:, C_SIN:C_SIN + S] = np.tile(np.sin(emb).T, (H, 1))
    c[:, C_UP:C_UP + P] = np.triu(np.ones((P, P)), 1)
    c[:, C_MASK:C_MASK + P] = np.triu(np.full((P, P), NEG), 1)
    c[:, C_IOTA:C_IOTA + NE] = np.arange(NE)
    c[:, C_OFF:C_OFF + NE] = np.arange(NE) * REG
    c[:, C_ROW] = np.arange(P)
    c[:, C_TILE:C_TILE + NT] = np.arange(NT)
    c[:, C_DUMMY:C_DUMMY + NT] = np.arange(NT) % 4 * P
    c[:, C_KAUG] = np.arange(P) % DH < 3
    return c


class Steps:

    def __init__(self, sem, names, first=0):
        self.sem, self.names, self.first = sem, names.split(), first

    def at(self, b, name):
        return b * len(self.names) + (self.names.index(name) + 1 + self.first)


def build(nc, x, log_A, B_w, B_b, C_w, C_b, wq, wk, wv, wo, w_router, wg, wu, wd, g1, g2, c, wmod, consts, out):
    ctx = ExitStack()
    with ctx:
        def sb(name, shape, dt=F32):
            return ctx.enter_context(nc.sbuf_tensor(name, shape, dt))

        def sem(name):
            return ctx.enter_context(nc.semaphore(name))

        mod_rows = nc.dram_tensor("mod_rows", [NB, 5 * P], F32).ap()
        q_stack_d = nc.dram_tensor("q_stack_d", [2, H, ROWS, S], BF16).ap()
        k_stack_d = nc.dram_tensor("k_stack_d", [2, H, ROWS, S], BF16).ap()
        routed = nc.dram_tensor("routed", [NROW, P], F32).ap()
        expert_out = nc.dram_tensor("expert_out", [NT * P, P], F32).ap()

        cst = sb("cst", [P, C_N])
        ident = cst[:, C_ID:C_ID + P]
        ident_b = sb("ident_b", [P, P], BF16)
        upper_b = sb("upper_b", [P, P], BF16)
        ones_b = sb("ones_b", [P, P], BF16)
        mask_b = sb("mask_b", [P, 4, P], BF16)
        zeros = sb("zeros", [P, P])
        zeros_b = sb("zeros_b", [P, S], BF16)
        kaug_b = sb("kaug_b", [P, 2 * S], BF16)
        neg_half = sb("neg_half", [P, 2])
        w_in = sb("w_in", [P, 2, P])
        bwT = sb("bwT", [P, P])
        cwT = sb("cwT", [P, P])
        cols = sb("cols", [P, 4])
        decay = sb("decay", [P, 1])
        decay_b = sb("decay_b", [P, S])
        wqkv = sb("wqkv", [P, 3, P])
        w_rot = sb("w_rot", [P, 2, P])
        wo_s = sb("wo_s", [P, P])
        wr_s = sb("wr_s", [P, NE])
        g2_b = sb("g2_b", [P, P])
        experts = sb("experts", [P, NE * EW])
        c_T = sb("c_T", [P, NB])
        c_e = sb("c_e", [P, NB])
        silu_T = sb("silu_T", [P, NB])
        wmod_s = sb("wmod_s", [P, 6 * P])
        mod_T = sb("mod_T", [P, 6, NB])
        mod_r = sb("mod_r", [NB, 6 * P])
        row_s = sb("row_s", [NB, 5 * P])
        cb_r = sb("cb_r", [NB, P])
        sgn = sb("sgn", [NB, 2, P])

        X = sb("X", [P, 2, QB, P])
        MB = sb("MB", [P, 2, 4 * P])
        GB = sb("GB", [P, 2, P])
        st = sb("st", [P, QB, 6])
        mv = sb("mv", [P, QB, 2])
        rs = sb("rs", [P, QB])
        nrm = sb("nrm", [P, QB, P])
        hT = sb("hT", [P, S])
        bx = sb("bx", [P, S])
        hs = sb("hs", [P, S])
        xg = sb("xg", [P, QB, P])
        tmp = sb("tmp", [P, QB, P])
        X1 = sb("X1", [P, 2, QB, P])
        H2 = sb("H2", [P, 2, QB, P])
        sq = sb("sq", [P, QB, P])
        modc = sb("modc", [P, 2, 2])
        ve = sb("ve", [P, QB])
        ve2 = sb("ve2", [P, QB])
        tiny = sb("tiny", [P, 1])
        qaug_b = sb("qaug_b", [P, 2 * S], BF16)
        ones_f = sb("ones_f", [P, NE])
        ss = sb("ss", [P, QB])
        xnT = sb("xnT", [P, S])
        r_c = sb("r_c", [P, 2, S])
        r_s = sb("r_s", [P, 2, S])
        qk = sb("qk", [P, 2, S])
        part = sb("part", [P, 3, 2, S], BF16)
        QST = sb("QST", [P, 2, H // 2, S], BF16)
        KST = sb("KST", [P, 2, H, S], BF16)
        VA = sb("VA", [P, 2, QB, H, 32])

        MX = sb("MX", [P, QB, H])
        rem = sb("rem", [P, QB, H])
        nmp = sb("nmp", [P, QB, 8, H], BF16)
        nmT = sb("nmT", [3 * H, S], BF16)
        PT = sb("PT", [P, 4, 3 * P])
        OT = sb("OT", [P, 4, S])
        rc = sb("rc", [P, QB, H])
        ON = sb("ON", [P, QB, P])
        ONT = sb("ONT", [P, S])
        h3 = sb("h3", [P, QB, P])
        gh = sb("gh", [P, QB, P])
        base = sb("base", [P, TT, P])
        sq2 = sb("sq2", [P, QB, P])
        ss2 = sb("ss2", [P, QB])
        rs2 = sb("rs2", [P, QB])
        xn2 = sb("xn2", [P, 2, QB, P])
        xn2T = sb("xn2T", [P, S])
        lg = sb("lg", [P, QB, NE])
        mx8 = sb("mx8", [P, QB, 8])
        ix8 = sb("ix8", [P, QB, 8], U32)
        ixf = sb("ixf", [P, QB, 2])
        dl = sb("dl", [P, QB])
        el = sb("el", [P, QB])
        e1 = sb("e1", [P, QB])
        w12 = sb("w12", [P, QB, 2])
        oh = sb("oh", [P, QB, 2, NE])
        ohs = sb("ohs", [P, QB, NE], BF16)
        carry = sb("carry", [P, NE])
        pall = sb("pall", [P, QB, NE])
        prod = sb("prod", [P, QB, 2, NE])
        posf = sb("posf", [P, QB, 2])
        posi = sb("posi", [P, 2, QB * 2], I32)
        POS = sb("POS", [P, TT * 2])
        WGT = sb("WGT", [P, TT * 2])

        padf = sb("padf", [P, NE])
        padi = sb("padi", [P, NE], I32)
        cnt = sb("cnt", [P, NE])
        cnti = sb("cnti", [P, NE], I32)
        cum = sb("cum", [P, NE])
        delta = sb("delta", [P, NE])
        shift = sb("shift", [P, NE])
        above = sb("above", [P, TT * 2, NE])
        moved = sb("moved", [P, TT * 2])
        GIDX = sb("GIDX", [P, TT * 2], I32)
        past = sb("past", [1, NT, NE])
        eidx = sb("eidx", [1, NT])
        first = sb("first", [1, NT])
        valid = sb("valid", [1, NT])
        tab = sb("tab", [1, 2, NT], I32)
        xin = sb("xin", [P, 2, P])
        xT = sb("xT", [P, 2, P])
        sg = sb("sg", [P, 2, HID])
        hm = sb("hm", [P, 2, HID])
        hmT = sb("hmT", [P, 2, HID])
        eo = sb("eo", [P, 2, P])
        got = sb("got", [P, 2, QB, 2, P])
        gidx = sb("gidx", [P, 2, 4], I32)
        wl = sb("wl", [P, 2, 4])
        res = sb("res", [P, 2, QB, P])

        banks = [ctx.enter_context(nc.psum_tensor(f"bank{i}", [P, 512], F32)) for i in range(8)]
        PF = banks[0:2]
        PA = banks[2:4]
        PS = banks[4:6]
        PO = banks[6:8]

        s_cst = sem("s_cst")
        s_w = sem("s_w")
        s_exp = sem("s_exp")
        s_scr = sem("s_scr")
        s_modrow = sem("s_modrow")
        s_x = [sem("s_x0"), sem("s_x1")]
        s_mb = [sem("s_mb0"), sem("s_mb1")]
        s_gt = [sem("s_gt0"), sem("s_gt1")]
        s_stw = sem("s_stw")
        s_stk = [sem("s_stk0"), sem("s_stk1")]
        s_nm = sem("s_nm")
        s_sc = [sem("s_sc0"), sem("s_sc1")]
        SU = {e: Steps(sem("setup_" + e), n) for e, n in dict(
            pe="bwcw modT modr", act="exp_a exp_c", pool="zero ones",
            dve="aug ea decay decb ec rc silu wT rot modT modr sgn2 sgn abs guard castb carry").items()}
        FR = {e: Steps(sem("front_" + e), n) for e, n in dict(
            pe="nT bx y xnT qk v",
            act="hT bx ss xnT ph va pm",
            pool="rs1 xg rs2 rs3",
            dve="st mv ve n1 scan ty x1 st2 mv2 ve2 n2 h2a h2 vs xn rc rs qk r1 pl").items()}
        AT = {e: Steps(sem("attn_" + e), n) for e, n in dict(
            pe=" ".join([f"a{i}" for i in range(12)] + ["nmT"] + [f"s{h} pv{h - 2}" if h >= 2 else f"s{h}" for h in range(H)]
                        + [f"pv{H - 2} pv{H - 1}"]),
            act="nmT " + " ".join(f"e{h}" for h in range(H)),
            pool=" ".join(f"c{h}" for h in range(H)),
            dve=" ".join(f"m{i}" for i in range(12)) + " nh rem nm rem2 nl").items()}
        TL = {e: Steps(sem("tail_" + e), n) for e, n in dict(
            pe="oT onT wo xT lg rank",
            act="OT onT ss xT el",
            pool="gh base rs",
            dve="rc on h3 vs xn lg mx ix ixf dl e1 w1 w2 oh ohs pall carry prod posf posi POS").items()}
        moe = {n: sem("moe_" + n) for n in "pe_xT pe_gu pe_tr pe_dn act_xT act_sg dve_hm dve_hT dve_eo".split()}
        RT = Steps(sem("tables"), "padf cnt cnt2 cnti nt cum past eidx pastn first inside valid jrow spare dummy sum row col tab startt delta shift above moves moved pos GIDX")
        LA = Steps(sem("last"), "idx a b g out")
        s_tab = sem("s_tab")
        s_idx = sem("s_idx")
        s_pad = sem("s_pad")
        s_in = [sem("s_in0"), sem("s_in1")]
        s_st = [sem("s_st0"), sem("s_st1")]
        s_got = [sem("s_got0"), sem("s_got1")]
        s_gb = [sem("s_gb0"), sem("s_gb1")]
        s_out = [sem("s_out0"), sem("s_out1")]
        PA_b = PA[0][:, :].bitcast(BF16)

        def run_periods(eng, period):
            period(0, None, None, 0)
            period(1, 0, None, 1)
            period(2, 1, 0, 0)
            period(3, 2, 1, 1)
            with eng.Fori(2, NB // 2) as j:
                period(2 * j, 2 * j - 1, 2 * j - 2, 0)
                period(2 * j + 1, 2 * j, 2 * j - 1, 1)
            period(None, NB - 1, NB - 2, 0)
            period(None, None, NB - 1, 1)

        def run_tiles(eng, tile):
            tile(-1, 1, gu=False, tr=False, dn=False)
            tile(0, 0, tr=False, dn=False)
            tile(1, 1, dn=False)
            tile(2, 0)
            tile(3, 1)
            with eng.Fori(2, NT // 2 - 1) as j:
                tile(2 * j, 0)
                tile(2 * j + 1, 1)
            tile(NT - 2, 0)
            tile(NT - 1, 1, xt=False)
            tile(NT, 0, xt=False, gu=False)
            tile(NT + 1, 1, xt=False, gu=False, tr=False)


        def bc(ap, axis, n):
            a = ap.unsqueeze(axis)
            shape = list(a.shape)
            shape[axis] = n
            return a.to_broadcast(shape)

        def old(b, k):
            return not isinstance(b, int) or b >= k

        passed = {}

        def alone(eng):
            if id(eng) not in passed:
                passed[id(eng)] = sem(f"passed{len(passed)}")
            eng.sem_inc(passed[id(eng)], 1)

        block = ctx.enter_context(nc.Block())

        @block.sync
        def _(sp):
            sp.dma_start(cst[:, :], consts).then_inc(s_cst, 16)
            sp.dma_start(w_in[:, 0, :], B_w).then_inc(s_w, 16)
            sp.dma_start(w_in[:, 1, :], C_w).then_inc(s_w, 16)
            sp.dma_start(wmod_s[:, :], wmod).then_inc(s_w, 16)
            with nc.allow_non_contiguous_dma(reason="small transposed loads"):
                sp.dma_start(c_T[:, :], c.rearrange("b d -> d b")).then_inc(s_w, 16)
                for i, v in enumerate((log_A, B_b, g1)):
                    sp.dma_start(cols[:, i:i + 1], v.rearrange("(d a) -> d a", a=1)).then_inc(s_w, 16)
            for i, w in enumerate((wq, wk, wv)):
                sp.dma_start(wqkv[:, i, :], w).then_inc(s_w, 16)
            sp.dma_start(wo_s[:, :], wo).then_inc(s_w, 16)
            sp.dma_start(wr_s[:, :], w_router).then_inc(s_w, 16)
            sp.dma_start(g2_b[:, :], g2.partition_broadcast(P)).then_inc(s_w, 16)
            sp.dma_start(cb_r[:, :], C_b.partition_broadcast(NB)).then_inc(s_w, 16)
            sp.wait_ge(SU["dve"].sem, SU["dve"].at(0, "aug"))
            for p in range(2):
                for dst, src in ((k_stack_d, kaug_b), (q_stack_d, qaug_b)):
                    sp.dma_start(dst[p].rearrange("h (d s) k -> (h d) s k", s=8)[:, AUG:8, :],
                                 src[:, :].rearrange("r (s k) -> r s k", s=2)).then_inc(s_scr, 16)
            for i in range(4):
                sp.dma_start(routed[NE * REG + i * P:NE * REG + (i + 1) * P, :], zeros[:, :]).then_inc(s_scr, 16)
            sp.wait_ge(SU["dve"].sem, SU["dve"].at(0, "castb"))
            sp.dma_start(mod_rows, row_s[:, :]).then_inc(s_modrow, 16)
            sp.wait_ge(s_modrow, 16)
            sp.wait_ge(s_scr, 16 * 8)

            def front_load(b, p):
                if old(b, 2):
                    sp.wait_ge(FR["dve"].sem, FR["dve"].at(b - 2, "st"))
                    alone(sp)
                    sp.wait_ge(FR["pool"].sem, FR["pool"].at(b - 2, "xg"))
                    alone(sp)
                    sp.wait_ge(FR["dve"].sem, FR["dve"].at(b - 2, "n1"))
                    alone(sp)
                sp.dma_start(X[:, p, :, :], x[bass.ds(b, 1), :, :].rearrange("a (t p) d -> p (a t) d", p=P)).then_inc(s_x[p], 16)
                if old(b, 2):
                    sp.wait_ge(FR["dve"].sem, FR["dve"].at(b - 2, "h2"))
                    alone(sp)
                sp.dma_start(MB[:, p, :], mod_rows[bass.ds(b, 1), 0:4 * P].to_broadcast([P, 4 * P])).then_inc(s_mb[p], 16)

            def gate_load(b, p):
                if old(b, 2):
                    sp.wait_ge(TL["pool"].sem, TL["pool"].at(b - 2, "gh"))
                    alone(sp)
                sp.dma_start(GB[:, p, :], mod_rows[bass.ds(b, 1), M_GB * P:].to_broadcast([P, P])).then_inc(s_gt[p], 16)

            def front_stack(b, p):
                if old(b, 2):
                    sp.wait_ge(s_stk[p], 24 * (b - p))
                    alone(sp)
                    sp.wait_ge(AT["pe"].sem, AT["pe"].at(b - 2, f"pv{H - 1}"))
                    alone(sp)
                for i, (e, name) in enumerate((("act", "ph"), ("act", "pm"), ("dve", "pl"))):
                    sp.wait_ge(FR[e].sem, FR[e].at(b, name))
                    alone(sp)
                    for qk_i, (slots, dst) in enumerate(((Q_SLOTS, q_stack_d), (K_SLOTS, k_stack_d))):
                        _, slot, step, n = slots[i]
                        to = dst[p].rearrange("h (d s) k -> (h d) s k", s=8)[:, slot:slot + step * (n - 1) + 1:step, :]
                        sp.dma_start(to, bc(part[:, i, qk_i, :], 1, n)).then_inc(s_stw, 16)
                sp.wait_ge(s_stw, 96 * b + 96)
                alone(sp)
                sp.dma_start(QST[:, p, :, :], q_stack_d[p].rearrange("(t j) r k -> (j r) t k", j=2)).then_inc(s_stk[p], 16)
                for j in range(2):
                    sp.dma_start(KST[64 * j:64 * j + 64, p, j::2, :],
                                 k_stack_d[p].rearrange("(t j) r k -> j r t k", j=2)[j]).then_inc(s_stk[p], 16)

            def attn_max(a, p):
                sp.wait_ge(AT["act"].sem, AT["act"].at(a, "nmT"))
                alone(sp)
                for j in range(2):
                    for i in range(3):
                        r = 64 * j + 8 * i + AUG
                        sp.dma_start(QST[r:r + 1, p, :, :], nmT[16 * i + j:16 * (i + 1):2, :]).then_inc(s_nm, 16)

            def period(f, a, t, pf):
                if f is not None:
                    front_load(f, pf)
                if a is not None:
                    attn_max(a, 1 - pf)
                if f is not None:
                    gate_load(f, pf)
                    front_stack(f, pf)

            run_periods(sp, period)

            sp.wait_ge(s_tab, 3)
            alone(sp)
            sp.wait_ge(s_pad, 16 * NE)
            alone(sp)

            def tile_load(T, p):
                row = sp.value_load(tab[0:1, 0, bass.ds(T, 1)], min_val=0, max_val=NROW - P)
                if old(T, 2):
                    sp.wait_ge(moe["pe_xT"], T - 2 + 1)
                    alone(sp)
                sp.dma_start(xin[:, p, :], routed[bass.ds(row, P), :]).then_inc(s_in[p], 16)

            tile_load(0, 0)
            tile_load(1, 1)
            with sp.Fori(1, NT // 2) as j:
                tile_load(2 * j, 0)
                tile_load(2 * j + 1, 1)

            def last_load(b, p):
                if old(b, 2):
                    sp.wait_ge(LA.sem, LA.at(b - 2, "g"))
                    alone(sp)
                else:
                    sp.wait_ge(TL["pool"].sem, TL["pool"].at(NB - 1, "gh"))
                    alone(sp)
                sp.dma_start(GB[:, p, :], mod_rows[bass.ds(b, 1), M_GB * P:].to_broadcast([P, P])).then_inc(s_gb[p], 16)
                if old(b, 2):
                    last_store(b - 2, p)

            def last_store(b, p):
                sp.wait_ge(LA.sem, LA.at(b, "out"))
                alone(sp)
                sp.dma_start(out[bass.ds(b, 1), :, :].rearrange("a (t p) d -> p (a t) d", p=P), res[:, p, :, :]).then_inc(s_out[p], 16)

            last_load(0, 0)
            last_load(1, 1)
            with sp.Fori(1, NB // 2) as j:
                last_load(2 * j, 0)
                last_load(2 * j + 1, 1)
            last_store(NB - 2, 0)
            last_store(NB - 1, 1)
            for p in range(2):
                sp.wait_ge(s_out[p], 16 * NB // 2)
                alone(sp)

        @block.gpsimd
        def _(pool):
            pool.memset(zeros[:, :], 0.0)
            pool.memset(neg_half[:, :], -0.5)
            pool.memset(KST[:, :, :, :], 0.0)
            pool.memset(VA[:, :, :, :, :], 0.0)
            pool.memset(qaug_b[:, :], 0.0).then_inc(SU["pool"].sem, 1)
            pool.wait_ge(SU["pool"].sem, 1)
            pool.memset(VA[:, :, :, :, DH:DH + 1], 1.0).then_inc(SU["pool"].sem, 1)

            def rstd(stage, name, dve, src, dst, b):
                pool.wait_ge(dve[0].sem, dve[0].at(b, dve[1]))
                pool.tensor_tensor(dst, src, neg_half[:, :], ALU.pow).then_inc(stage.sem, 1)

            def front(b, p, level):
                if level == 1:
                    rstd(FR["pool"], "rs1", (FR["dve"], "ve"), ve[:, :], rs[:, :], b)
                elif level == 8:
                    pool.wait_ge(s_mb[p], 8 * (b - p) + 16)
                    pool.wait_ge(s_x[p], 8 * (b - p) + 16)
                    if old(b, 1):
                        pool.wait_ge(FR["dve"].sem, FR["dve"].at(b - 1, "x1"))
                    pool.tensor_tensor(xg[:, :, :], X[:, p, :, :], bc(MB[:, p, M_CBGA * P:(M_CBGA + 1) * P], 1, QB),
                                       ALU.add).then_inc(FR["pool"].sem, 1)
                elif level == 10:
                    rstd(FR["pool"], "rs2", (FR["dve"], "ve2"), ve[:, :], rs[:, :], b)
                elif level == 14:
                    rstd(FR["pool"], "rs3", (FR["dve"], "vs"), ve[:, :], rs[:, :], b)

            def attn_head(a, p, h):
                pool.wait_ge(AT["act"].sem, AT["act"].at(a, f"e{h}"))
                alone(pool)
                d = PT[:, h % 4, :].rearrange("p (x q) -> p x q", x=3)[:, 0:3:2, :]
                pool.affine_select(out=d, in_=d, compare_op=ALU.is_ge, fill=0.0, base=0,
                                   pattern=[[0, 2], [1, P]], channel_multiplier=-1).then_inc(AT["pool"].sem, 1)

            def tail(t, p, level):
                if level == 9:
                    pool.wait_ge(s_gt[p], 8 * (t - p) + 16)
                    pool.wait_ge(TL["dve"].sem, TL["dve"].at(t, "h3"))
                    pool.tensor_tensor(gh[:, :, :], h3[:, :, :], bc(GB[:, p, :], 1, QB),
                                       ALU.mult).then_inc(TL["pool"].sem, 1)
                    pool.wait_ge(TL["pool"].sem, TL["pool"].at(t, "gh"))
                    pool.tensor_tensor(base[:, bass.ds(t * QB, QB), :], gh[:, :, :], X1[:, p, :, :],
                                       ALU.add).then_inc(TL["pool"].sem, 1)
                elif level == 11:
                    rstd(TL["pool"], "rs", (TL["dve"], "vs"), ve2[:, :], rs2[:, :], t)
                elif level == 25:
                    pool.wait_ge(TL["dve"].sem, TL["dve"].at(t, "posi"))
                    alone(pool)
                    for i in range(QB):
                        for k in range(2):
                            pool.indirect_dma_start(
                                routed[:, :], bass.IndirectOffsetOnAxis(ap=posi[:, p, 2 * i + k:2 * i + k + 1], axis=0),
                                xn2[:, p, i, :], None).then_inc(s_sc[p], 16)

            def period(f, a, t, pf):
                for slot in range(SLOTS):
                    if a is not None and slot >= 12:
                        attn_head(a, 1 - pf, slot - 12)
                    if t is not None:
                        tail(t, pf, slot)
                    if f is not None:
                        front(f, pf, slot)

            run_periods(pool, period)

            pool.wait_ge(s_idx, 1)
            for e in range(NE):
                pool.indirect_dma_start(routed[:, :], bass.IndirectOffsetOnAxis(ap=padi[:, e:e + 1], axis=0),
                                        zeros[:, :], None).then_inc(s_pad, 16)
            for p in range(2):
                pool.wait_ge(s_sc[p], 64 * NB // 2)
            pool.sem_inc(s_tab, 1)
            pool.wait_ge(s_tab, 3)

            def tile_store(T, p):
                pool.wait_ge(moe["dve_eo"], T + 1)
                pool.dma_start(expert_out[bass.ds(T * P, P), :], eo[:, p, :]).then_inc(s_st[p], 16)

            with pool.Fori(0, NT // 2) as j:
                tile_store(2 * j, 0)
                tile_store(2 * j + 1, 1)
            for p in range(2):
                pool.wait_ge(s_st[p], 16 * NT // 2)

            def gather(b, p):
                pool.wait_ge(LA.sem, LA.at(b, "idx"))
                alone(pool)
                for i in range(QB):
                    for k in range(2):
                        pool.indirect_dma_start(
                            got[:, p, i, k, :], None, expert_out[:, :],
                            bass.IndirectOffsetOnAxis(ap=gidx[:, p, 2 * i + k:2 * i + k + 1], axis=0)).then_inc(s_got[p], 16)

            with pool.Fori(0, NB // 2) as j:
                gather(2 * j, 0)
                gather(2 * j + 1, 1)

        @block.scalar
        def _(act):
            A, B, C = FR["act"], AT["act"], TL["act"]
            wg_v, wu_v = wg.rearrange("e d h -> d e h"), wu.rearrange("e d h -> d e h")
            ex = experts[:, :].rearrange("p (e n) -> p e n", e=NE)
            act.dma_start(ex[:, :, 0:HID], wg_v).then_inc(s_exp, 16)
            act.dma_start(ex[:, :, HID:2 * HID], wu_v).then_inc(s_exp, 16)
            for e in range(NE):
                act.dma_start(ex[:, e, 2 * HID:].rearrange("p (c d) -> p c d", c=HC),
                              wd[e].rearrange("(c p) d -> p c d", p=P)).then_inc(s_exp, 16)
            act.wait_ge(s_w, 16 * N_W)
            act.activation(decay[:, :], cols[:, 0:1], ACT.Exp, scale=-1.0).then_inc(SU["act"].sem, 1)
            act.activation(c_e[:, :], c_T[:, :], ACT.Exp, scale=-1.0).then_inc(SU["act"].sem, 1)
            act.wait_ge(SU["dve"].sem, SU["dve"].at(0, "carry"))

            def front(b, p, level):
                if level == 4:
                    act.wait_ge(FR["pe"].sem, FR["pe"].at(b, "nT"))
                    act.activation(hT[:, :], PF[0][:, 0:S], ACT.Identity, scale=modc[:, p, 0:1],
                                   bias=modc[:, p, 1:2]).then_inc(A.sem, 1)
                elif level == 6:
                    act.wait_ge(FR["pe"].sem, FR["pe"].at(b, "bx"))
                    if old(b, 1):
                        act.wait_ge(FR["dve"].sem, FR["dve"].at(b - 1, "scan"))
                    act.activation(bx[:, :], PF[1][:, 0:S], ACT.Identity, bias=cols[:, 1:2]).then_inc(A.sem, 1)
                elif level == 13:
                    act.wait_ge(FR["dve"].sem, FR["dve"].at(b, "h2"))
                    for i in range(QB):
                        r = act.activation(sq[:, i, :], H2[:, p, i, :], ACT.Square, accum_out=ss[:, i:i + 1])
                    r.then_inc(A.sem, 1)
                elif level == 17:
                    act.wait_ge(FR["pe"].sem, FR["pe"].at(b, "xnT"))
                    act.activation(xnT[:, :], PF[1][:, 0:S], ACT.Copy, scale=cols[:, 2:3]).then_inc(A.sem, 1)
                elif level == 21:
                    act.wait_ge(FR["pe"].sem, FR["pe"].at(b, "v"))
                    if old(b, 2):
                        act.wait_ge(AT["pe"].sem, AT["pe"].at(b - 2, f"pv{H - 1}"))
                    for i in range(QB):
                        r = act.activation(VA[:, p, i, :, 0:DH],
                                           PF[0][:, i * P:(i + 1) * P].rearrange("p (h d) -> p h d", h=H), ACT.Copy)
                    r.then_inc(A.sem, 1)
                elif level == 20:
                    act.wait_ge(FR["dve"].sem, FR["dve"].at(b, "qk"))
                    if old(b, 1):
                        act.wait_ge(s_stw, 96 * b)
                    act.activation(part[:, 0, :, :], qk[:, :, :], ACT.Copy).then_inc(A.sem, 1)
                elif level == 22:
                    act.wait_ge(FR["dve"].sem, FR["dve"].at(b, "r1"))
                    act.activation(part[:, 1, :, :], qk[:, :, :], ACT.Copy).then_inc(A.sem, 1)

            def attn_max(a, p):
                act.wait_ge(AT["pe"].sem, AT["pe"].at(a, "nmT"))
                if old(a, 1):
                    act.wait_ge(s_nm, 96 * a)
                act.activation(nmT[:, :], PA_b[0:3 * H, 0:S], ACT.Copy).then_inc(B.sem, 1)

            def attn_head(a, p, h):
                act.wait_ge(AT["pe"].sem, AT["pe"].at(a, f"s{h}"))
                if h >= 4:
                    act.wait_ge(AT["pe"].sem, AT["pe"].at(a, f"pv{h - 4}"))
                elif old(a, 1):
                    act.wait_ge(AT["pe"].sem, AT["pe"].at(a - 1, f"pv{H - 4 + h}"))
                act.activation(PT[:, h % 4, :], PS[h % 2][:, 0:3 * P], ACT.Exp, scale=SCALE).then_inc(B.sem, 1)

            def tail(t, p, level):
                if level == 0:
                    act.wait_ge(AT["pe"].sem, AT["pe"].at(t, f"pv{H - 1}"))
                    for i in range(2):
                        r = act.activation(OT[:, 2 * i:2 * i + 2, :], PO[i][:, :], ACT.Copy)
                    r.then_inc(C.sem, 1)
                elif level == 5:
                    act.wait_ge(TL["pe"].sem, TL["pe"].at(t, "onT"))
                    act.activation(ONT[:, :], PO[0][:, 0:S], ACT.Copy).then_inc(C.sem, 1)
                elif level == 9:
                    act.wait_ge(TL["dve"].sem, TL["dve"].at(t, "h3"))
                    for i in range(QB):
                        r = act.activation(sq2[:, i, :], h3[:, i, :], ACT.Square, accum_out=ss2[:, i:i + 1])
                    r.then_inc(C.sem, 1)
                elif level == 15:
                    act.wait_ge(TL["pe"].sem, TL["pe"].at(t, "xT"))
                    act.activation(xn2T[:, :], PA[1][:, 0:S], ACT.Copy).then_inc(C.sem, 1)
                elif level == 19:
                    act.wait_ge(TL["dve"].sem, TL["dve"].at(t, "dl"))
                    act.activation(el[:, :], dl[:, :], ACT.Exp).then_inc(C.sem, 1)

            def period(f, a, t, pf):
                for slot in range(SLOTS):
                    if a is not None and slot == 12:
                        attn_max(a, 1 - pf)
                    if a is not None and slot >= 12:
                        attn_head(a, 1 - pf, slot - 12)
                    if t is not None:
                        tail(t, pf, slot)
                    if f is not None:
                        front(f, pf, slot)

            run_periods(act, period)

            def tile(T, p, xt=True, gu=True, tr=True, dn=True):
                if xt:
                    act.wait_ge(moe["pe_xT"], T + 1 + 1)
                    if old(T, 1):
                        act.wait_ge(moe["pe_gu"], T)
                    act.activation(xT[:, 1 - p, :], PO[0][:, 0:P], ACT.Copy).then_inc(moe["act_xT"], 1)
                if gu:
                    act.wait_ge(moe["pe_gu"], T + 1)
                    if old(T, 2):
                        act.wait_ge(moe["dve_hm"], T - 1)
                    act.activation(sg[:, p, :], PA[p][:, 0:HID], ACT.Silu).then_inc(moe["act_sg"], 1)

            run_tiles(act, tile)

        @block.vector
        def _(dve):
            D = SU["dve"]

            def link(ins, stage=D):
                return ins.then_inc(stage.sem, 1)

            def setup_done(name):
                dve.wait_ge(D.sem, D.at(0, name))

            dve.wait_ge(s_cst, 16)
            dve.wait_ge(s_w, 16 * N_W)
            dve.memset(ones_f[:, :], 1.0)
            dve.memset(nmp[:, :, :, :], 0.0)
            dve.tensor_copy(ident_b[:, :], ident)
            dve.tensor_copy(upper_b[:, :], cst[:, C_UP:C_UP + P])
            dve.tensor_copy(mask_b[:, :, :], bc(cst[:, C_MASK:C_MASK + P], 1, 4))
            dve.memset(ones_b[:, :], 1.0)
            dve.tensor_copy(carry[:, :], cst[:, C_OFF:C_OFF + NE])
            dve.tensor_copy(kaug_b[:, 0:S], cst[:, C_KAUG:C_KAUG + 1].to_broadcast([P, S]))
            dve.memset(kaug_b[:, S:2 * S], 0.0)
            dve.wait_ge(SU["pool"].sem, 2)
            link(dve.memset(tiny[:, :], 0.0))
            dve.wait_ge(SU["act"].sem, 1)
            link(dve.tensor_scalar_add(decay[:, :], decay[:, :], 1.0))
            setup_done("ea")
            link(dve.reciprocal(decay[:, :], decay[:, :]))
            setup_done("decay")
            link(dve.tensor_copy(decay_b[:, :], decay[:, :].to_broadcast([P, S])))
            dve.wait_ge(SU["act"].sem, 2)
            link(dve.tensor_scalar_add(c_e[:, :], c_e[:, :], 1.0))
            setup_done("ec")
            link(dve.reciprocal(c_e[:, :], c_e[:, :]))
            setup_done("rc")
            link(dve.tensor_tensor(silu_T[:, :], c_T[:, :], c_e[:, :], ALU.mult))
            dve.wait_ge(SU["pe"].sem, SU["pe"].at(0, "bwcw"))
            dve.tensor_copy(bwT[:, :], PF[0][:, 0:P])
            link(dve.tensor_copy(cwT[:, :], PF[0][:, P:2 * P]))
            for i in range(2):
                src = wqkv[:, i, :].rearrange("p (h x d) -> p h x d", h=H, x=2)
                dst = w_rot[:, i, :].rearrange("p (h x d) -> p h x d", h=H, x=2)
                dve.tensor_scalar(dst[:, :, 0, :], src[:, :, 1, :], -1.0, None, ALU.mult)
                r = dve.tensor_copy(dst[:, :, 1, :], src[:, :, 0, :])
            link(r)
            dve.wait_ge(SU["pe"].sem, SU["pe"].at(0, "modT"))
            dve.tensor_copy(mod_T[:, 0, :], PF[1][:, 0:NB])
            link(dve.tensor_scalar_add(mod_T[:, 1, :], PF[1][:, NB:2 * NB], 1.0))
            dve.wait_ge(SU["pe"].sem, SU["pe"].at(0, "modr"))
            dve.tensor_copy(mod_r[:, 0:3 * P], PA[0][0:NB, 0:3 * P])
            link(dve.tensor_copy(mod_r[:, 3 * P:6 * P], PA[1][0:NB, 0:3 * P]))
            setup_done("modr")
            gates = mod_r[:, :].rearrange("b (x d) -> b x d", x=6)[:, 2:6:3, :]
            rows = row_s[:, :].rearrange("b (x d) -> b x d", x=5)
            link(dve.tensor_scalar(sgn[:, :, :], gates, 0.0, 2.0, ALU.is_ge, ALU.mult))
            setup_done("sgn2")
            link(dve.tensor_scalar(sgn[:, :, :], sgn[:, :, :], 1.0, None, ALU.subtract))
            setup_done("sgn")
            link(dve.tensor_tensor(rows[:, 0:5:4, :], gates, sgn[:, :, :], ALU.mult))
            setup_done("abs")
            link(dve.scalar_tensor_tensor(out=rows[:, 0:5:4, :], in0=rows[:, 0:5:4, :], scalar=0.25, in1=sgn[:, :, :],
                                          op0=ALU.max, op1=ALU.mult))
            setup_done("guard")
            dve.tensor_tensor(rows[:, M_CBGA, :], rows[:, M_GA, :], cb_r[:, :], ALU.mult)
            dve.tensor_scalar_add(rows[:, M_CB1, :], mod_r[:, 4 * P:5 * P], 1.0)
            link(dve.tensor_copy(rows[:, M_SB, :], mod_r[:, 3 * P:4 * P]))
            link(dve.memset(tiny[:, :], 0.0))
            setup_done("carry")

            F, B, C = FR["dve"], AT["dve"], TL["dve"]

            def layernorm_stats(b, src, stage, names):
                for i in range(QB):
                    r = dve.bn_stats(st[:, i, :], src[:, i, :])
                link(r, F)
                dve.wait_ge(F.sem, F.at(b, names[0]))
                alone(dve)
                for i in range(QB):
                    r = dve.bn_aggr(mv[:, i, :], st[:, i, :])
                link(r, F)
                dve.wait_ge(F.sem, F.at(b, names[1]))
                link(dve.tensor_scalar_add(ve[:, :], mv[:, :, 1], LN_EPS), F)

            def normalise(dst, src):
                for i in range(QB):
                    r = dve.tensor_scalar(dst[:, i, :], src[:, i, :], mv[:, i, 0:1], rs[:, i:i + 1],
                                          ALU.subtract, ALU.mult)
                link(r, F)

            def front(b, p, level):
                if level == 0:
                    dve.wait_ge(s_x[p], 8 * (b - p) + 16)
                    if old(b, 1):
                        dve.wait_ge(FR["pool"].sem, FR["pool"].at(b - 1, "rs3"))
                    if old(b, 2):
                        dve.wait_ge(FR["act"].sem, FR["act"].at(b - 2, "hT"))
                    dve.tensor_copy(modc[:, p, 0:1], mod_T[:, 1, bass.ds(b, 1)])
                    dve.tensor_copy(modc[:, p, 1:2], mod_T[:, 0, bass.ds(b, 1)])
                    layernorm_stats(b, X[:, p, :, :], F, ("st", "mv"))
                elif level == 2:
                    dve.wait_ge(FR["pool"].sem, FR["pool"].at(b, "rs1"))
                    if old(b, 1):
                        dve.wait_ge(FR["pe"].sem, FR["pe"].at(b - 1, "xnT"))
                    normalise(nrm, X[:, p, :, :])
                elif level == 7:
                    dve.wait_ge(FR["act"].sem, FR["act"].at(b, "bx"))
                    if old(b, 1):
                        dve.wait_ge(FR["pe"].sem, FR["pe"].at(b - 1, "y"))
                    link(dve.tensor_tensor_scan(hs[:, :], decay_b[:, :], bx[:, :], 0.0, ALU.mult, ALU.add), F)
                elif level == 9:
                    dve.wait_ge(FR["pe"].sem, FR["pe"].at(b, "y"))
                    dve.wait_ge(s_mb[p], 8 * (b - p) + 16)
                    link(dve.tensor_tensor(tmp[:, :, :], PF[0][:, 0:S].rearrange("p (t d) -> p t d", t=QB),
                                           bc(MB[:, p, 0:P], 1, QB), ALU.mult), F)
                    dve.wait_ge(F.sem, F.at(b, "ty"))
                    dve.wait_ge(FR["pool"].sem, FR["pool"].at(b, "xg"))
                    if old(b, 2):
                        dve.wait_ge(TL["pool"].sem, TL["pool"].at(b - 2, "base"))
                    link(dve.tensor_tensor(X1[:, p, :, :], tmp[:, :, :], xg[:, :, :], ALU.add), F)
                    dve.wait_ge(F.sem, F.at(b, "x1"))
                    layernorm_stats(b, X1[:, p, :, :], F, ("st2", "mv2"))
                elif level == 11:
                    dve.wait_ge(FR["pool"].sem, FR["pool"].at(b, "rs2"))
                    dve.wait_ge(FR["pe"].sem, FR["pe"].at(b, "nT"))
                    normalise(nrm, X1[:, p, :, :])
                elif level == 12:
                    dve.wait_ge(F.sem, F.at(b, "n2"))
                    link(dve.tensor_tensor(H2[:, p, :, :], nrm[:, :, :], bc(MB[:, p, M_CB1 * P:(M_CB1 + 1) * P], 1, QB),
                                           ALU.mult), F)
                    dve.wait_ge(F.sem, F.at(b, "h2a"))
                    link(dve.tensor_tensor(H2[:, p, :, :], H2[:, p, :, :], bc(MB[:, p, M_SB * P:(M_SB + 1) * P], 1, QB),
                                           ALU.add), F)
                elif level == 14:
                    dve.wait_ge(FR["act"].sem, FR["act"].at(b, "ss"))
                    link(dve.tensor_scalar(ve[:, :], ss[:, :], 1.0 / P, RMS_EPS, ALU.mult, ALU.add), F)
                elif level == 15:
                    dve.wait_ge(FR["pool"].sem, FR["pool"].at(b, "rs3"))
                    for i in range(QB):
                        r = dve.tensor_scalar(nrm[:, i, :], H2[:, p, i, :], rs[:, i:i + 1], None, ALU.mult)
                    link(r, F)
                elif level == 19:
                    dve.wait_ge(FR["pe"].sem, FR["pe"].at(b, "qk"))
                    two = lambda t: t[:, :].rearrange("p (x k) -> p x k", x=2)
                    link(dve.tensor_tensor(r_c[:, :, :], two(PF[0]), bc(cst[:, C_COS:C_COS + S], 1, 2), ALU.mult), F)
                    link(dve.tensor_tensor(r_s[:, :, :], two(PF[1]), bc(cst[:, C_SIN:C_SIN + S], 1, 2), ALU.mult), F)
                    dve.wait_ge(F.sem, F.at(b, "rs"))
                    link(dve.tensor_tensor(qk[:, :, :], r_c[:, :, :], r_s[:, :, :], ALU.add), F)
                elif level == 21:
                    dve.wait_ge(FR["act"].sem, FR["act"].at(b, "ph"))
                    link(dve.tensor_tensor(qk[:, :, :], qk[:, :, :], part[:, 0, :, :], ALU.subtract), F)
                elif level == 23:
                    dve.wait_ge(FR["act"].sem, FR["act"].at(b, "pm"))
                    link(dve.tensor_tensor(part[:, 2, :, :], qk[:, :, :], part[:, 1, :, :], ALU.subtract), F)

            def attn_unit(a, p, u):
                g, k = divmod(u, 3)
                dve.wait_ge(AT["pe"].sem, AT["pe"].at(a, f"a{u}"))
                if k == 0:
                    dst, src = MX[:, 0, 4 * g:4 * g + 4], PA[u % 2][:, :].rearrange("p (h k) -> p h k", h=4)
                else:
                    h = 4 * g + 2 * (k - 1)
                    dst, src = MX[:, 1, h:h + 2], PA[u % 2][:, :].rearrange("p (h k) -> p h k", h=2)
                link(dve.tensor_reduce(dst, src, op=ALU.max, axis=AX_X), B)

            def attn_max(a, p):
                dve.wait_ge(B.sem, B.at(a, "m11"))
                if old(a, 1):
                    dve.wait_ge(AT["pe"].sem, AT["pe"].at(a - 1, "nmT"))
                link(dve.tensor_scalar(nmp[:, :, 0, :], MX[:, :, :], -1.0, None, ALU.mult), B)
                dve.wait_ge(B.sem, B.at(a, "nh"))
                link(dve.scalar_tensor_tensor(out=rem[:, :, :], in0=MX[:, :, :], scalar=-1.0, in1=nmp[:, :, 0, :],
                                              op0=ALU.mult, op1=ALU.subtract), B)
                dve.wait_ge(B.sem, B.at(a, "rem"))
                link(dve.tensor_copy(nmp[:, :, 1, :], rem[:, :, :]), B)
                dve.wait_ge(B.sem, B.at(a, "nm"))
                link(dve.tensor_tensor(rem[:, :, :], rem[:, :, :], nmp[:, :, 1, :], ALU.subtract), B)
                dve.wait_ge(B.sem, B.at(a, "rem2"))
                link(dve.tensor_copy(nmp[:, :, 2, :], rem[:, :, :]), B)

            def tail(t, p, level):
                def chain(ins, name):
                    link(ins, C)
                    dve.wait_ge(C.sem, C.at(t, name))

                if level == 3:
                    dve.wait_ge(TL["pe"].sem, TL["pe"].at(t, "oT"))
                    heads = [PO[i][:, :].rearrange("p (h r) -> p h r", r=32) for i in range(QB)]
                    for i in range(QB):
                        r = dve.reciprocal(rc[:, i, :], heads[i][:, :, DH])
                    chain(r, "rc")
                    for i in range(QB):
                        r = dve.tensor_tensor(ON[:, i, :].rearrange("p (h d) -> p h d", h=H), heads[i][:, :, 0:DH],
                                              bc(rc[:, i, :], 2, DH), ALU.mult)
                    link(r, C)
                elif level == 8:
                    dve.wait_ge(TL["pe"].sem, TL["pe"].at(t, "wo"))
                    link(dve.tensor_tensor(h3[:, :, :], PO[1][:, 0:S].rearrange("p (t d) -> p t d", t=QB),
                                           H2[:, p, :, :], ALU.add), C)
                elif level == 10:
                    dve.wait_ge(TL["act"].sem, TL["act"].at(t, "ss"))
                    link(dve.tensor_scalar(ve2[:, :], ss2[:, :], 1.0 / P, RMS_EPS, ALU.mult, ALU.add), C)
                elif level == 12:
                    dve.wait_ge(TL["pool"].sem, TL["pool"].at(t, "rs"))
                    if old(t, 2):
                        dve.wait_ge(s_sc[p], 32 * (t - p))
                    for i in range(QB):
                        r = dve.scalar_tensor_tensor(out=xn2[:, p, i, :], in0=h3[:, i, :], scalar=rs2[:, i:i + 1],
                                                     in1=g2_b[:, :], op0=ALU.mult, op1=ALU.mult)
                    link(r, C)
                elif level == 17:
                    dve.wait_ge(TL["pe"].sem, TL["pe"].at(t, "lg"))
                    chain(dve.tensor_copy(lg[:, :, :], PA[1][:, 0:QB * NE].rearrange("p (t e) -> p t e", t=QB)), "lg")
                    alone(dve)
                    for i in range(QB):
                        r = dve.max(mx8[:, i, :], lg[:, i, :])
                    chain(r, "mx")
                    alone(dve)
                    for i in range(QB):
                        r = dve.max_index(ix8[:, i, :], mx8[:, i, :], lg[:, i, :])
                    chain(r, "ix")
                    chain(dve.tensor_copy(ixf[:, :, :], ix8[:, :, 0:2]), "ixf")
                    link(dve.tensor_tensor(dl[:, :], mx8[:, :, 1], mx8[:, :, 0], ALU.subtract), C)
                elif level == 20:
                    w = WGT[:, bass.ds(t * 4, 4)].rearrange("p (t k) -> p t k", t=QB)
                    dve.wait_ge(TL["act"].sem, TL["act"].at(t, "el"))
                    chain(dve.tensor_scalar_add(e1[:, :], el[:, :], 1.0), "e1")
                    chain(dve.reciprocal(w12[:, :, 0], e1[:, :]), "w1")
                    chain(dve.tensor_tensor(w12[:, :, 1], w12[:, :, 0], el[:, :], ALU.mult), "w2")
                    dve.tensor_copy(w, w12[:, :, :])
                    chain(dve.tensor_tensor(oh[:, :, :, :], bc(bc(cst[:, C_IOTA:C_IOTA + NE], 1, 2), 1, QB),
                                            bc(ixf[:, :, :], 3, NE), ALU.is_equal), "oh")
                    link(dve.tensor_tensor(ohs[:, :, :], oh[:, :, 0, :], oh[:, :, 1, :], ALU.add), C)
                elif level == 23:
                    dve.wait_ge(TL["pe"].sem, TL["pe"].at(t, "rank"))
                    rk = PA[1][:, 0:3 * NE].rearrange("p (t e) -> p t e", t=3)
                    chain(dve.tensor_tensor(pall[:, :, :], rk[:, 0:QB, :], bc(carry[:, :], 1, QB), ALU.add), "pall")
                    chain(dve.tensor_tensor(carry[:, :], rk[:, QB, :], carry[:, :], ALU.add), "carry")
                    chain(dve.tensor_tensor(prod[:, :, :, :], oh[:, :, :, :], bc(pall[:, :, :], 2, 2), ALU.mult), "prod")
                    chain(dve.tensor_reduce(posf[:, :, :], prod[:, :, :, :], op=ALU.add, axis=AX_X), "posf")
                    link(dve.tensor_copy(posi[:, p, :], posf[:, :, :].rearrange("p t k -> p (t k)")), C)
                    link(dve.tensor_copy(POS[:, bass.ds(t * 4, 4)], posf[:, :, :].rearrange("p t k -> p (t k)")), C)

            def period(f, a, t, pf):
                for slot in range(SLOTS):
                    if a is not None and slot < 12:
                        attn_unit(a, 1 - pf, slot)
                    if a is not None and slot == 11:
                        attn_max(a, 1 - pf)
                    if t is not None:
                        tail(t, pf, slot)
                    if f is not None:
                        front(f, pf, slot)

            run_periods(dve, period)

            R = RT

            def step(ins, name):
                ins.then_inc(R.sem, 1)
                dve.wait_ge(R.sem, R.at(0, name))

            dve.wait_ge(C.sem, C.at(NB - 1, "POS"))
            step(dve.tensor_scalar(padf[:, :], carry[:, :], cst[:, C_ROW:C_ROW + 1], None, ALU.add), "padf")
            dve.tensor_copy(padi[:, :], padf[:, :]).then_inc(s_idx, 1)
            step(dve.tensor_tensor(cnt[:, :], carry[:, :], cst[:, C_OFF:C_OFF + NE], ALU.subtract), "cnt")
            step(dve.tensor_scalar(cnt[:, :], cnt[:, :], P / 2 - 0.5, 1.0 / P, ALU.add, ALU.mult), "cnt2")
            step(dve.tensor_copy(cnti[:, :], cnt[:, :]), "cnti")
            step(dve.tensor_copy(cnt[:, :], cnti[:, :]), "nt")
            step(dve.tensor_tensor_scan(cum[:, :], ones_f[:, :], cnt[:, :], 0.0, ALU.mult, ALU.add), "cum")
            tiles = cst[0:1, C_TILE:C_TILE + NT]
            step(dve.tensor_tensor(past[:, :, :], bc(tiles, 2, NE), bc(cum[0:1, :], 1, NT), ALU.is_ge), "past")
            step(dve.tensor_reduce(eidx[:, :], past[:, :, :], op=ALU.add, axis=AX_X), "eidx")
            step(dve.tensor_tensor(past[:, :, :], past[:, :, :], bc(cnt[0:1, :], 1, NT), ALU.mult), "pastn")
            step(dve.tensor_reduce(first[:, :], past[:, :, :], op=ALU.add, axis=AX_X), "first")
            step(dve.tensor_tensor(first[:, :], tiles, first[:, :], ALU.subtract), "inside")
            step(dve.tensor_scalar(valid[:, :], eidx[:, :], NE - 0.5, None, ALU.is_lt), "valid")
            step(dve.scalar_tensor_tensor(out=first[:, :], in0=first[:, :], scalar=float(P), in1=valid[:, :],
                                          op0=ALU.mult, op1=ALU.mult), "jrow")
            step(dve.tensor_scalar(valid[:, :], valid[:, :], -1.0, 1.0, ALU.mult, ALU.add), "spare")
            step(dve.tensor_tensor(valid[:, :], valid[:, :], cst[0:1, C_DUMMY:C_DUMMY + NT], ALU.mult), "dummy")
            step(dve.tensor_tensor(first[:, :], first[:, :], valid[:, :], ALU.add), "sum")
            step(dve.scalar_tensor_tensor(out=first[:, :], in0=eidx[:, :], scalar=float(REG), in1=first[:, :],
                                          op0=ALU.mult, op1=ALU.add), "row")
            step(dve.tensor_scalar(eidx[:, :], eidx[:, :], NE - 1.0, float(EW), ALU.min, ALU.mult), "col")
            dve.tensor_copy(tab[:, 0, :], first[:, :]).then_inc(s_tab, 1)
            dve.tensor_copy(tab[:, 1, :], eidx[:, :]).then_inc(s_tab, 1)
            step(dve.tensor_tensor(delta[:, :], cum[:, :], cnt[:, :], ALU.subtract), "tab")
            step(dve.tensor_scalar(delta[:, :], delta[:, :], float(P), None, ALU.mult), "startt")
            step(dve.tensor_tensor(delta[:, :], delta[:, :], cst[:, C_OFF:C_OFF + NE], ALU.subtract), "delta")
            dve.tensor_copy(shift[:, 0:1], delta[:, 0:1])
            step(dve.tensor_tensor(shift[:, 1:NE], delta[:, 1:NE], delta[:, 0:NE - 1], ALU.subtract), "shift")
            step(dve.tensor_tensor(above[:, :, :], bc(POS[:, :], 2, NE), bc(cst[:, C_OFF:C_OFF + NE], 1, TT * 2),
                                   ALU.is_ge), "above")
            step(dve.tensor_tensor(above[:, :, :], above[:, :, :], bc(shift[:, :], 1, TT * 2), ALU.mult), "moves")
            step(dve.tensor_reduce(moved[:, :], above[:, :, :], op=ALU.add, axis=AX_X), "moved")
            step(dve.tensor_tensor(moved[:, :], moved[:, :], POS[:, :], ALU.add), "pos")
            step(dve.tensor_copy(GIDX[:, :], moved[:, :]), "GIDX")

            def tile(T, p, xt=True, gu=True, tr=True, dn=True):
                if gu:
                    dve.wait_ge(moe["act_sg"], T + 1)
                    if old(T, 2):
                        dve.wait_ge(moe["pe_tr"], T - 2 + 1)
                    dve.tensor_tensor(hm[:, p, :], PS[p][:, 0:HID], sg[:, p, :], ALU.mult).then_inc(moe["dve_hm"], 1)
                if tr:
                    dve.wait_ge(moe["pe_tr"], T - 1 + 1)
                    if old(T, 3):
                        dve.wait_ge(moe["pe_dn"], T - 2)
                    dve.tensor_copy(hmT[:, 1 - p, :], PF[1 - p][:, 0:HID]).then_inc(moe["dve_hT"], 1)
                if dn:
                    dve.wait_ge(moe["pe_dn"], T - 2 + 1)
                    if old(T, 4):
                        dve.wait_ge(s_st[p], 8 * (T - 4 - p) + 16)
                    dve.tensor_copy(eo[:, p, :], PO[1][:, 0:P]).then_inc(moe["dve_eo"], 1)

            run_tiles(dve, tile)

            L = LA

            def last(b, p):
                def step(ins, name):
                    ins.then_inc(L.sem, 1)
                    dve.wait_ge(L.sem, L.at(b, name))

                if old(b, 2):
                    dve.wait_ge(s_got[p], 32 * (b - p))
                dve.tensor_copy(wl[:, p, :], WGT[:, bass.ds(b * 4, 4)])
                step(dve.tensor_copy(gidx[:, p, :], GIDX[:, bass.ds(b * 4, 4)]), "idx")
                dve.wait_ge(s_got[p], 32 * (b - p) + 64)
                if old(b, 2):
                    dve.wait_ge(s_out[p], 8 * (b - p))
                for i in range(QB):
                    r = dve.tensor_scalar(res[:, p, i, :], got[:, p, i, 0, :], wl[:, p, 2 * i:2 * i + 1], None, ALU.mult)
                step(r, "a")
                for i in range(QB):
                    r = dve.scalar_tensor_tensor(out=res[:, p, i, :], in0=got[:, p, i, 1, :],
                                                 scalar=wl[:, p, 2 * i + 1:2 * i + 2], in1=res[:, p, i, :],
                                                 op0=ALU.mult, op1=ALU.add)
                step(r, "b")
                dve.wait_ge(s_gb[p], 8 * (b - p) + 16)
                step(dve.tensor_tensor(res[:, p, :, :], res[:, p, :, :], bc(GB[:, p, :], 1, QB), ALU.mult), "g")
                dve.tensor_tensor(res[:, p, :, :], res[:, p, :, :], base[:, bass.ds(b * QB, QB), :], ALU.add).then_inc(L.sem, 1)

            last(0, 0)
            last(1, 1)
            with dve.Fori(1, NB // 2) as j:
                last(2 * j, 0)
                last(2 * j + 1, 1)

        @block.tensor
        def _(pe):
            mm = nc.tensor.matmul
            transpose = nc.tensor.transpose
            pe.wait_ge(s_cst, 16)
            pe.wait_ge(s_w, 16 * N_W)
            transpose(PF[0][:, 0:P], w_in[:, 0, :], ident)
            transpose(PF[0][:, P:2 * P], w_in[:, 1, :], ident).then_inc(SU["pe"].sem, 1)
            pe.wait_ge(SU["dve"].sem, SU["dve"].at(0, "silu"))
            for i in range(2):
                r = mm(PF[1][:, i * NB:(i + 1) * NB], wmod_s[:, i * P:(i + 1) * P], silu_T[:, :], start=True, stop=True)
            r.then_inc(SU["pe"].sem, 1)
            for i in range(2):
                r = mm(PA[i][0:NB, 0:3 * P], silu_T[:, :], wmod_s[:, i * 3 * P:(i + 1) * 3 * P], start=True, stop=True)
            r.then_inc(SU["pe"].sem, 1)
            pe.wait_ge(SU["dve"].sem, SU["dve"].at(0, "carry"))
            pe.wait_ge(SU["pool"].sem, 2)
            A, B, C = FR["pe"], AT["pe"], TL["pe"]

            def front(b, p, level):
                if level == 3:
                    pe.wait_ge(FR["dve"].sem, FR["dve"].at(b, "n1"))
                    if old(b, 1):
                        pe.wait_ge(FR["act"].sem, FR["act"].at(b - 1, "va"))
                    for i in range(QB):
                        r = transpose(PF[0][:, i * P:(i + 1) * P], nrm[:, i, :], ident)
                    r.then_inc(A.sem, 1)
                elif level == 5:
                    pe.wait_ge(FR["act"].sem, FR["act"].at(b, "hT"))
                    if old(b, 1):
                        pe.wait_ge(FR["dve"].sem, FR["dve"].at(b - 1, "rs"))
                    mm(PF[1][:, 0:S], bwT[:, :], hT[:, :], start=True, stop=True).then_inc(A.sem, 1)
                elif level == 8:
                    pe.wait_ge(FR["dve"].sem, FR["dve"].at(b, "scan"))
                    for i in range(QB):
                        r = mm(PF[0][:, i * P:(i + 1) * P], hs[:, i * P:(i + 1) * P], cwT[:, :], start=True, stop=True)
                    r.then_inc(A.sem, 1)
                elif level == 16:
                    pe.wait_ge(FR["dve"].sem, FR["dve"].at(b, "xn"))
                    for i in range(QB):
                        r = transpose(PF[1][:, i * P:(i + 1) * P], nrm[:, i, :], ident)
                    r.then_inc(A.sem, 1)
                elif level == 18:
                    pe.wait_ge(FR["act"].sem, FR["act"].at(b, "xnT"))
                    for i in range(2):
                        mm(PF[0][:, i * S:(i + 1) * S], wqkv[:, i, :], xnT[:, :], start=True, stop=True)
                        r = mm(PF[1][:, i * S:(i + 1) * S], w_rot[:, i, :], xnT[:, :], start=True, stop=True)
                    r.then_inc(A.sem, 1)
                elif level == 20:
                    pe.wait_ge(FR["dve"].sem, FR["dve"].at(b, "rc"))
                    for i in range(QB):
                        r = mm(PF[0][:, i * P:(i + 1) * P], xnT[:, i * P:(i + 1) * P], wqkv[:, 2, :], start=True, stop=True)
                    r.then_inc(A.sem, 1)

            def attn_unit(a, p, u):
                g, k = divmod(u, 3)
                if u == 0:
                    pe.wait_ge(s_stk[p], 24 * (a - p) + 48)
                    if old(a, 1):
                        pe.wait_ge(AT["act"].sem, AT["act"].at(a - 1, "nmT"))
                if u == 1 and old(a, 2):
                    pe.wait_ge(TL["dve"].sem, TL["dve"].at(a - 2, "carry"))
                if u >= 2:
                    pe.wait_ge(AT["dve"].sem, AT["dve"].at(a, f"m{u - 2}"))
                elif old(a, 1):
                    pe.wait_ge(AT["dve"].sem, AT["dve"].at(a - 1, f"m{10 + u}"))
                bank = PA[u % 2]
                if k == 0:
                    heads, n = range(4 * g, 4 * g + 4), P
                else:
                    heads, n = range(4 * g + 2 * (k - 1), 4 * g + 2 * k), S
                q0 = 0 if k == 0 else P
                for i, h in enumerate(heads):
                    mm(bank[:, i * n:(i + 1) * n], QST[:, p, h // 2, q0:q0 + P], KST[:, p, h, 0:n],
                       start=(i == 0), stop=False, skip_group_check=True)
                diag = bank[:, :].rearrange("p (h k) -> p h k", k=n)[:, :, n - P:n]
                mm(diag, ident_b[:, :], mask_b[:, 0:len(heads), :], start=False, stop=True,
                   skip_group_check=True).then_inc(B.sem, 1)

            def attn_max(a, p):
                pe.wait_ge(AT["dve"].sem, AT["dve"].at(a, "nl"))
                for i in range(QB):
                    r = transpose(PA_b[:, i * P:(i + 1) * P], nmp[:, i, :, :].rearrange("p x h -> p (x h)"), ident_b[:, :])
                r.then_inc(B.sem, 1)

            def attn_scores(a, p, h):
                if h == 0:
                    pe.wait_ge(s_nm, 96 * a + 96)
                if h >= 2:
                    pe.wait_ge(AT["act"].sem, AT["act"].at(a, f"e{h - 2}"))
                elif old(a, 1):
                    pe.wait_ge(AT["act"].sem, AT["act"].at(a - 1, f"e{H - 2 + h}"))
                bank = PS[h % 2]
                mm(bank[:, 0:S], KST[:, p, h, 0:P], QST[:, p, h // 2, :], start=True, stop=True)
                mm(bank[:, S:S + P], KST[:, p, h, P:S], QST[:, p, h // 2, P:S], start=True, stop=True).then_inc(B.sem, 1)

            def attn_pv(a, p, h):
                pe.wait_ge(AT["pool"].sem, AT["pool"].at(a, f"c{h}"))
                if h == 0 and old(a, 1):
                    pe.wait_ge(TL["dve"].sem, TL["dve"].at(a - 1, "h3"))
                g, j = divmod(h, 4)
                o = PO[g // 2][32 * j:32 * j + 32, (g % 2) * S:(g % 2) * S + S]
                mm(o, VA[:, p, 0, h, :], PT[:, h % 4, 0:S], start=True, stop=False)
                mm(o[:, P:S], VA[:, p, 1, h, :], PT[:, h % 4, S:3 * P], start=False, stop=True).then_inc(B.sem, 1)

            def tail(t, p, level):
                if level == 1:
                    pe.wait_ge(TL["act"].sem, TL["act"].at(t, "OT"))
                    for i in range(QB):
                        for g in range(4):
                            r = transpose(PO[i][:, g * P:(g + 1) * P], OT[:, g, i * P:(i + 1) * P], ident)
                    r.then_inc(C.sem, 1)
                elif level == 4:
                    pe.wait_ge(TL["dve"].sem, TL["dve"].at(t, "on"))
                    for i in range(QB):
                        r = transpose(PO[0][:, i * P:(i + 1) * P], ON[:, i, :], ident)
                    r.then_inc(C.sem, 1)
                elif level == 6:
                    pe.wait_ge(TL["act"].sem, TL["act"].at(t, "onT"))
                    for i in range(QB):
                        r = mm(PO[1][:, i * P:(i + 1) * P], ONT[:, i * P:(i + 1) * P], wo_s[:, :], start=True, stop=True)
                    r.then_inc(C.sem, 1)
                elif level == 14:
                    pe.wait_ge(TL["dve"].sem, TL["dve"].at(t, "xn"))
                    for i in range(QB):
                        r = transpose(PA[1][:, i * P:(i + 1) * P], xn2[:, p, i, :], ident)
                    r.then_inc(C.sem, 1)
                elif level == 16:
                    pe.wait_ge(TL["act"].sem, TL["act"].at(t, "xT"))
                    for i in range(QB):
                        r = mm(PA[1][:, i * NE:(i + 1) * NE], xn2T[:, i * P:(i + 1) * P], wr_s[:, :], start=True, stop=True)
                    r.then_inc(C.sem, 1)
                elif level == 22:
                    pe.wait_ge(TL["dve"].sem, TL["dve"].at(t, "ohs"))
                    for i, (o, terms) in enumerate((
                            (0, ((upper_b, 0),)), (1, ((ones_b, 0), (upper_b, 1))), (2, ((ones_b, 0), (ones_b, 1))))):
                        for k, (w, blk) in enumerate(terms):
                            r = mm(PA[1][:, o * NE:(o + 1) * NE], w[:, :], ohs[:, blk, :], start=(k == 0),
                                   stop=(k == len(terms) - 1))
                    r.then_inc(C.sem, 1)

            def period(f, a, t, pf):
                for slot in range(SLOTS):
                    if a is not None:
                        if slot < 12:
                            attn_unit(a, 1 - pf, slot)
                        if slot == 12:
                            attn_max(a, 1 - pf)
                        if slot >= 12:
                            attn_scores(a, 1 - pf, slot - 12)
                            if slot >= 14:
                                attn_pv(a, 1 - pf, slot - 14)
                        if slot == SLOTS - 1:
                            attn_pv(a, 1 - pf, H - 2)
                            attn_pv(a, 1 - pf, H - 1)
                    if t is not None:
                        tail(t, pf, slot)
                    if f is not None:
                        front(f, pf, slot)

            run_periods(pe, period)
            pe.wait_ge(s_tab, 3)
            pe.wait_ge(s_exp, 16 * (2 + NE))
            def tile(T, p, xt=True, gu=True, tr=True, dn=True):
                if gu:
                    col = pe.value_load(tab[0:1, 1, bass.ds(T, 1)], min_val=0, max_val=(NE - 1) * EW)
                if xt:
                    pe.wait_ge(s_in[1 - p], 8 * (T + p) + 16)
                    if old(T, 0):
                        pe.wait_ge(moe["act_xT"], T + 1)
                    transpose(PO[0][:, 0:P], xin[:, 1 - p, :], ident).then_inc(moe["pe_xT"], 1)
                if gu:
                    pe.wait_ge(moe["act_xT"], T + 1)
                    if old(T, 2):
                        pe.wait_ge(moe["dve_hm"], T - 2 + 1)
                    mm(PA[p][:, 0:HID], xT[:, p, :], experts[:, bass.ds(col, HID)], start=True, stop=True)
                    mm(PS[p][:, 0:HID], xT[:, p, :], experts[:, bass.ds(col + HID, HID)], start=True, stop=True).then_inc(moe["pe_gu"], 1)
                if tr:
                    pe.wait_ge(moe["dve_hm"], T - 1 + 1)
                    if old(T, 3):
                        pe.wait_ge(moe["dve_hT"], T - 2)
                    for c_ in range(HC):
                        r = transpose(PF[1 - p][:, c_ * P:(c_ + 1) * P], hm[:, 1 - p, c_ * P:(c_ + 1) * P], ident)
                    r.then_inc(moe["pe_tr"], 1)
                if dn:
                    pcol = pe.value_load(tab[0:1, 1, bass.ds(T - 2, 1)], min_val=0, max_val=(NE - 1) * EW)
                    pe.wait_ge(moe["dve_hT"], T - 2 + 1)
                    if old(T, 3):
                        pe.wait_ge(moe["dve_eo"], T - 3 + 1)
                    for c_ in range(HC):
                        r = mm(PO[1][:, 0:P], hmT[:, p, c_ * P:(c_ + 1) * P],
                               experts[:, bass.ds(pcol + 2 * HID + c_ * P, P)], start=(c_ == 0), stop=(c_ == HC - 1))
                    r.then_inc(moe["pe_dn"], 1)

            run_tiles(pe, tile)


_INS = ['L0_attn_x', 'L0_attn_log_A', 'L0_attn_B_w', 'L0_attn_B_b', 'L0_attn_C_w', 'L0_attn_C_b', 'L0_ffn_wq',
        'L0_ffn_wk', 'L0_ffn_wv', 'L0_ffn_wo', 'L0_ffn_w_router', 'L0_ffn_wg', 'L0_ffn_wu', 'L0_ffn_wd',
        'L0_ffn_g1', 'L0_ffn_g2', 'L0_c', 'L0_wmod']


def kernel(**inputs):
    import concourse.bacc as _bacc
    from concourse.bass_utils import run_bass_kernel_spmd as _run

    nc = _bacc.Bacc("TRN2", target_bir_lowering=False, num_devices=1)
    arrays, args = {}, []
    for name in _INS:
        a = np.ascontiguousarray(inputs[name])
        arrays[name + "_dram"] = a
        args.append(nc.dram_tensor(name + "_dram", a.shape, mybir.dt.from_np(a.dtype), kind="ExternalInput").ap())
    arrays["consts_dram"] = constants()
    args.append(nc.dram_tensor("consts_dram", [P, C_N], F32, kind="ExternalInput").ap())
    args.append(nc.dram_tensor("out_dram", [NB, S, P], F32, kind="ExternalOutput").ap())
    build(nc, *args)
    r = _run(nc, [arrays], core_ids=[0])
    return r.results[0]["out_dram"]
```

```python
from contextlib import ExitStack

import numpy as np

import concourse.bass as bass
from concourse import mybir

F32 = mybir.dt.float32
BF16 = mybir.dt.bfloat16
I32 = mybir.dt.int32
U32 = mybir.dt.uint32
ALU = mybir.AluOpType
ACT = mybir.ActivationFunctionType
AX_X = mybir.AxisListType.X

P = 128
NB = 16
S = 256
QB = S // P
TT = NB * QB
H = 16
DH = P // H
NE = 8
HID = 384
HC = HID // P
EW = 2 * HID + HC * P
REG = NB * S + P
NT = 2 * NB * S // P + NE
NROW = NE * REG + 4 * P
LN_EPS, RMS_EPS = 1e-5, 1e-6
SCALE = float(DH) ** -0.5
ROWS = 64
Q_SLOTS = ((0, 2, 1, 3), (1, 0, 5, 2), (2, 1, 1, 1))
K_SLOTS = ((0, 0, 1, 3), (1, 3, 2, 2), (2, 4, 1, 1))
AUG = 6
NEG = -1.0e30
N_W = 14

SLOTS = 28
WHEN = dict(
    load=0, stats=12, rstd1=13, norm1=15, T1=16, h=17, bx_mm=18, bx=21, scan=22, y=23, xg=23, x1=24, rstd2=25,
    keep=25, norm2=26, h2=27, squares=28, mean3=29, rstd3=29, norm3=30, T3=34, xT=34, qk=35, rope=36, part0=37,
    rest1=38, part1=39, part2=40, stack=40, v=43, unit0=44, max_parts=55, max_T=56, max_rows=56, head0=66,
    o_copy=81, oT=81, divide=82, T_on=83, onT=84, wo=85, h3=87, load_gate=67, base=88, squares2=88, mean4=89,
    rstd4=90, x2=91, T_x2=92, x2T=93, logits=94, top2=95, exp_d=96, weights=97, rank=98, rows=99,
    scatters=(101, 103, 105, 107))
UNITS_PER_SLOT, HEADS_PER_SLOT, PV_LATER = 2, 2, 1
BATCH_SLOTS = max(WHEN["scatters"]) + 1
LAGS = -(-BATCH_SLOTS // SLOTS)


def units_at(now):
    u = (now - WHEN["unit0"]) * UNITS_PER_SLOT
    return [v for v in range(u, u + UNITS_PER_SLOT) if 0 <= v < 12]


def heads_at(now):
    h = (now - WHEN["head0"]) * HEADS_PER_SLOT
    return [v for v in range(h, h + HEADS_PER_SLOT) if 0 <= v < H]


C_ID, C_COS, C_SIN, C_UP, C_MASK, C_IOTA, C_OFF, C_ROW = 0, 128, 384, 640, 768, 896, 904, 912
C_TILE, C_DUMMY, C_KAUG, C_N = 920, 992, 1064, 1080
M_GA, M_CBGA, M_CB1, M_SB, M_GB = range(5)


def constants():
    c = np.zeros((P, C_N), np.float32)
    c[:, C_ID:C_ID + P] = np.eye(P)
    inv = 1.0 / 10000.0 ** (np.arange(0, DH, 2, dtype=np.float32) / DH)
    f = np.einsum('i,j->ij', np.arange(S, dtype=np.float32), inv)
    emb = np.concatenate([f, f], axis=-1)
    c[:, C_COS:C_COS + S] = np.tile(np.cos(emb).T, (H, 1))
    c[:, C_SIN:C_SIN + S] = np.tile(np.sin(emb).T, (H, 1))
    c[:, C_UP:C_UP + P] = np.triu(np.ones((P, P)), 1)
    c[:, C_MASK:C_MASK + P] = np.triu(np.full((P, P), NEG), 1)
    c[:, C_IOTA:C_IOTA + NE] = np.arange(NE)
    c[:, C_OFF:C_OFF + NE] = np.arange(NE) * REG
    c[:, C_ROW] = np.arange(P)
    c[:, C_TILE:C_TILE + NT] = np.arange(NT)
    c[:, C_DUMMY:C_DUMMY + NT] = np.arange(NT) % 4 * P
    c[:, C_KAUG] = np.arange(P) % DH < 3
    return c


class Steps:

    def __init__(self, sem, names, first=0):
        self.sem, self.names, self.first = sem, names.split(), first

    def at(self, b, name):
        return b * len(self.names) + (self.names.index(name) + 1 + self.first)


def build(nc, x, log_A, B_w, B_b, C_w, C_b, wq, wk, wv, wo, w_router, wg, wu, wd, g1, g2, c, wmod, consts, out):
    ctx = ExitStack()
    with ctx:
        def sb(name, shape, dt=F32):
            return ctx.enter_context(nc.sbuf_tensor(name, shape, dt))

        def sem(name):
            return ctx.enter_context(nc.semaphore(name))

        mod_rows = nc.dram_tensor("mod_rows", [NB, 5 * P], F32).ap()
        q_stack_d = nc.dram_tensor("q_stack_d", [2, H, ROWS, S], BF16).ap()
        k_stack_d = nc.dram_tensor("k_stack_d", [2, H, ROWS, S], BF16).ap()
        routed = nc.dram_tensor("routed", [NROW, P], F32).ap()
        expert_out = nc.dram_tensor("expert_out", [NT * P, P], F32).ap()

        cst = sb("cst", [P, C_N])
        ident = cst[:, C_ID:C_ID + P]
        ident_b = sb("ident_b", [P, P], BF16)
        upper_b = sb("upper_b", [P, P], BF16)
        ones_b = sb("ones_b", [P, P], BF16)
        mask_b = sb("mask_b", [P, 4, P], BF16)
        zeros = sb("zeros", [P, P])
        zeros_b = sb("zeros_b", [P, S], BF16)
        kaug_b = sb("kaug_b", [P, 2 * S], BF16)
        neg_half = sb("neg_half", [P, 2])
        w_in = sb("w_in", [P, 2, P])
        bwT = sb("bwT", [P, P])
        cwT = sb("cwT", [P, P])
        cols = sb("cols", [P, 4])
        decay = sb("decay", [P, 1])
        decay_b = sb("decay_b", [P, S])
        wqkv = sb("wqkv", [P, 3, P])
        w_rot = sb("w_rot", [P, 2, P])
        wo_s = sb("wo_s", [P, P])
        wr_s = sb("wr_s", [P, NE])
        g2_b = sb("g2_b", [P, P])
        experts = sb("experts", [P, NE * EW])
        c_T = sb("c_T", [P, NB])
        c_e = sb("c_e", [P, NB])
        silu_T = sb("silu_T", [P, NB])
        wmod_s = sb("wmod_s", [P, 6 * P])
        mod_T = sb("mod_T", [P, 6, NB])
        mod_r = sb("mod_r", [NB, 6 * P])
        row_s = sb("row_s", [NB, 5 * P])
        cb_r = sb("cb_r", [NB, P])
        sgn = sb("sgn", [NB, 2, P])

        X = sb("X", [P, 2, QB, P])
        MB = sb("MB", [P, 2, 4 * P])
        GB = sb("GB", [P, 2, P])
        st = sb("st", [P, QB, 6])
        mv = sb("mv", [P, QB, 2])
        rs = sb("rs", [P, QB])
        nrm = sb("nrm", [P, QB, P])
        hT = sb("hT", [P, S])
        bx = sb("bx", [P, S])
        hs = sb("hs", [P, S])
        xg = sb("xg", [P, QB, P])
        tmp = sb("tmp", [P, QB, P])
        x1 = sb("x1", [P, QB, P])
        H2 = sb("H2", [P, TT, P])
        sq = sb("sq", [P, QB, P])
        modc = sb("modc", [P, 2, 2])
        ve = sb("ve", [P, QB])
        ve2 = sb("ve2", [P, QB])
        tiny = sb("tiny", [P, 1])
        qaug_b = sb("qaug_b", [P, 2 * S], BF16)
        ones_f = sb("ones_f", [P, NE])
        ss = sb("ss", [P, QB])
        xnT = sb("xnT", [P, S])
        r_c = sb("r_c", [P, 2, S])
        r_s = sb("r_s", [P, 2, S])
        qk = sb("qk", [P, 2, S])
        part = sb("part", [P, 3, 2, S], BF16)
        QST = sb("QST", [P, 2, H // 2, S], BF16)
        KST = sb("KST", [P, 2, H, S], BF16)
        VA = sb("VA", [P, 2, QB, H, 32])

        MX = sb("MX", [P, QB, H])
        rem = sb("rem", [P, QB, H])
        nmp = sb("nmp", [P, QB, 8, H], BF16)
        nmT = sb("nmT", [3 * H, S], BF16)
        PT = sb("PT", [P, 4, 3 * P])
        OT = sb("OT", [P, 4, S])
        rc = sb("rc", [P, QB, H])
        ON = sb("ON", [P, QB, P])
        ONT = sb("ONT", [P, S])
        h3 = sb("h3", [P, QB, P])
        gh = sb("gh", [P, QB, P])
        base = sb("base", [P, TT, P])
        sq2 = sb("sq2", [P, QB, P])
        ss2 = sb("ss2", [P, QB])
        rs2 = sb("rs2", [P, QB])
        xn2 = sb("xn2", [P, 2, QB, P])
        xn2T = sb("xn2T", [P, S])
        lg = sb("lg", [P, QB, NE])
        mx8 = sb("mx8", [P, QB, 8])
        ix8 = sb("ix8", [P, QB, 8], U32)
        ixf = sb("ixf", [P, QB, 2])
        dl = sb("dl", [P, QB])
        el = sb("el", [P, QB])
        e1 = sb("e1", [P, QB])
        w12 = sb("w12", [P, QB, 2])
        oh = sb("oh", [P, QB, 2, NE])
        ohs = sb("ohs", [P, QB, NE], BF16)
        carry = sb("carry", [P, NE])
        pall = sb("pall", [P, QB, NE])
        prod = sb("prod", [P, QB, 2, NE])
        posf = sb("posf", [P, QB, 2])
        posi = sb("posi", [P, 2, QB * 2], I32)
        POS = sb("POS", [P, TT * 2])
        WGT = sb("WGT", [P, TT * 2])

        padf = sb("padf", [P, NE])
        padi = sb("padi", [P, NE], I32)
        cnt = sb("cnt", [P, NE])
        cnti = sb("cnti", [P, NE], I32)
        cum = sb("cum", [P, NE])
        delta = sb("delta", [P, NE])
        shift = sb("shift", [P, NE])
        above = sb("above", [P, TT * 2, NE])
        moved = sb("moved", [P, TT * 2])
        GIDX = sb("GIDX", [P, TT * 2], I32)
        past = sb("past", [1, NT, NE])
        eidx = sb("eidx", [1, NT])
        first = sb("first", [1, NT])
        valid = sb("valid", [1, NT])
        tab = sb("tab", [1, 2, NT], I32)
        xin = sb("xin", [P, 4, P])
        xT = sb("xT", [P, 2, P])
        sg = sb("sg", [P, 2, HID])
        hm = sb("hm", [P, 2, HID])
        hmT = sb("hmT", [P, 2, HID])
        eo = sb("eo", [P, 2, P])
        got = sb("got", [P, 2, QB, 2, P])
        gidx = sb("gidx", [P, 2, 4], I32)
        wl = sb("wl", [P, 2, 4])
        res = sb("res", [P, 2, QB, P])

        banks = [ctx.enter_context(nc.psum_tensor(f"bank{i}", [P, 512], F32)) for i in range(8)]
        PF = banks[0:2]
        PA = banks[2:4]
        PS = banks[4:6]
        PO = banks[6:8]

        s_cst = sem("s_cst")
        s_w = sem("s_w")
        s_exp = sem("s_exp")
        s_scr = sem("s_scr")
        s_modrow = sem("s_modrow")
        s_x = [sem("s_x0"), sem("s_x1")]
        s_mb = [sem("s_mb0"), sem("s_mb1")]
        s_gt = [sem("s_gt0"), sem("s_gt1")]
        s_stw = sem("s_stw")
        s_stk = [[sem(f"s_stk{p}_{half}") for half in range(2)] for p in range(2)]
        s_nm = sem("s_nm")
        s_sc = [sem("s_sc0"), sem("s_sc1")]
        SU = {e: Steps(sem("setup_" + e), n) for e, n in dict(
            pe="bwcw modT modr", act="exp_a exp_c", pool="zero ones",
            dve="aug ea decay decb ec rc silu wT rot modT modr sgn2 sgn abs guard castb carry").items()}
        FR = {e: Steps(sem("front_" + e), n) for e, n in dict(
            pe="nT bx y xnT qk v",
            act="hT bx keep ss xnT ph pm va",
            pool="rs1 xg rs2 rs3",
            dve="st mv ve n1 scan ty x1 st2 mv2 ve2 n2 h2a h2 vs xn rc rs qk r1 pl").items()}
        MA = {e: Steps(sem("max_" + e), n) for e, n in dict(
            pe=" ".join([f"a{i}" for i in range(12)] + ["nmT"]), act="nmT",
            dve=" ".join(f"m{i}" for i in range(12)) + " nh rem nm rem2 nl").items()}
        AT = {e: Steps(sem("attn_" + e), n) for e, n in dict(
            pe=" ".join(f"{kind}{h}" for now in range(BATCH_SLOTS) for kind, when in (("s", now), ("pv", now - PV_LATER))
                        for h in heads_at(when)),
            act=" ".join(f"e{h}" for h in range(H)),
            pool=" ".join(f"c{h}" for h in range(H))).items()}
        TL = {e: Steps(sem("tail_" + e), n) for e, n in dict(
            pe="oT onT wo xT lg rank",
            act="OT onT ss xT el",
            pool="gh base rs",
            dve="rc on h3 vs xn lg mx ix ixf dl e1 w1 w2 oh ohs pall carry prod posf posi POS").items()}
        moe = {n: sem("moe_" + n) for n in "pe_xT pe_gu pe_tr pe_dn act_xT act_sg dve_hm dve_hT dve_eo".split()}
        RT = Steps(sem("tables"), "padf cnt cnt2 cnti nt cum past eidx pastn first inside valid jrow spare dummy sum row col tab startt delta shift above moves moved pos GIDX")
        LA = Steps(sem("last"), "a b g out")
        LI = Steps(sem("last_idx"), "idx")
        s_tab = sem("s_tab")
        s_idx = sem("s_idx")
        s_pad = sem("s_pad")
        s_in = [sem(f"s_in{i}") for i in range(4)]
        s_st = [sem("s_st0"), sem("s_st1")]
        s_got = [sem("s_got0"), sem("s_got1")]
        s_gb = [sem("s_gb0"), sem("s_gb1")]
        s_out = [sem("s_out0"), sem("s_out1")]
        PA_b = PA[0][:, :].bitcast(BF16)

        def run_periods(eng, step):
            def period(k, pf):
                for slot in range(SLOTS):
                    for n in reversed(range(LAGS)):
                        if not isinstance(k, int) or 0 <= k - n < NB:
                            step(k - n, (pf + n) % 2, slot + n * SLOTS)

            first = -(-(LAGS + 2) // 2)
            for k in range(2 * first):
                period(k, k % 2)
            with eng.Fori(first, NB // 2) as j:
                period(2 * j, 0)
                period(2 * j + 1, 1)
            for k in range(NB, NB + LAGS - 1):
                period(k, k % 2)

        LEAD = (WHEN["T_x2"] - WHEN["max_parts"] - 1) // SLOTS

        def run_tiles(eng, tile):
            tile(-1, 3, gu=False, tr=False, dn=False)
            tile(0, 0, tr=False, dn=False)
            tile(1, 1, dn=False)
            for T in range(2, 8):
                tile(T, T % 4)
            with eng.Fori(2, NT // 4 - 1) as j:
                for u in range(4):
                    tile(4 * j + u, u)
            for T in range(NT - 4, NT - 1):
                tile(T, T % 4)
            tile(NT - 1, 3, xt=False)
            tile(NT, 0, xt=False, gu=False)
            tile(NT + 1, 1, xt=False, gu=False, tr=False)

        def bc(ap, axis, n):
            a = ap.unsqueeze(axis)
            shape = list(a.shape)
            shape[axis] = n
            return a.to_broadcast(shape)

        def old(b, k):
            return not isinstance(b, int) or b >= k

        passed = {}

        def alone(eng):
            if id(eng) not in passed:
                passed[id(eng)] = sem(f"passed{len(passed)}")
            eng.sem_inc(passed[id(eng)], 1)

        block = ctx.enter_context(nc.Block())

        @block.sync
        def _(sp):
            sp.dma_start(cst[:, :], consts).then_inc(s_cst, 16)
            sp.dma_start(w_in[:, 0, :], B_w).then_inc(s_w, 16)
            sp.dma_start(w_in[:, 1, :], C_w).then_inc(s_w, 16)
            sp.dma_start(wmod_s[:, :], wmod).then_inc(s_w, 16)
            with nc.allow_non_contiguous_dma(reason="small transposed loads"):
                sp.dma_start(c_T[:, :], c.rearrange("b d -> d b")).then_inc(s_w, 16)
                for i, v in enumerate((log_A, B_b, g1)):
                    sp.dma_start(cols[:, i:i + 1], v.rearrange("(d a) -> d a", a=1)).then_inc(s_w, 16)
            for i, w in enumerate((wq, wk, wv)):
                sp.dma_start(wqkv[:, i, :], w).then_inc(s_w, 16)
            sp.dma_start(wo_s[:, :], wo).then_inc(s_w, 16)
            sp.dma_start(wr_s[:, :], w_router).then_inc(s_w, 16)
            sp.dma_start(g2_b[:, :], g2.partition_broadcast(P)).then_inc(s_w, 16)
            sp.dma_start(cb_r[:, :], C_b.partition_broadcast(NB)).then_inc(s_w, 16)
            sp.wait_ge(SU["dve"].sem, SU["dve"].at(0, "aug"))
            for p in range(2):
                for dst, src in ((k_stack_d, kaug_b), (q_stack_d, qaug_b)):
                    sp.dma_start(dst[p].rearrange("h (d s) k -> (h d) s k", s=8)[:, AUG:8, :],
                                 src[:, :].rearrange("r (s k) -> r s k", s=2)).then_inc(s_scr, 16)
            for i in range(4):
                sp.dma_start(routed[NE * REG + i * P:NE * REG + (i + 1) * P, :], zeros[:, :]).then_inc(s_scr, 16)
            sp.wait_ge(SU["dve"].sem, SU["dve"].at(0, "castb"))
            sp.dma_start(mod_rows, row_s[:, :]).then_inc(s_modrow, 16)
            sp.wait_ge(s_modrow, 16)
            sp.wait_ge(s_scr, 16 * 8)

            def front_load(b, p):
                if old(b, 2):
                    sp.wait_ge(FR["dve"].sem, FR["dve"].at(b - 2, "st"))
                    alone(sp)
                    sp.wait_ge(FR["pool"].sem, FR["pool"].at(b - 2, "xg"))
                    alone(sp)
                    sp.wait_ge(FR["dve"].sem, FR["dve"].at(b - 2, "n1"))
                    alone(sp)
                sp.dma_start(X[:, p, :, :], x[bass.ds(b, 1), :, :].rearrange("a (t p) d -> p (a t) d", p=P)).then_inc(s_x[p], 16)
                if old(b, 2):
                    sp.wait_ge(FR["dve"].sem, FR["dve"].at(b - 2, "h2"))
                    alone(sp)
                sp.dma_start(MB[:, p, :], mod_rows[bass.ds(b, 1), 0:4 * P].to_broadcast([P, 4 * P])).then_inc(s_mb[p], 16)

            def gate_load(b, p):
                if old(b, 2):
                    sp.wait_ge(TL["pool"].sem, TL["pool"].at(b - 2, "gh"))
                    alone(sp)
                sp.dma_start(GB[:, p, :], mod_rows[bass.ds(b, 1), M_GB * P:].to_broadcast([P, P])).then_inc(s_gt[p], 16)

            def front_stack(b, p):
                if old(b, 2):
                    for half in range(2):
                        sp.wait_ge(s_stk[p][half], 24 * (b - p))
                        alone(sp)
                for i, (e, name) in enumerate((("act", "ph"), ("act", "pm"), ("dve", "pl"))):
                    sp.wait_ge(FR[e].sem, FR[e].at(b, name))
                    alone(sp)
                    for qk_i, (slots, dst) in enumerate(((Q_SLOTS, q_stack_d), (K_SLOTS, k_stack_d))):
                        _, slot, step, n = slots[i]
                        to = dst[p].rearrange("h (d s) k -> (h d) s k", s=8)[:, slot:slot + step * (n - 1) + 1:step, :]
                        sp.dma_start(to, bc(part[:, i, qk_i, :], 1, n)).then_inc(s_stw, 16)
                sp.wait_ge(s_stw, 96 * b + 96)
                alone(sp)
                for half in range(2):
                    h0 = half * H // 2
                    if old(b, 2):
                        sp.wait_ge(AT["pe"].sem, AT["pe"].at(b - 2, f"s{h0 + H // 2 - 1}"))
                        alone(sp)
                    sp.dma_start(QST[:, p, h0 // 2:h0 // 2 + H // 4, :],
                                 q_stack_d[p][h0:h0 + H // 2].rearrange("(t j) r k -> (j r) t k", j=2)
                                 ).then_inc(s_stk[p][half], 16)
                    for j in range(2):
                        sp.dma_start(KST[64 * j:64 * j + 64, p, h0 + j:h0 + H // 2:2, :],
                                     k_stack_d[p][h0:h0 + H // 2].rearrange("(t j) r k -> j r t k", j=2)[j]
                                     ).then_inc(s_stk[p][half], 16)

            def attn_max(a, p):
                sp.wait_ge(MA["act"].sem, MA["act"].at(a, "nmT"))
                alone(sp)
                for j in range(2):
                    for i in range(3):
                        r = 64 * j + 8 * i + AUG
                        sp.dma_start(QST[r:r + 1, p, :, :], nmT[16 * i + j:16 * (i + 1):2, :]).then_inc(s_nm, 16)

            def step(b, p, now):
                if now == WHEN["load"]:
                    front_load(b, p)
                if now == WHEN["stack"]:
                    front_stack(b, p)
                if now == WHEN["max_rows"]:
                    attn_max(b, p)
                if now == WHEN["load_gate"]:
                    gate_load(b, p)

            run_periods(sp, step)

            sp.wait_ge(s_tab, 3)
            alone(sp)
            sp.wait_ge(s_pad, 16 * NE)
            alone(sp)

            def tile_load(T, p):
                row = sp.value_load(tab[0:1, 0, bass.ds(T, 1)], min_val=0, max_val=NROW - P)
                if old(T, 4):
                    sp.wait_ge(moe["pe_xT"], T - 4 + 1)
                    alone(sp)
                sp.dma_start(xin[:, p, :], routed[bass.ds(row, P), :]).then_inc(s_in[p], 16)

            for T in range(4):
                tile_load(T, T)
            with sp.Fori(1, NT // 4) as j:
                for u in range(4):
                    tile_load(4 * j + u, u)

            def last_load(b, p):
                if old(b, 2):
                    sp.wait_ge(LA.sem, LA.at(b - 2, "g"))
                    alone(sp)
                else:
                    sp.wait_ge(TL["pool"].sem, TL["pool"].at(NB - 1, "gh"))
                    alone(sp)
                sp.dma_start(GB[:, p, :], mod_rows[bass.ds(b, 1), M_GB * P:].to_broadcast([P, P])).then_inc(s_gb[p], 16)
                if old(b, 2):
                    last_store(b - 2, p)

            def last_store(b, p):
                sp.wait_ge(LA.sem, LA.at(b, "out"))
                alone(sp)
                sp.dma_start(out[bass.ds(b, 1), :, :].rearrange("a (t p) d -> p (a t) d", p=P), res[:, p, :, :]).then_inc(s_out[p], 16)

            last_load(0, 0)
            last_load(1, 1)
            with sp.Fori(1, NB // 2) as j:
                last_load(2 * j, 0)
                last_load(2 * j + 1, 1)
            last_store(NB - 2, 0)
            last_store(NB - 1, 1)
            for p in range(2):
                sp.wait_ge(s_out[p], 16 * NB // 2)
                alone(sp)

        @block.gpsimd
        def _(pool):
            pool.memset(zeros[:, :], 0.0)
            pool.memset(neg_half[:, :], -0.5)
            pool.memset(KST[:, :, :, :], 0.0)
            pool.memset(VA[:, :, :, :, :], 0.0)
            pool.memset(qaug_b[:, :], 0.0).then_inc(SU["pool"].sem, 1)
            pool.wait_ge(SU["pool"].sem, 1)
            pool.memset(VA[:, :, :, :, DH:DH + 1], 1.0).then_inc(SU["pool"].sem, 1)

            def rstd(stage, name, dve, src, dst, b):
                pool.wait_ge(dve[0].sem, dve[0].at(b, dve[1]))
                pool.tensor_tensor(dst, src, neg_half[:, :], ALU.pow).then_inc(stage.sem, 1)

            def front(b, p, now):
                if now == WHEN["rstd1"]:
                    rstd(FR["pool"], "rs1", (FR["dve"], "ve"), ve[:, :], rs[:, :], b)
                if now == WHEN["xg"]:
                    pool.wait_ge(s_mb[p], 8 * (b - p) + 16)
                    pool.wait_ge(s_x[p], 8 * (b - p) + 16)
                    if old(b, 1):
                        pool.wait_ge(FR["dve"].sem, FR["dve"].at(b - 1, "x1"))
                    pool.tensor_tensor(xg[:, :, :], X[:, p, :, :], bc(MB[:, p, M_CBGA * P:(M_CBGA + 1) * P], 1, QB),
                                       ALU.add).then_inc(FR["pool"].sem, 1)
                if now == WHEN["rstd2"]:
                    rstd(FR["pool"], "rs2", (FR["dve"], "ve2"), ve[:, :], rs[:, :], b)
                if now == WHEN["rstd3"]:
                    rstd(FR["pool"], "rs3", (FR["dve"], "vs"), ve[:, :], rs[:, :], b)

            def attn_head(a, p, h):
                pool.wait_ge(AT["act"].sem, AT["act"].at(a, f"e{h}"))
                alone(pool)
                d = PT[:, h % 4, :].rearrange("p (x q) -> p x q", x=3)[:, 0:3:2, :]
                pool.affine_select(out=d, in_=d, compare_op=ALU.is_ge, fill=0.0, base=0,
                                   pattern=[[0, 2], [1, P]], channel_multiplier=-1).then_inc(AT["pool"].sem, 1)

            def tail(t, p, now):
                if now == WHEN["base"]:
                    pool.wait_ge(s_gt[p], 8 * (t - p) + 16)
                    pool.wait_ge(TL["dve"].sem, TL["dve"].at(t, "h3"))
                    pool.tensor_tensor(gh[:, :, :], h3[:, :, :], bc(GB[:, p, :], 1, QB),
                                       ALU.mult).then_inc(TL["pool"].sem, 1)
                    pool.wait_ge(TL["pool"].sem, TL["pool"].at(t, "gh"))
                    pool.wait_ge(FR["act"].sem, FR["act"].at(t, "keep"))
                    pool.tensor_tensor(base[:, bass.ds(t * QB, QB), :], gh[:, :, :], base[:, bass.ds(t * QB, QB), :],
                                       ALU.add).then_inc(TL["pool"].sem, 1)
                if now == WHEN["rstd4"]:
                    rstd(TL["pool"], "rs", (TL["dve"], "vs"), ve2[:, :], rs2[:, :], t)

            def scatter(z, p, i, k):
                pool.wait_ge(TL["dve"].sem, TL["dve"].at(z, "posi"))
                alone(pool)
                pool.indirect_dma_start(
                    routed[:, :], bass.IndirectOffsetOnAxis(ap=posi[:, p, 2 * i + k:2 * i + k + 1], axis=0),
                    xn2[:, p, i, :], None).then_inc(s_sc[p], 16)

            def step(b, p, now):
                for h in heads_at(now):
                    attn_head(b, p, h)
                for n, when in enumerate(WHEN["scatters"]):
                    if now == when:
                        scatter(b, p, *divmod(n, 2))
                tail(b, p, now)
                front(b, p, now)

            run_periods(pool, step)

            pool.wait_ge(s_idx, 1)
            for e in range(NE):
                pool.indirect_dma_start(routed[:, :], bass.IndirectOffsetOnAxis(ap=padi[:, e:e + 1], axis=0),
                                        zeros[:, :], None).then_inc(s_pad, 16)
            for p in range(2):
                pool.wait_ge(s_sc[p], 64 * NB // 2)
            pool.sem_inc(s_tab, 1)
            pool.wait_ge(s_tab, 3)

            def tile_store(T, p):
                pool.wait_ge(moe["dve_eo"], T + 1)
                pool.dma_start(expert_out[bass.ds(T * P, P), :], eo[:, p, :]).then_inc(s_st[p], 16)

            with pool.Fori(0, NT // 2) as j:
                tile_store(2 * j, 0)
                tile_store(2 * j + 1, 1)
            for p in range(2):
                pool.wait_ge(s_st[p], 16 * NT // 2)

            def gather(b, p):
                pool.wait_ge(LI.sem, LI.at(b, "idx"))
                alone(pool)
                for i in range(QB):
                    for k in range(2):
                        pool.indirect_dma_start(
                            got[:, p, i, k, :], None, expert_out[:, :],
                            bass.IndirectOffsetOnAxis(ap=gidx[:, p, 2 * i + k:2 * i + k + 1], axis=0)).then_inc(s_got[p], 16)

            with pool.Fori(0, NB // 2) as j:
                gather(2 * j, 0)
                gather(2 * j + 1, 1)

        @block.scalar
        def _(act):
            A, B, C = FR["act"], AT["act"], TL["act"]
            wg_v, wu_v = wg.rearrange("e d h -> d e h"), wu.rearrange("e d h -> d e h")
            ex = experts[:, :].rearrange("p (e n) -> p e n", e=NE)
            act.dma_start(ex[:, :, 0:HID], wg_v).then_inc(s_exp, 16)
            act.dma_start(ex[:, :, HID:2 * HID], wu_v).then_inc(s_exp, 16)
            for e in range(NE):
                act.dma_start(ex[:, e, 2 * HID:].rearrange("p (c d) -> p c d", c=HC),
                              wd[e].rearrange("(c p) d -> p c d", p=P)).then_inc(s_exp, 16)
            act.wait_ge(s_w, 16 * N_W)
            act.activation(decay[:, :], cols[:, 0:1], ACT.Exp, scale=-1.0).then_inc(SU["act"].sem, 1)
            act.activation(c_e[:, :], c_T[:, :], ACT.Exp, scale=-1.0).then_inc(SU["act"].sem, 1)
            act.wait_ge(SU["dve"].sem, SU["dve"].at(0, "carry"))

            def front(b, p, now):
                if now == WHEN["h"]:
                    act.wait_ge(FR["pe"].sem, FR["pe"].at(b, "nT"))
                    act.activation(hT[:, :], PF[0][:, 0:S], ACT.Identity, scale=modc[:, p, 0:1],
                                   bias=modc[:, p, 1:2]).then_inc(A.sem, 1)
                if now == WHEN["bx"]:
                    act.wait_ge(FR["pe"].sem, FR["pe"].at(b, "bx"))
                    if old(b, 1):
                        act.wait_ge(FR["dve"].sem, FR["dve"].at(b - 1, "scan"))
                    act.activation(bx[:, :], PF[1][:, 0:S], ACT.Identity, bias=cols[:, 1:2]).then_inc(A.sem, 1)
                if now == WHEN["keep"]:
                    act.wait_ge(FR["dve"].sem, FR["dve"].at(b, "x1"))
                    act.activation(base[:, bass.ds(b * QB, QB), :], x1[:, :, :], ACT.Copy).then_inc(A.sem, 1)
                if now == WHEN["squares"]:
                    act.wait_ge(FR["dve"].sem, FR["dve"].at(b, "h2"))
                    for i in range(QB):
                        r = act.activation(sq[:, i, :], H2[:, bass.ds(b * QB + i, 1), :].rearrange("p a d -> p (a d)"), ACT.Square, accum_out=ss[:, i:i + 1])
                    r.then_inc(A.sem, 1)
                if now == WHEN["xT"]:
                    act.wait_ge(FR["pe"].sem, FR["pe"].at(b, "xnT"))
                    act.activation(xnT[:, :], PF[1][:, 0:S], ACT.Copy, scale=cols[:, 2:3]).then_inc(A.sem, 1)
                if now == WHEN["part0"]:
                    act.wait_ge(FR["dve"].sem, FR["dve"].at(b, "qk"))
                    if old(b, 1):
                        act.wait_ge(s_stw, 96 * b)
                    act.activation(part[:, 0, :, :], qk[:, :, :], ACT.Copy).then_inc(A.sem, 1)
                if now == WHEN["part1"]:
                    act.wait_ge(FR["dve"].sem, FR["dve"].at(b, "r1"))
                    act.activation(part[:, 1, :, :], qk[:, :, :], ACT.Copy).then_inc(A.sem, 1)

            def values(b, p):
                act.wait_ge(FR["pe"].sem, FR["pe"].at(b, "v"))
                if old(b, 2):
                    act.wait_ge(AT["pe"].sem, AT["pe"].at(b - 2, f"pv{H - 1}"))
                for i in range(QB):
                    r = act.activation(VA[:, p, i, :, 0:DH],
                                       PF[0][:, i * P:(i + 1) * P].rearrange("p (h d) -> p h d", h=H), ACT.Copy)
                r.then_inc(A.sem, 1)

            def attn_max(a, p):
                act.wait_ge(MA["pe"].sem, MA["pe"].at(a, "nmT"))
                if old(a, 1):
                    act.wait_ge(s_nm, 96 * a)
                act.activation(nmT[:, :], PA_b[0:3 * H, 0:S], ACT.Copy).then_inc(MA["act"].sem, 1)

            def attn_head(a, p, h):
                act.wait_ge(AT["pe"].sem, AT["pe"].at(a, f"s{h}"))
                if h >= 4:
                    act.wait_ge(AT["pe"].sem, AT["pe"].at(a, f"pv{h - 4}"))
                elif old(a, 1):
                    act.wait_ge(AT["pe"].sem, AT["pe"].at(a - 1, f"pv{H - 4 + h}"))
                act.activation(PT[:, h % 4, :], PS[h % 2][:, 0:3 * P], ACT.Exp, scale=SCALE).then_inc(B.sem, 1)

            def tail(t, p, now):
                if now == WHEN["o_copy"]:
                    act.wait_ge(AT["pe"].sem, AT["pe"].at(t, f"pv{H - 1}"))
                    for i in range(2):
                        r = act.activation(OT[:, 2 * i:2 * i + 2, :], PO[i][:, :], ACT.Copy)
                    r.then_inc(C.sem, 1)
                if now == WHEN["onT"]:
                    act.wait_ge(TL["pe"].sem, TL["pe"].at(t, "onT"))
                    act.activation(ONT[:, :], PO[0][:, 0:S], ACT.Copy).then_inc(C.sem, 1)
                if now == WHEN["squares2"]:
                    act.wait_ge(TL["dve"].sem, TL["dve"].at(t, "h3"))
                    for i in range(QB):
                        r = act.activation(sq2[:, i, :], h3[:, i, :], ACT.Square, accum_out=ss2[:, i:i + 1])
                    r.then_inc(C.sem, 1)
                if now == WHEN["x2T"]:
                    act.wait_ge(TL["pe"].sem, TL["pe"].at(t, "xT"))
                    act.activation(xn2T[:, :], PA[1][:, 0:S], ACT.Copy).then_inc(C.sem, 1)
                if now == WHEN["exp_d"]:
                    act.wait_ge(TL["dve"].sem, TL["dve"].at(t, "dl"))
                    act.activation(el[:, :], dl[:, :], ACT.Exp).then_inc(C.sem, 1)

            def step(b, p, now):
                if now == WHEN["v"]:
                    values(b, p)
                if now == WHEN["max_T"]:
                    attn_max(b, p)
                for h in heads_at(now):
                    attn_head(b, p, h)
                tail(b, p, now)
                front(b, p, now)

            run_periods(act, step)

            def tile(T, u, xt=True, gu=True, tr=True, dn=True):
                p = u % 2
                if xt:
                    act.wait_ge(moe["pe_xT"], T + 1 + 1)
                    if old(T, 1):
                        act.wait_ge(moe["pe_gu"], T)
                    act.activation(xT[:, 1 - p, :], PO[0][:, 0:P], ACT.Copy).then_inc(moe["act_xT"], 1)
                if gu:
                    act.wait_ge(moe["pe_gu"], T + 1)
                    if old(T, 2):
                        act.wait_ge(moe["dve_hm"], T - 1)
                    act.activation(sg[:, p, :], PA[p][:, 0:HID], ACT.Silu).then_inc(moe["act_sg"], 1)

            run_tiles(act, tile)

        @block.vector
        def _(dve):
            D = SU["dve"]

            def link(ins, stage=D):
                return ins.then_inc(stage.sem, 1)

            def setup_done(name):
                dve.wait_ge(D.sem, D.at(0, name))

            dve.wait_ge(s_cst, 16)
            dve.wait_ge(s_w, 16 * N_W)
            dve.memset(ones_f[:, :], 1.0)
            dve.memset(nmp[:, :, :, :], 0.0)
            dve.tensor_copy(ident_b[:, :], ident)
            dve.tensor_copy(upper_b[:, :], cst[:, C_UP:C_UP + P])
            dve.tensor_copy(mask_b[:, :, :], bc(cst[:, C_MASK:C_MASK + P], 1, 4))
            dve.memset(ones_b[:, :], 1.0)
            dve.tensor_copy(carry[:, :], cst[:, C_OFF:C_OFF + NE])
            dve.tensor_copy(kaug_b[:, 0:S], cst[:, C_KAUG:C_KAUG + 1].to_broadcast([P, S]))
            dve.memset(kaug_b[:, S:2 * S], 0.0)
            dve.wait_ge(SU["pool"].sem, 2)
            link(dve.memset(tiny[:, :], 0.0))
            dve.wait_ge(SU["act"].sem, 1)
            link(dve.tensor_scalar_add(decay[:, :], decay[:, :], 1.0))
            setup_done("ea")
            link(dve.reciprocal(decay[:, :], decay[:, :]))
            setup_done("decay")
            link(dve.tensor_copy(decay_b[:, :], decay[:, :].to_broadcast([P, S])))
            dve.wait_ge(SU["act"].sem, 2)
            link(dve.tensor_scalar_add(c_e[:, :], c_e[:, :], 1.0))
            setup_done("ec")
            link(dve.reciprocal(c_e[:, :], c_e[:, :]))
            setup_done("rc")
            link(dve.tensor_tensor(silu_T[:, :], c_T[:, :], c_e[:, :], ALU.mult))
            dve.wait_ge(SU["pe"].sem, SU["pe"].at(0, "bwcw"))
            dve.tensor_copy(bwT[:, :], PF[0][:, 0:P])
            link(dve.tensor_copy(cwT[:, :], PF[0][:, P:2 * P]))
            for i in range(2):
                src = wqkv[:, i, :].rearrange("p (h x d) -> p h x d", h=H, x=2)
                dst = w_rot[:, i, :].rearrange("p (h x d) -> p h x d", h=H, x=2)
                dve.tensor_scalar(dst[:, :, 0, :], src[:, :, 1, :], -1.0, None, ALU.mult)
                r = dve.tensor_copy(dst[:, :, 1, :], src[:, :, 0, :])
            link(r)
            dve.wait_ge(SU["pe"].sem, SU["pe"].at(0, "modT"))
            dve.tensor_copy(mod_T[:, 0, :], PF[1][:, 0:NB])
            link(dve.tensor_scalar_add(mod_T[:, 1, :], PF[1][:, NB:2 * NB], 1.0))
            dve.wait_ge(SU["pe"].sem, SU["pe"].at(0, "modr"))
            dve.tensor_copy(mod_r[:, 0:3 * P], PA[0][0:NB, 0:3 * P])
            link(dve.tensor_copy(mod_r[:, 3 * P:6 * P], PA[1][0:NB, 0:3 * P]))
            setup_done("modr")
            gates = mod_r[:, :].rearrange("b (x d) -> b x d", x=6)[:, 2:6:3, :]
            rows = row_s[:, :].rearrange("b (x d) -> b x d", x=5)
            link(dve.tensor_scalar(sgn[:, :, :], gates, 0.0, 2.0, ALU.is_ge, ALU.mult))
            setup_done("sgn2")
            link(dve.tensor_scalar(sgn[:, :, :], sgn[:, :, :], 1.0, None, ALU.subtract))
            setup_done("sgn")
            link(dve.tensor_tensor(rows[:, 0:5:4, :], gates, sgn[:, :, :], ALU.mult))
            setup_done("abs")
            link(dve.scalar_tensor_tensor(out=rows[:, 0:5:4, :], in0=rows[:, 0:5:4, :], scalar=0.25, in1=sgn[:, :, :],
                                          op0=ALU.max, op1=ALU.mult))
            setup_done("guard")
            dve.tensor_tensor(rows[:, M_CBGA, :], rows[:, M_GA, :], cb_r[:, :], ALU.mult)
            dve.tensor_scalar_add(rows[:, M_CB1, :], mod_r[:, 4 * P:5 * P], 1.0)
            link(dve.tensor_copy(rows[:, M_SB, :], mod_r[:, 3 * P:4 * P]))
            link(dve.memset(tiny[:, :], 0.0))
            setup_done("carry")

            F, B, C = FR["dve"], MA["dve"], TL["dve"]

            def layernorm_stats(b, src, stage, names):
                for i in range(QB):
                    r = dve.bn_stats(st[:, i, :], src(i))
                link(r, F)
                dve.wait_ge(F.sem, F.at(b, names[0]))
                alone(dve)
                for i in range(QB):
                    r = dve.bn_aggr(mv[:, i, :], st[:, i, :])
                link(r, F)
                dve.wait_ge(F.sem, F.at(b, names[1]))
                link(dve.tensor_scalar_add(ve[:, :], mv[:, :, 1], LN_EPS), F)

            def normalise(dst, src):
                for i in range(QB):
                    r = dve.tensor_scalar(dst[:, i, :], src(i), mv[:, i, 0:1], rs[:, i:i + 1],
                                          ALU.subtract, ALU.mult)
                link(r, F)

            def front(b, p, now):
                if now == WHEN["stats"]:
                    dve.wait_ge(s_x[p], 8 * (b - p) + 16)
                    if old(b, 1):
                        dve.wait_ge(FR["pool"].sem, FR["pool"].at(b - 1, "rs3"))
                    if old(b, 2):
                        dve.wait_ge(FR["act"].sem, FR["act"].at(b - 2, "hT"))
                    dve.tensor_copy(modc[:, p, 0:1], mod_T[:, 1, bass.ds(b, 1)])
                    dve.tensor_copy(modc[:, p, 1:2], mod_T[:, 0, bass.ds(b, 1)])
                    layernorm_stats(b, lambda i: X[:, p, i, :], F, ("st", "mv"))
                if now == WHEN["norm1"]:
                    dve.wait_ge(FR["pool"].sem, FR["pool"].at(b, "rs1"))
                    if old(b, 1):
                        dve.wait_ge(FR["pe"].sem, FR["pe"].at(b - 1, "xnT"))
                    normalise(nrm, lambda i: X[:, p, i, :])
                if now == WHEN["scan"]:
                    dve.wait_ge(FR["act"].sem, FR["act"].at(b, "bx"))
                    if old(b, 1):
                        dve.wait_ge(FR["pe"].sem, FR["pe"].at(b - 1, "y"))
                    link(dve.tensor_tensor_scan(hs[:, :], decay_b[:, :], bx[:, :], 0.0, ALU.mult, ALU.add), F)
                if now == WHEN["x1"]:
                    dve.wait_ge(FR["pe"].sem, FR["pe"].at(b, "y"))
                    dve.wait_ge(s_mb[p], 8 * (b - p) + 16)
                    link(dve.tensor_tensor(tmp[:, :, :], PF[0][:, 0:S].rearrange("p (t d) -> p t d", t=QB),
                                           bc(MB[:, p, 0:P], 1, QB), ALU.mult), F)
                    dve.wait_ge(F.sem, F.at(b, "ty"))
                    dve.wait_ge(FR["pool"].sem, FR["pool"].at(b, "xg"))
                    if old(b, 1):
                        dve.wait_ge(FR["act"].sem, FR["act"].at(b - 1, "keep"))
                    link(dve.tensor_tensor(x1[:, :, :], tmp[:, :, :], xg[:, :, :], ALU.add), F)
                    dve.wait_ge(F.sem, F.at(b, "x1"))
                    layernorm_stats(b, lambda i: x1[:, i, :], F, ("st2", "mv2"))
                if now == WHEN["norm2"]:
                    dve.wait_ge(FR["pool"].sem, FR["pool"].at(b, "rs2"))
                    dve.wait_ge(FR["pe"].sem, FR["pe"].at(b, "nT"))
                    normalise(nrm, lambda i: x1[:, i, :])
                if now == WHEN["h2"]:
                    dve.wait_ge(F.sem, F.at(b, "n2"))
                    link(dve.tensor_tensor(H2[:, bass.ds(b * QB, QB), :], nrm[:, :, :], bc(MB[:, p, M_CB1 * P:(M_CB1 + 1) * P], 1, QB),
                                           ALU.mult), F)
                    dve.wait_ge(F.sem, F.at(b, "h2a"))
                    link(dve.tensor_tensor(H2[:, bass.ds(b * QB, QB), :], H2[:, bass.ds(b * QB, QB), :], bc(MB[:, p, M_SB * P:(M_SB + 1) * P], 1, QB),
                                           ALU.add), F)
                if now == WHEN["mean3"]:
                    dve.wait_ge(FR["act"].sem, FR["act"].at(b, "ss"))
                    link(dve.tensor_scalar(ve[:, :], ss[:, :], 1.0 / P, RMS_EPS, ALU.mult, ALU.add), F)
                if now == WHEN["norm3"]:
                    dve.wait_ge(FR["pool"].sem, FR["pool"].at(b, "rs3"))
                    for i in range(QB):
                        r = dve.tensor_scalar(nrm[:, i, :], H2[:, bass.ds(b * QB + i, 1), :].rearrange("p a d -> p (a d)"), rs[:, i:i + 1], None, ALU.mult)
                    link(r, F)
                if now == WHEN["rope"]:
                    dve.wait_ge(FR["pe"].sem, FR["pe"].at(b, "qk"))
                    two = lambda t: t[:, :].rearrange("p (x k) -> p x k", x=2)
                    link(dve.tensor_tensor(r_c[:, :, :], two(PF[0]), bc(cst[:, C_COS:C_COS + S], 1, 2), ALU.mult), F)
                    link(dve.tensor_tensor(r_s[:, :, :], two(PF[1]), bc(cst[:, C_SIN:C_SIN + S], 1, 2), ALU.mult), F)
                    dve.wait_ge(F.sem, F.at(b, "rs"))
                    link(dve.tensor_tensor(qk[:, :, :], r_c[:, :, :], r_s[:, :, :], ALU.add), F)
                if now == WHEN["rest1"]:
                    dve.wait_ge(FR["act"].sem, FR["act"].at(b, "ph"))
                    link(dve.tensor_tensor(qk[:, :, :], qk[:, :, :], part[:, 0, :, :], ALU.subtract), F)
                if now == WHEN["part2"]:
                    dve.wait_ge(FR["act"].sem, FR["act"].at(b, "pm"))
                    link(dve.tensor_tensor(part[:, 2, :, :], qk[:, :, :], part[:, 1, :, :], ALU.subtract), F)

            def attn_unit(a, p, u):
                g, k = divmod(u, 3)
                dve.wait_ge(MA["pe"].sem, MA["pe"].at(a, f"a{u}"))
                if k == 0:
                    dst, src = MX[:, 0, 4 * g:4 * g + 4], PA[u % 2][:, :].rearrange("p (h k) -> p h k", h=4)
                else:
                    h = 4 * g + 2 * (k - 1)
                    dst, src = MX[:, 1, h:h + 2], PA[u % 2][:, :].rearrange("p (h k) -> p h k", h=2)
                link(dve.tensor_reduce(dst, src, op=ALU.max, axis=AX_X), B)

            def attn_max(a, p):
                dve.wait_ge(B.sem, B.at(a, "m11"))
                if old(a, 1):
                    dve.wait_ge(MA["pe"].sem, MA["pe"].at(a - 1, "nmT"))
                link(dve.tensor_scalar(nmp[:, :, 0, :], MX[:, :, :], -1.0, None, ALU.mult), B)
                dve.wait_ge(B.sem, B.at(a, "nh"))
                link(dve.scalar_tensor_tensor(out=rem[:, :, :], in0=MX[:, :, :], scalar=-1.0, in1=nmp[:, :, 0, :],
                                              op0=ALU.mult, op1=ALU.subtract), B)
                dve.wait_ge(B.sem, B.at(a, "rem"))
                link(dve.tensor_copy(nmp[:, :, 1, :], rem[:, :, :]), B)
                dve.wait_ge(B.sem, B.at(a, "nm"))
                link(dve.tensor_tensor(rem[:, :, :], rem[:, :, :], nmp[:, :, 1, :], ALU.subtract), B)
                dve.wait_ge(B.sem, B.at(a, "rem2"))
                link(dve.tensor_copy(nmp[:, :, 2, :], rem[:, :, :]), B)

            def tail(t, p, now):
                def chain(ins, name):
                    link(ins, C)
                    dve.wait_ge(C.sem, C.at(t, name))

                if now == WHEN["divide"]:
                    dve.wait_ge(TL["pe"].sem, TL["pe"].at(t, "oT"))
                    heads = [PO[i][:, :].rearrange("p (h r) -> p h r", r=32) for i in range(QB)]
                    for i in range(QB):
                        r = dve.reciprocal(rc[:, i, :], heads[i][:, :, DH])
                    chain(r, "rc")
                    for i in range(QB):
                        r = dve.tensor_tensor(ON[:, i, :].rearrange("p (h d) -> p h d", h=H), heads[i][:, :, 0:DH],
                                              bc(rc[:, i, :], 2, DH), ALU.mult)
                    link(r, C)
                if now == WHEN["h3"]:
                    dve.wait_ge(TL["pe"].sem, TL["pe"].at(t, "wo"))
                    link(dve.tensor_tensor(h3[:, :, :], PO[1][:, 0:S].rearrange("p (t d) -> p t d", t=QB),
                                           H2[:, bass.ds(t * QB, QB), :], ALU.add), C)
                if now == WHEN["mean4"]:
                    dve.wait_ge(TL["act"].sem, TL["act"].at(t, "ss"))
                    link(dve.tensor_scalar(ve2[:, :], ss2[:, :], 1.0 / P, RMS_EPS, ALU.mult, ALU.add), C)
                if now == WHEN["x2"]:
                    dve.wait_ge(TL["pool"].sem, TL["pool"].at(t, "rs"))
                    if old(t, 2):
                        dve.wait_ge(s_sc[p], 32 * (t - p))
                    for i in range(QB):
                        r = dve.scalar_tensor_tensor(out=xn2[:, p, i, :], in0=h3[:, i, :], scalar=rs2[:, i:i + 1],
                                                     in1=g2_b[:, :], op0=ALU.mult, op1=ALU.mult)
                    link(r, C)
                if now == WHEN["top2"]:
                    dve.wait_ge(TL["pe"].sem, TL["pe"].at(t, "lg"))
                    chain(dve.tensor_copy(lg[:, :, :], PA[1][:, 0:QB * NE].rearrange("p (t e) -> p t e", t=QB)), "lg")
                    alone(dve)
                    for i in range(QB):
                        r = dve.max(mx8[:, i, :], lg[:, i, :])
                    chain(r, "mx")
                    alone(dve)
                    for i in range(QB):
                        r = dve.max_index(ix8[:, i, :], mx8[:, i, :], lg[:, i, :])
                    chain(r, "ix")
                    chain(dve.tensor_copy(ixf[:, :, :], ix8[:, :, 0:2]), "ixf")
                    link(dve.tensor_tensor(dl[:, :], mx8[:, :, 1], mx8[:, :, 0], ALU.subtract), C)
                if now == WHEN["weights"]:
                    w = WGT[:, bass.ds(t * 4, 4)].rearrange("p (t k) -> p t k", t=QB)
                    dve.wait_ge(TL["act"].sem, TL["act"].at(t, "el"))
                    chain(dve.tensor_scalar_add(e1[:, :], el[:, :], 1.0), "e1")
                    chain(dve.reciprocal(w12[:, :, 0], e1[:, :]), "w1")
                    chain(dve.tensor_tensor(w12[:, :, 1], w12[:, :, 0], el[:, :], ALU.mult), "w2")
                    dve.tensor_copy(w, w12[:, :, :])
                    chain(dve.tensor_tensor(oh[:, :, :, :], bc(bc(cst[:, C_IOTA:C_IOTA + NE], 1, 2), 1, QB),
                                            bc(ixf[:, :, :], 3, NE), ALU.is_equal), "oh")
                    link(dve.tensor_tensor(ohs[:, :, :], oh[:, :, 0, :], oh[:, :, 1, :], ALU.add), C)
                if now == WHEN["rows"]:
                    dve.wait_ge(TL["pe"].sem, TL["pe"].at(t, "rank"))
                    rk = PA[1][:, 0:3 * NE].rearrange("p (t e) -> p t e", t=3)
                    chain(dve.tensor_tensor(pall[:, :, :], rk[:, 0:QB, :], bc(carry[:, :], 1, QB), ALU.add), "pall")
                    chain(dve.tensor_tensor(carry[:, :], rk[:, QB, :], carry[:, :], ALU.add), "carry")
                    chain(dve.tensor_tensor(prod[:, :, :, :], oh[:, :, :, :], bc(pall[:, :, :], 2, 2), ALU.mult), "prod")
                    chain(dve.tensor_reduce(posf[:, :, :], prod[:, :, :, :], op=ALU.add, axis=AX_X), "posf")
                    link(dve.tensor_copy(posi[:, p, :], posf[:, :, :].rearrange("p t k -> p (t k)")), C)
                    link(dve.tensor_copy(POS[:, bass.ds(t * 4, 4)], posf[:, :, :].rearrange("p t k -> p (t k)")), C)

            def step(b, p, now):
                for u in units_at(now):
                    attn_unit(b, p, u)
                if now == WHEN["max_parts"]:
                    attn_max(b, p)
                tail(b, p, now)
                front(b, p, now)

            run_periods(dve, step)

            R = RT

            def step(ins, name):
                ins.then_inc(R.sem, 1)
                dve.wait_ge(R.sem, R.at(0, name))

            dve.wait_ge(C.sem, C.at(NB - 1, "POS"))
            step(dve.tensor_scalar(padf[:, :], carry[:, :], cst[:, C_ROW:C_ROW + 1], None, ALU.add), "padf")
            dve.tensor_copy(padi[:, :], padf[:, :]).then_inc(s_idx, 1)
            step(dve.tensor_tensor(cnt[:, :], carry[:, :], cst[:, C_OFF:C_OFF + NE], ALU.subtract), "cnt")
            step(dve.tensor_scalar(cnt[:, :], cnt[:, :], P / 2 - 0.5, 1.0 / P, ALU.add, ALU.mult), "cnt2")
            step(dve.tensor_copy(cnti[:, :], cnt[:, :]), "cnti")
            step(dve.tensor_copy(cnt[:, :], cnti[:, :]), "nt")
            step(dve.tensor_tensor_scan(cum[:, :], ones_f[:, :], cnt[:, :], 0.0, ALU.mult, ALU.add), "cum")
            tiles = cst[0:1, C_TILE:C_TILE + NT]
            step(dve.tensor_tensor(past[:, :, :], bc(tiles, 2, NE), bc(cum[0:1, :], 1, NT), ALU.is_ge), "past")
            step(dve.tensor_reduce(eidx[:, :], past[:, :, :], op=ALU.add, axis=AX_X), "eidx")
            step(dve.tensor_tensor(past[:, :, :], past[:, :, :], bc(cnt[0:1, :], 1, NT), ALU.mult), "pastn")
            step(dve.tensor_reduce(first[:, :], past[:, :, :], op=ALU.add, axis=AX_X), "first")
            step(dve.tensor_tensor(first[:, :], tiles, first[:, :], ALU.subtract), "inside")
            step(dve.tensor_scalar(valid[:, :], eidx[:, :], NE - 0.5, None, ALU.is_lt), "valid")
            step(dve.scalar_tensor_tensor(out=first[:, :], in0=first[:, :], scalar=float(P), in1=valid[:, :],
                                          op0=ALU.mult, op1=ALU.mult), "jrow")
            step(dve.tensor_scalar(valid[:, :], valid[:, :], -1.0, 1.0, ALU.mult, ALU.add), "spare")
            step(dve.tensor_tensor(valid[:, :], valid[:, :], cst[0:1, C_DUMMY:C_DUMMY + NT], ALU.mult), "dummy")
            step(dve.tensor_tensor(first[:, :], first[:, :], valid[:, :], ALU.add), "sum")
            step(dve.scalar_tensor_tensor(out=first[:, :], in0=eidx[:, :], scalar=float(REG), in1=first[:, :],
                                          op0=ALU.mult, op1=ALU.add), "row")
            step(dve.tensor_scalar(eidx[:, :], eidx[:, :], NE - 1.0, float(EW), ALU.min, ALU.mult), "col")
            dve.tensor_copy(tab[:, 0, :], first[:, :]).then_inc(s_tab, 1)
            dve.tensor_copy(tab[:, 1, :], eidx[:, :]).then_inc(s_tab, 1)
            step(dve.tensor_tensor(delta[:, :], cum[:, :], cnt[:, :], ALU.subtract), "tab")
            step(dve.tensor_scalar(delta[:, :], delta[:, :], float(P), None, ALU.mult), "startt")
            step(dve.tensor_tensor(delta[:, :], delta[:, :], cst[:, C_OFF:C_OFF + NE], ALU.subtract), "delta")
            dve.tensor_copy(shift[:, 0:1], delta[:, 0:1])
            step(dve.tensor_tensor(shift[:, 1:NE], delta[:, 1:NE], delta[:, 0:NE - 1], ALU.subtract), "shift")
            step(dve.tensor_tensor(above[:, :, :], bc(POS[:, :], 2, NE), bc(cst[:, C_OFF:C_OFF + NE], 1, TT * 2),
                                   ALU.is_ge), "above")
            step(dve.tensor_tensor(above[:, :, :], above[:, :, :], bc(shift[:, :], 1, TT * 2), ALU.mult), "moves")
            step(dve.tensor_reduce(moved[:, :], above[:, :, :], op=ALU.add, axis=AX_X), "moved")
            step(dve.tensor_tensor(moved[:, :], moved[:, :], POS[:, :], ALU.add), "pos")
            step(dve.tensor_copy(GIDX[:, :], moved[:, :]), "GIDX")

            def tile(T, u, xt=True, gu=True, tr=True, dn=True):
                p = u % 2
                if gu:
                    dve.wait_ge(moe["act_sg"], T + 1)
                    if old(T, 2):
                        dve.wait_ge(moe["pe_tr"], T - 2 + 1)
                    dve.tensor_tensor(hm[:, p, :], PS[p][:, 0:HID], sg[:, p, :], ALU.mult).then_inc(moe["dve_hm"], 1)
                if tr:
                    dve.wait_ge(moe["pe_tr"], T - 1 + 1)
                    if old(T, 3):
                        dve.wait_ge(moe["pe_dn"], T - 2)
                    dve.tensor_copy(hmT[:, 1 - p, :], PF[1 - p][:, 0:HID]).then_inc(moe["dve_hT"], 1)
                if dn:
                    dve.wait_ge(moe["pe_dn"], T - 2 + 1)
                    if old(T, 4):
                        dve.wait_ge(s_st[p], 8 * (T - 4 - p) + 16)
                    dve.tensor_copy(eo[:, p, :], PO[1][:, 0:P]).then_inc(moe["dve_eo"], 1)

            run_tiles(dve, tile)

            L = LA

            def last_index(b, p):
                dve.tensor_copy(wl[:, p, :], WGT[:, bass.ds(b * 4, 4)])
                dve.tensor_copy(gidx[:, p, :], GIDX[:, bass.ds(b * 4, 4)]).then_inc(LI.sem, 1)

            def last(b, p, more=True):
                def step(ins, name):
                    ins.then_inc(L.sem, 1)
                    dve.wait_ge(L.sem, L.at(b, name))

                dve.wait_ge(s_got[p], 32 * (b - p) + 64)
                if old(b, 2):
                    dve.wait_ge(s_out[p], 8 * (b - p))
                for i in range(QB):
                    r = dve.tensor_scalar(res[:, p, i, :], got[:, p, i, 0, :], wl[:, p, 2 * i:2 * i + 1], None, ALU.mult)
                step(r, "a")
                for i in range(QB):
                    r = dve.scalar_tensor_tensor(out=res[:, p, i, :], in0=got[:, p, i, 1, :],
                                                 scalar=wl[:, p, 2 * i + 1:2 * i + 2], in1=res[:, p, i, :],
                                                 op0=ALU.mult, op1=ALU.add)
                step(r, "b")
                if more:
                    last_index(b + 2, p)
                dve.wait_ge(s_gb[p], 8 * (b - p) + 16)
                step(dve.tensor_tensor(res[:, p, :, :], res[:, p, :, :], bc(GB[:, p, :], 1, QB), ALU.mult), "g")
                dve.tensor_tensor(res[:, p, :, :], res[:, p, :, :], base[:, bass.ds(b * QB, QB), :], ALU.add).then_inc(L.sem, 1)

            last_index(0, 0)
            last_index(1, 1)
            last(0, 0)
            last(1, 1)
            with dve.Fori(1, NB // 2 - 1) as j:
                last(2 * j, 0)
                last(2 * j + 1, 1)
            last(NB - 2, 0, more=False)
            last(NB - 1, 1, more=False)

        @block.tensor
        def _(pe):
            mm = nc.tensor.matmul
            transpose = nc.tensor.transpose
            pe.wait_ge(s_cst, 16)
            pe.wait_ge(s_w, 16 * N_W)
            transpose(PF[0][:, 0:P], w_in[:, 0, :], ident)
            transpose(PF[0][:, P:2 * P], w_in[:, 1, :], ident).then_inc(SU["pe"].sem, 1)
            pe.wait_ge(SU["dve"].sem, SU["dve"].at(0, "silu"))
            for i in range(2):
                r = mm(PF[1][:, i * NB:(i + 1) * NB], wmod_s[:, i * P:(i + 1) * P], silu_T[:, :], start=True, stop=True)
            r.then_inc(SU["pe"].sem, 1)
            for i in range(2):
                r = mm(PA[i][0:NB, 0:3 * P], silu_T[:, :], wmod_s[:, i * 3 * P:(i + 1) * 3 * P], start=True, stop=True)
            r.then_inc(SU["pe"].sem, 1)
            pe.wait_ge(SU["dve"].sem, SU["dve"].at(0, "carry"))
            pe.wait_ge(SU["pool"].sem, 2)
            A, B, C = FR["pe"], AT["pe"], TL["pe"]

            def front(b, p, now):
                if now == WHEN["T1"]:
                    pe.wait_ge(FR["dve"].sem, FR["dve"].at(b, "n1"))
                    if old(b, 1):
                        pe.wait_ge(FR["act"].sem, FR["act"].at(b - 1, "va"))
                    for i in range(QB):
                        r = transpose(PF[0][:, i * P:(i + 1) * P], nrm[:, i, :], ident)
                    r.then_inc(A.sem, 1)
                if now == WHEN["bx_mm"]:
                    pe.wait_ge(FR["act"].sem, FR["act"].at(b, "hT"))
                    if old(b, 1):
                        pe.wait_ge(FR["dve"].sem, FR["dve"].at(b - 1, "rs"))
                    mm(PF[1][:, 0:S], bwT[:, :], hT[:, :], start=True, stop=True).then_inc(A.sem, 1)
                if now == WHEN["y"]:
                    pe.wait_ge(FR["dve"].sem, FR["dve"].at(b, "scan"))
                    for i in range(QB):
                        r = mm(PF[0][:, i * P:(i + 1) * P], hs[:, i * P:(i + 1) * P], cwT[:, :], start=True, stop=True)
                    r.then_inc(A.sem, 1)
                if now == WHEN["T3"]:
                    pe.wait_ge(FR["dve"].sem, FR["dve"].at(b, "xn"))
                    for i in range(QB):
                        r = transpose(PF[1][:, i * P:(i + 1) * P], nrm[:, i, :], ident)
                    r.then_inc(A.sem, 1)
                if now == WHEN["qk"]:
                    pe.wait_ge(FR["act"].sem, FR["act"].at(b, "xnT"))
                    for i in range(2):
                        mm(PF[0][:, i * S:(i + 1) * S], wqkv[:, i, :], xnT[:, :], start=True, stop=True)
                        r = mm(PF[1][:, i * S:(i + 1) * S], w_rot[:, i, :], xnT[:, :], start=True, stop=True)
                    r.then_inc(A.sem, 1)

            def values(b, p):
                pe.wait_ge(FR["dve"].sem, FR["dve"].at(b, "rc"))
                for i in range(QB):
                    r = mm(PF[0][:, i * P:(i + 1) * P], xnT[:, i * P:(i + 1) * P], wqkv[:, 2, :], start=True, stop=True)
                r.then_inc(A.sem, 1)

            def attn_unit(a, p, u):
                g, k = divmod(u, 3)
                if u == 0:
                    pe.wait_ge(s_stk[p][0], 24 * (a - p) + 48)
                    if old(a, 1):
                        pe.wait_ge(MA["act"].sem, MA["act"].at(a - 1, "nmT"))
                if u == 6:
                    pe.wait_ge(s_stk[p][1], 24 * (a - p) + 48)
                if u == 1 and old(a, LEAD + 1):
                    pe.wait_ge(TL["dve"].sem, TL["dve"].at(a - LEAD - 1, "carry"))
                if u >= 2:
                    pe.wait_ge(MA["dve"].sem, MA["dve"].at(a, f"m{u - 2}"))
                elif old(a, 1):
                    pe.wait_ge(MA["dve"].sem, MA["dve"].at(a - 1, f"m{10 + u}"))
                bank = PA[u % 2]
                if k == 0:
                    heads, n = range(4 * g, 4 * g + 4), P
                else:
                    heads, n = range(4 * g + 2 * (k - 1), 4 * g + 2 * k), S
                q0 = 0 if k == 0 else P
                for i, h in enumerate(heads):
                    mm(bank[:, i * n:(i + 1) * n], QST[:, p, h // 2, q0:q0 + P], KST[:, p, h, 0:n],
                       start=(i == 0), stop=False, skip_group_check=True)
                diag = bank[:, :].rearrange("p (h k) -> p h k", k=n)[:, :, n - P:n]
                mm(diag, ident_b[:, :], mask_b[:, 0:len(heads), :], start=False, stop=True,
                   skip_group_check=True).then_inc(MA["pe"].sem, 1)

            def attn_max(a, p):
                pe.wait_ge(MA["dve"].sem, MA["dve"].at(a, "nl"))
                for i in range(QB):
                    r = transpose(PA_b[:, i * P:(i + 1) * P], nmp[:, i, :, :].rearrange("p x h -> p (x h)"), ident_b[:, :])
                r.then_inc(MA["pe"].sem, 1)

            def attn_scores(a, p, h):
                if h == 0:
                    pe.wait_ge(s_nm, 96 * a + 96)
                if h >= 2:
                    pe.wait_ge(AT["act"].sem, AT["act"].at(a, f"e{h - 2}"))
                elif old(a, 1):
                    pe.wait_ge(AT["act"].sem, AT["act"].at(a - 1, f"e{H - 2 + h}"))
                bank = PS[h % 2]
                mm(bank[:, 0:S], KST[:, p, h, 0:P], QST[:, p, h // 2, :], start=True, stop=True)
                mm(bank[:, S:S + P], KST[:, p, h, P:S], QST[:, p, h // 2, P:S], start=True, stop=True).then_inc(B.sem, 1)

            def attn_pv(a, p, h):
                pe.wait_ge(AT["pool"].sem, AT["pool"].at(a, f"c{h}"))
                if h == 0 and old(a, 1):
                    pe.wait_ge(TL["dve"].sem, TL["dve"].at(a - 1, "h3"))
                g, j = divmod(h, 4)
                o = PO[g // 2][32 * j:32 * j + 32, (g % 2) * S:(g % 2) * S + S]
                mm(o, VA[:, p, 0, h, :], PT[:, h % 4, 0:S], start=True, stop=False)
                mm(o[:, P:S], VA[:, p, 1, h, :], PT[:, h % 4, S:3 * P], start=False, stop=True).then_inc(B.sem, 1)

            def tail(t, p, now):
                if now == WHEN["oT"]:
                    pe.wait_ge(TL["act"].sem, TL["act"].at(t, "OT"))
                    for i in range(QB):
                        for g in range(4):
                            r = transpose(PO[i][:, g * P:(g + 1) * P], OT[:, g, i * P:(i + 1) * P], ident)
                    r.then_inc(C.sem, 1)
                if now == WHEN["T_on"]:
                    pe.wait_ge(TL["dve"].sem, TL["dve"].at(t, "on"))
                    for i in range(QB):
                        r = transpose(PO[0][:, i * P:(i + 1) * P], ON[:, i, :], ident)
                    r.then_inc(C.sem, 1)
                if now == WHEN["wo"]:
                    pe.wait_ge(TL["act"].sem, TL["act"].at(t, "onT"))
                    for i in range(QB):
                        r = mm(PO[1][:, i * P:(i + 1) * P], ONT[:, i * P:(i + 1) * P], wo_s[:, :], start=True, stop=True)
                    r.then_inc(C.sem, 1)
                if now == WHEN["T_x2"]:
                    pe.wait_ge(TL["dve"].sem, TL["dve"].at(t, "xn"))
                    if not isinstance(t, int) or t + LEAD < NB:
                        pe.wait_ge(MA["dve"].sem, MA["dve"].at(t + LEAD, "m11"))
                    for i in range(QB):
                        r = transpose(PA[1][:, i * P:(i + 1) * P], xn2[:, p, i, :], ident)
                    r.then_inc(C.sem, 1)
                if now == WHEN["logits"]:
                    pe.wait_ge(TL["act"].sem, TL["act"].at(t, "xT"))
                    for i in range(QB):
                        r = mm(PA[1][:, i * NE:(i + 1) * NE], xn2T[:, i * P:(i + 1) * P], wr_s[:, :], start=True, stop=True)
                    r.then_inc(C.sem, 1)
                if now == WHEN["rank"]:
                    pe.wait_ge(TL["dve"].sem, TL["dve"].at(t, "ohs"))
                    for i, (o, terms) in enumerate((
                            (0, ((upper_b, 0),)), (1, ((ones_b, 0), (upper_b, 1))), (2, ((ones_b, 0), (ones_b, 1))))):
                        for k, (w, blk) in enumerate(terms):
                            r = mm(PA[1][:, o * NE:(o + 1) * NE], w[:, :], ohs[:, blk, :], start=(k == 0),
                                   stop=(k == len(terms) - 1))
                    r.then_inc(C.sem, 1)

            def step(b, p, now):
                if now == WHEN["v"]:
                    values(b, p)
                for u in units_at(now):
                    attn_unit(b, p, u)
                if now == WHEN["max_T"]:
                    attn_max(b, p)
                for h in heads_at(now):
                    attn_scores(b, p, h)
                for h in heads_at(now - PV_LATER):
                    attn_pv(b, p, h)
                tail(b, p, now)
                front(b, p, now)

            run_periods(pe, step)
            pe.wait_ge(s_tab, 3)
            pe.wait_ge(s_exp, 16 * (2 + NE))
            def tile(T, u, xt=True, gu=True, tr=True, dn=True):
                p = u % 2
                if gu:
                    col = pe.value_load(tab[0:1, 1, bass.ds(T, 1)], min_val=0, max_val=(NE - 1) * EW)
                if xt:
                    v = (u + 1) % 4
                    pe.wait_ge(s_in[v], 4 * (T + 1 - v) + 16)
                    if old(T, 0):
                        pe.wait_ge(moe["act_xT"], T + 1)
                    transpose(PO[0][:, 0:P], xin[:, v, :], ident).then_inc(moe["pe_xT"], 1)
                if gu:
                    pe.wait_ge(moe["act_xT"], T + 1)
                    if old(T, 2):
                        pe.wait_ge(moe["dve_hm"], T - 2 + 1)
                    mm(PA[p][:, 0:HID], xT[:, p, :], experts[:, bass.ds(col, HID)], start=True, stop=True)
                    mm(PS[p][:, 0:HID], xT[:, p, :], experts[:, bass.ds(col + HID, HID)], start=True, stop=True).then_inc(moe["pe_gu"], 1)
                if tr:
                    pe.wait_ge(moe["dve_hm"], T - 1 + 1)
                    if old(T, 3):
                        pe.wait_ge(moe["dve_hT"], T - 2)
                    for c_ in range(HC):
                        r = transpose(PF[1 - p][:, c_ * P:(c_ + 1) * P], hm[:, 1 - p, c_ * P:(c_ + 1) * P], ident)
                    r.then_inc(moe["pe_tr"], 1)
                if dn:
                    pcol = pe.value_load(tab[0:1, 1, bass.ds(T - 2, 1)], min_val=0, max_val=(NE - 1) * EW)
                    pe.wait_ge(moe["dve_hT"], T - 2 + 1)
                    if old(T, 3):
                        pe.wait_ge(moe["dve_eo"], T - 3 + 1)
                    for c_ in range(HC):
                        r = mm(PO[1][:, 0:P], hmT[:, p, c_ * P:(c_ + 1) * P],
                               experts[:, bass.ds(pcol + 2 * HID + c_ * P, P)], start=(c_ == 0), stop=(c_ == HC - 1))
                    r.then_inc(moe["pe_dn"], 1)

            run_tiles(pe, tile)


_INS = ['L0_attn_x', 'L0_attn_log_A', 'L0_attn_B_w', 'L0_attn_B_b', 'L0_attn_C_w', 'L0_attn_C_b', 'L0_ffn_wq',
        'L0_ffn_wk', 'L0_ffn_wv', 'L0_ffn_wo', 'L0_ffn_w_router', 'L0_ffn_wg', 'L0_ffn_wu', 'L0_ffn_wd',
        'L0_ffn_g1', 'L0_ffn_g2', 'L0_c', 'L0_wmod']


def kernel(**inputs):
    import concourse.bacc as _bacc
    from concourse.bass_utils import run_bass_kernel_spmd as _run

    nc = _bacc.Bacc("TRN2", target_bir_lowering=False, num_devices=1)
    arrays, args = {}, []
    for name in _INS:
        a = np.ascontiguousarray(inputs[name])
        arrays[name + "_dram"] = a
        args.append(nc.dram_tensor(name + "_dram", a.shape, mybir.dt.from_np(a.dtype), kind="ExternalInput").ap())
    arrays["consts_dram"] = constants()
    args.append(nc.dram_tensor("consts_dram", [P, C_N], F32, kind="ExternalInput").ap())
    args.append(nc.dram_tensor("out_dram", [NB, S, P], F32, kind="ExternalOutput").ap())
    build(nc, *args)
    r = _run(nc, [arrays], core_ids=[0])
    return r.results[0]["out_dram"]
```

```python
from contextlib import ExitStack

import numpy as np

import concourse.bass as bass
from concourse import mybir

F32 = mybir.dt.float32
BF16 = mybir.dt.bfloat16
I32 = mybir.dt.int32
U32 = mybir.dt.uint32
ALU = mybir.AluOpType
ACT = mybir.ActivationFunctionType
AX_X = mybir.AxisListType.X

P = 128
NB = 16
S = 256
QB = S // P
TT = NB * QB
H = 16
DH = P // H
NE = 8
HID = 384
HC = HID // P
EW = 2 * HID + HC * P
DST, WT, RW = P, P + 1, P + 2
REG = NB * S + P
NT = 2 * NB * S // P + NE - 1
NROW = NE * REG + NE * P
LN_EPS, RMS_EPS = 1e-5, 1e-6
SCALE = float(DH) ** -0.5
ROWS = 64
Q_SLOTS = ((0, 2, 1, 3), (1, 0, 5, 2), (2, 1, 1, 1))
K_SLOTS = ((0, 0, 1, 3), (1, 3, 2, 2), (2, 4, 1, 1))
AUG = 6
NEG = -1.0e30
N_W = 11

SLOTS = 22
WHEN = dict(
    load=0, stats=12, rstd1=15, norm1=16, T1=17, h=18, bx_mm=19, bx=20, scan=22, y=22, xg=21, x1=22, rstd2=24,
    keep=24, norm2=24, h2=25, squares=27, mean3=27, rstd3=28, norm3=29, T3=31, xT=32, qk=34, rope=34, part0=35,
    rest1=36, part1=37, part2=41, stack=41, v=36, v_heads=51, unit0=45, max_parts=56, max_T=57, max_rows=58,
    load_gate=45, head0=61, o_copy=70, oT=72, divide=72, T_on=74, onT=74, wo=76, h3=76, base=76, squares2=77,
    mean4=78, rstd4=79, x2=80, T_x2=81, x2T=81, logits=83, top2=85, exp_d=86, weights=87, rank=86, rows=88,
    scatters=(91, 93, 93, 95))
UNITS_PER_SLOT, HEADS_PER_SLOT, PV_LATER = 1, 2, 1
BATCH_SLOTS = max(WHEN["scatters"]) + 1
LAGS = -(-BATCH_SLOTS // SLOTS)


def units_at(now):
    u = (now - WHEN["unit0"]) * UNITS_PER_SLOT
    return [v for v in range(u, u + UNITS_PER_SLOT) if 0 <= v < 12]


def heads_at(now):
    h = (now - WHEN["head0"]) * HEADS_PER_SLOT
    return [v for v in range(h, h + HEADS_PER_SLOT) if 0 <= v < H]


C_ID, C_COS, C_SIN, C_UP, C_MASK, C_IOTA, C_OFF = 0, 128, 384, 640, 768, 896, 904
C_TILE, C_KAUG, C_JUNK, C_DST, C_N = 912, 984, 985, 1001, 1001 + 2 * TT
M_GA, M_CBGA, M_CB1, M_SB, M_GB = range(5)


def constants():
    c = np.zeros((P, C_N), np.float32)
    c[:, C_ID:C_ID + P] = np.eye(P)
    inv = 1.0 / 10000.0 ** (np.arange(0, DH, 2, dtype=np.float32) / DH)
    f = np.einsum('i,j->ij', np.arange(S, dtype=np.float32), inv)
    emb = np.concatenate([f, f], axis=-1)
    c[:, C_COS:C_COS + S] = np.tile(np.cos(emb).T, (H, 1))
    c[:, C_SIN:C_SIN + S] = np.tile(np.sin(emb).T, (H, 1))
    c[:, C_UP:C_UP + P] = np.triu(np.ones((P, P)), 1)
    c[:, C_MASK:C_MASK + P] = np.triu(np.full((P, P), NEG), 1)
    c[:, C_IOTA:C_IOTA + NE] = np.arange(NE)
    c[:, C_OFF:C_OFF + NE] = np.arange(NE) * REG
    c[:, C_TILE:C_TILE + NT] = np.arange(NT)
    c[:, C_KAUG] = np.arange(P) % DH < 3
    token = np.arange(TT)[None, :, None] * P + np.arange(P)[:, None, None]
    c[:, C_DST:C_DST + 2 * TT] = (2 * token + np.arange(2)).reshape(P, 2 * TT)
    c[:, C_JUNK:C_JUNK + 2 * NE] = 2 * TT * P + np.arange(2 * NE) * P + np.arange(P)[:, None]
    return c


class Steps:

    def __init__(self, sem, names, first=0):
        self.sem, self.names, self.first = sem, names.split(), first

    def at(self, b, name):
        return b * len(self.names) + (self.names.index(name) + 1 + self.first)


def build(nc, x, log_A, B_w, B_b, C_w, C_b, wq, wk, wv, wo, w_router, wg, wu, wd, g1, g2, c, wmod, consts, out):
    ctx = ExitStack()
    with ctx:
        def sb(name, shape, dt=F32):
            return ctx.enter_context(nc.sbuf_tensor(name, shape, dt))

        def sem(name):
            return ctx.enter_context(nc.semaphore(name))

        mod_rows = nc.dram_tensor("mod_rows", [NB, 5 * P], F32).ap()
        q_stack_d = nc.dram_tensor("q_stack_d", [2, H, ROWS, S], BF16).ap()
        k_stack_d = nc.dram_tensor("k_stack_d", [2, H, ROWS, S], BF16).ap()
        routed = nc.dram_tensor("routed", [NROW, RW], F32).ap()
        expert_out = nc.dram_tensor("expert_out", [2 * TT * P + 2 * NE * P, P], F32).ap()

        cst = sb("cst", [P, C_N])
        ident = cst[:, C_ID:C_ID + P]
        ident_b = sb("ident_b", [P, P], BF16)
        upper_b = sb("upper_b", [P, P], BF16)
        ones_b = sb("ones_b", [P, P], BF16)
        mask_b = sb("mask_b", [P, 4, P], BF16)
        pad_rows = sb("pad_rows", [P, 2 * NE, RW])
        pad_rows_i = pad_rows[:, :, :].bitcast(I32)
        kaug_b = sb("kaug_b", [P, 2 * S], BF16)
        neg_half = sb("neg_half", [P, 2])
        w_in = sb("w_in", [P, 2, P])
        bwT = sb("bwT", [P, P])
        cwT = sb("cwT", [P, P])
        cols = sb("cols", [P, 4])
        decay = sb("decay", [P, 1])
        decay_b = sb("decay_b", [P, S])
        wqkv = sb("wqkv", [P, 3, P])
        w_rot = sb("w_rot", [P, 2, P])
        wo_s = sb("wo_s", [P, P])
        wr_s = sb("wr_s", [P, NE])
        g2_b = sb("g2_b", [P, P])
        experts = sb("experts", [P, NE * EW])
        c_T = sb("c_T", [P, NB])
        c_e = sb("c_e", [P, NB])
        silu_T = sb("silu_T", [P, NB])
        wmod_s = sb("wmod_s", [P, 6 * P])
        mod_T = sb("mod_T", [P, 2, NB])
        mod_r = sb("mod_r", [NB, 4 * P])
        row_s = sb("row_s", [NB, 5 * P])
        cb_r = sb("cb_r", [NB, P])
        sgn = sb("sgn", [NB, 2, P])

        X = sb("X", [P, 2, QB, P])
        MB = sb("MB", [P, 2, 4 * P])
        GB = sb("GB", [P, 2, P])
        st = sb("st", [P, QB, 6])
        mv = sb("mv", [P, QB, 2])
        rs = sb("rs", [P, QB])
        nrm = sb("nrm", [P, QB, P])
        hT = sb("hT", [P, S])
        bx = sb("bx", [P, S])
        hs = sb("hs", [P, S])
        xg = sb("xg", [P, QB, P])
        tmp = sb("tmp", [P, QB, P])
        x1 = sb("x1", [P, QB, P])
        H2 = sb("H2", [P, TT, P])
        sq = sb("sq", [P, QB, P])
        modc = sb("modc", [P, 2, 2])
        ve = sb("ve", [P, QB])
        ve2 = sb("ve2", [P, QB])
        tiny = sb("tiny", [P, 1])
        warm = sb("warm", [P, 1])
        qaug_b = sb("qaug_b", [P, 2 * S], BF16)
        ones_f = sb("ones_f", [P, NE])
        ss = sb("ss", [P, QB])
        xnT = sb("xnT", [P, S])
        r_c = sb("r_c", [P, 2, S])
        r_s = sb("r_s", [P, 2, S])
        qk = sb("qk", [P, 2, S])
        part = sb("part", [P, 3, 2, S], BF16)
        QST = sb("QST", [P, 2, H // 2, S], BF16)
        KST = sb("KST", [P, 2, H, S], BF16)
        vs = sb("vs", [P, QB, P])
        VA = sb("VA", [P, 2, QB, H, 32])

        MX = sb("MX", [P, QB, H])
        rem = sb("rem", [P, QB, H])
        nmp = sb("nmp", [P, QB, 8, H], BF16)
        nmT = sb("nmT", [3 * H, S], BF16)
        PT = sb("PT", [P, 4, 3 * P])
        OT = sb("OT", [P, 4, S])
        rc = sb("rc", [P, QB, H])
        ON = sb("ON", [P, QB, P])
        ONT = sb("ONT", [P, S])
        h3 = sb("h3", [P, QB, P])
        gh = sb("gh", [P, QB, P])
        base = sb("base", [P, TT, P])
        sq2 = sb("sq2", [P, QB, P])
        ss2 = sb("ss2", [P, QB])
        rs2 = sb("rs2", [P, QB])
        xn2 = sb("xn2", [P, 2, QB, 2, RW])
        xn2_i = xn2[:, :, :, :, :].bitcast(I32)
        xn2T = sb("xn2T", [P, S])
        lg = sb("lg", [P, QB, NE])
        mx8 = sb("mx8", [P, QB, 8])
        ix8 = sb("ix8", [P, QB, 8], U32)
        ixf = sb("ixf", [P, QB, 2])
        dl = sb("dl", [P, QB])
        el = sb("el", [P, QB])
        e1 = sb("e1", [P, QB])
        w12 = sb("w12", [P, QB, 2])
        oh = sb("oh", [P, QB, 2, NE])
        ohs = sb("ohs", [P, QB, NE], BF16)
        carry = sb("carry", [P, NE])
        pall = sb("pall", [P, QB, NE])
        prod = sb("prod", [P, QB, 2, NE])
        posf = sb("posf", [P, QB, 2])
        posi = sb("posi", [P, 2, QB * 2], I32)

        endi = sb("endi", [P, NE], I32)
        cnt = sb("cnt", [P, NE])
        cnti = sb("cnti", [P, NE], I32)
        cum = sb("cum", [P, NE])
        past = sb("past", [1, NT, NE])
        eidx = sb("eidx", [1, NT])
        first = sb("first", [1, NT])
        tab = sb("tab", [1, 2, NT], I32)
        xin = sb("xin", [P, 4, RW])
        xin_i = xin[:, :, :].bitcast(I32)
        xT = sb("xT", [P, 2, P])
        sg = sb("sg", [P, 2, HID])
        hm = sb("hm", [P, 2, HID])
        hmT = sb("hmT", [P, 2, HID])
        eo = sb("eo", [P, 4, P])
        dest = sb("dest", [P, 4], I32)
        in_dest = sb("in_dest", [P, 4], I32)
        in_w = sb("in_w", [P, 4])
        gates = H2[:, TT - NB:, :]
        got = H2[:, 0:4 * QB * 2, :].rearrange("p (q t k) d -> p q t k d", q=4, t=QB)
        res = sb("res", [P, 2, QB, P])

        banks = [ctx.enter_context(nc.psum_tensor(f"bank{i}", [P, 512], F32)) for i in range(8)]
        PF = banks[0:2]
        PA = banks[2:4]
        PS = banks[4:6]
        PO = banks[6:8]

        s_cst = sem("s_cst")
        s_mod = sem("s_mod")
        s_w = sem("s_w")
        s_exp = sem("s_exp")
        s_scr = sem("s_scr")
        s_modrow = sem("s_modrow")
        s_x = [sem("s_x0"), sem("s_x1")]
        s_mb = [sem("s_mb0"), sem("s_mb1")]
        s_gt = [sem("s_gt0"), sem("s_gt1")]
        s_stw = sem("s_stw")
        s_stk = [[sem(f"s_stk{p}_{half}") for half in range(2)] for p in range(2)]
        s_nm = sem("s_nm")
        s_sc = [sem("s_sc0"), sem("s_sc1")]
        SU = {e: Steps(sem("setup_" + e), n) for e, n in dict(
            pe="modT modr bwcw", act="exp_c exp_a", pool="pads kst ones",
            dve="aug ec rc silu modT modr sgn2 sgn abs guard castb wT rot ea decay decb carry").items()}
        FR = {e: Steps(sem("front_" + e), n) for e, n in dict(
            pe="nT bx y", act="hT bx keep", pool="rs1 xg rs2",
            dve="st mv ve n1 scan ty x1 st2 mv2 ve2 n2 h2a h2").items()}
        QK = {e: Steps(sem("qk_" + e), n) for e, n in dict(
            pe="xnT qk", act="ss xnT ph pm", pool="rs3", dve="vs xn rc rs qk r1 pl").items()}
        VS = {e: Steps(sem("values_" + e), n) for e, n in dict(pe="v", act="v heads").items()}
        MA = {e: Steps(sem("max_" + e), n) for e, n in dict(
            pe=" ".join([f"a{i}" for i in range(12)] + ["nmT"]), act="nmT",
            dve=" ".join(f"m{i}" for i in range(12)) + " nh rem nm rem2 nl").items()}
        AT = {e: Steps(sem("attn_" + e), n) for e, n in dict(
            pe=" ".join(f"{kind}{h}" for now in range(BATCH_SLOTS) for kind, when in (("s", now), ("pv", now - PV_LATER))
                        for h in heads_at(when)),
            act=" ".join(f"e{h}" for h in range(H)),
            pool=" ".join(f"c{h}" for h in range(H))).items()}
        TL = {e: Steps(sem("tail_" + e), n) for e, n in dict(
            pe="oT onT wo xT lg rank",
            act="OT onT ss xT twin el",
            pool="gh base rs",
            dve="rc on h3 vs xn lg mx ix ixf oh ohs dl e1 w1 w2 pall carry prod posf posi").items()}
        moe = {n: sem("moe_" + n) for n in "pe_xT pe_gu pe_tr pe_dn act_xT act_sg dve_in dve_hm dve_hT dve_eo".split()}
        RT = Steps(sem("tables"), "cnt cnt2 cnti nt cum past eidx pastn first inside jrow row col tab")
        LA = Steps(sem("last"), "sum g out")
        s_rows = sem("s_rows")
        s_tab = sem("s_tab")
        s_idx = sem("s_idx")
        s_pad = sem("s_pad")
        s_in = [sem(f"s_in{i}") for i in range(4)]
        s_st = [sem(f"s_st{i}") for i in range(4)]
        s_got = [sem(f"s_got{i}") for i in range(4)]
        s_gb = sem("s_gb")
        s_out = [sem("s_out0"), sem("s_out1")]
        PA_b = PA[0][:, :].bitcast(BF16)

        def run_periods(eng, step):
            def period(k, pf):
                for slot in range(SLOTS):
                    for n in reversed(range(LAGS)):
                        if not isinstance(k, int) or 0 <= k - n < NB:
                            step(k - n, (pf + n) % 2, slot + n * SLOTS)

            first = -(-(LAGS + 2) // 2)
            for k in range(2 * first):
                period(k, k % 2)
            with eng.Fori(first, NB // 2) as j:
                period(2 * j, 0)
                period(2 * j + 1, 1)
            for k in range(NB, NB + LAGS - 1):
                period(k, k % 2)

        LEAD = (WHEN["T_x2"] - WHEN["max_parts"] - 1) // SLOTS

        def run_tiles(eng, tile):
            tile(-1, 3, gu=False, tr=False, dn=False)
            tile(0, 0, tr=False, dn=False)
            tile(1, 1, dn=False)
            for T in range(2, 8):
                tile(T, T % 4)
            with eng.Fori(2, NT // 4) as j:
                for u in range(4):
                    tile(4 * j + u, u)
            for T in range(NT // 4 * 4, NT - 1):
                tile(T, T % 4)
            tile(NT - 1, (NT - 1) % 4, xt=False)
            tile(NT, NT % 4, xt=False, gu=False)
            tile(NT + 1, (NT + 1) % 4, xt=False, gu=False, tr=False)

        def bc(ap, axis, n):
            a = ap.unsqueeze(axis)
            shape = list(a.shape)
            shape[axis] = n
            return a.to_broadcast(shape)

        def old(b, k):
            return not isinstance(b, int) or b >= k

        passed = {}

        def alone(eng):
            if id(eng) not in passed:
                passed[id(eng)] = sem(f"passed{len(passed)}")
            eng.sem_inc(passed[id(eng)], 1)

        def pad_experts(eng, which):
            for e in which:
                row = eng.value_load(endi[0:1, e:e + 1], min_val=0, max_val=NE * REG - P)
                eng.dma_start(routed[bass.ds(row, P), :], pad_rows[:, e, :]).then_inc(s_pad, 16)

        block = ctx.enter_context(nc.Block())

        @block.sync
        def _(sp):
            def load_x(b, p):
                sp.dma_start(X[:, p, :, :], x[bass.ds(b, 1), :, :].rearrange("a (t p) d -> p (a t) d", p=P)).then_inc(s_x[p], 16)

            def front_load(b, p):
                if old(b, 2):
                    sp.wait_ge(FR["dve"].sem, FR["dve"].at(b - 2, "st"))
                    alone(sp)
                    sp.wait_ge(FR["pool"].sem, FR["pool"].at(b - 2, "xg"))
                    alone(sp)
                    sp.wait_ge(FR["dve"].sem, FR["dve"].at(b - 2, "n1"))
                    alone(sp)
                    load_x(b, p)
                    sp.wait_ge(FR["dve"].sem, FR["dve"].at(b - 2, "h2"))
                    alone(sp)
                elif b == 0:
                    sp.wait_ge(s_modrow, 16)
                sp.dma_start(MB[:, p, :], mod_rows[bass.ds(b, 1), 0:4 * P].to_broadcast([P, 4 * P])).then_inc(s_mb[p], 16)

            sp.dma_start(cst[:, :], consts).then_inc(s_cst, 16)
            sp.dma_start(wmod_s[:, :], wmod).then_inc(s_mod, 16)
            sp.dma_start(cb_r[:, :], C_b.partition_broadcast(NB)).then_inc(s_mod, 16)
            with nc.allow_non_contiguous_dma(reason="small transposed loads"):
                sp.dma_start(c_T[:, :], c.rearrange("b d -> d b")).then_inc(s_mod, 16)
                for i, v in enumerate((log_A, B_b, g1)):
                    sp.dma_start(cols[:, i:i + 1], v.rearrange("(d a) -> d a", a=1)).then_inc(s_w, 16)
            sp.dma_start(w_in[:, 0, :], B_w).then_inc(s_w, 16)
            sp.dma_start(w_in[:, 1, :], C_w).then_inc(s_w, 16)
            for b in range(2):
                load_x(b, b)
            for i, w in enumerate((wq, wk, wv)):
                sp.dma_start(wqkv[:, i, :], w).then_inc(s_w, 16)
            sp.dma_start(wo_s[:, :], wo).then_inc(s_w, 16)
            sp.dma_start(wr_s[:, :], w_router).then_inc(s_w, 16)
            sp.dma_start(g2_b[:, :], g2.partition_broadcast(P)).then_inc(s_w, 16)
            sp.wait_ge(SU["dve"].sem, SU["dve"].at(0, "aug"))
            for p in range(2):
                for dst, src in ((k_stack_d, kaug_b), (q_stack_d, qaug_b)):
                    sp.dma_start(dst[p].rearrange("h (d s) k -> (h d) s k", s=8)[:, AUG:8, :],
                                 src[:, :].rearrange("r (s k) -> r s k", s=2)).then_inc(s_scr, 16)
            sp.dma_start(routed[NE * REG:, :].rearrange("(e p) r -> p e r", p=P), pad_rows[:, NE:, :]).then_inc(s_scr, 16)
            sp.wait_ge(SU["dve"].sem, SU["dve"].at(0, "castb"))
            sp.dma_start(mod_rows, row_s[:, :]).then_inc(s_modrow, 16)

            def gate_load(b, p):
                if old(b, 2):
                    sp.wait_ge(TL["pool"].sem, TL["pool"].at(b - 2, "gh"))
                    alone(sp)
                sp.dma_start(GB[:, p, :], mod_rows[bass.ds(b, 1), M_GB * P:].to_broadcast([P, P])).then_inc(s_gt[p], 16)

            def front_stack(b, p):
                if isinstance(b, int) and b == 0:
                    sp.wait_ge(s_scr, 16 * 5)
                    sp.wait_ge(SU["pool"].sem, SU["pool"].at(0, "kst"))
                if old(b, 2):
                    for half in range(2):
                        sp.wait_ge(s_stk[p][half], 24 * (b - p))
                        alone(sp)
                for i, (e, name) in enumerate((("act", "ph"), ("act", "pm"), ("dve", "pl"))):
                    sp.wait_ge(QK[e].sem, QK[e].at(b, name))
                    alone(sp)
                    for qk_i, (slots, dst) in enumerate(((Q_SLOTS, q_stack_d), (K_SLOTS, k_stack_d))):
                        _, slot, step, n = slots[i]
                        to = dst[p].rearrange("h (d s) k -> (h d) s k", s=8)[:, slot:slot + step * (n - 1) + 1:step, :]
                        sp.dma_start(to, bc(part[:, i, qk_i, :], 1, n)).then_inc(s_stw, 16)
                sp.wait_ge(s_stw, 96 * b + 96)
                alone(sp)
                for half in range(2):
                    h0 = half * H // 2
                    if old(b, 2):
                        sp.wait_ge(AT["pe"].sem, AT["pe"].at(b - 2, f"s{h0 + H // 2 - 1}"))
                        alone(sp)
                    sp.dma_start(QST[:, p, h0 // 2:h0 // 2 + H // 4, :],
                                 q_stack_d[p][h0:h0 + H // 2].rearrange("(t j) r k -> (j r) t k", j=2)
                                 ).then_inc(s_stk[p][half], 16)
                    for j in range(2):
                        sp.dma_start(KST[64 * j:64 * j + 64, p, h0 + j:h0 + H // 2:2, :],
                                     k_stack_d[p][h0:h0 + H // 2].rearrange("(t j) r k -> j r t k", j=2)[j]
                                     ).then_inc(s_stk[p][half], 16)

            def attn_max(a, p):
                sp.wait_ge(MA["act"].sem, MA["act"].at(a, "nmT"))
                alone(sp)
                for j in range(2):
                    for i in range(3):
                        r = 64 * j + 8 * i + AUG
                        sp.dma_start(QST[r:r + 1, p, :, :], nmT[16 * i + j:16 * (i + 1):2, :]).then_inc(s_nm, 16)

            def step(b, p, now):
                if now == WHEN["load"]:
                    front_load(b, p)
                if now == WHEN["stack"]:
                    front_stack(b, p)
                if now == WHEN["max_rows"]:
                    attn_max(b, p)
                if now == WHEN["load_gate"]:
                    gate_load(b, p)

            run_periods(sp, step)

            sp.wait_ge(s_idx, 1)
            alone(sp)
            pad_experts(sp, range(0, NE // 2))

            sp.wait_ge(s_tab, 3)
            alone(sp)
            sp.wait_ge(s_pad, 16 * NE)
            alone(sp)

            def tile_load(T, p):
                row = sp.value_load(tab[0:1, 0, bass.ds(T, 1)], min_val=0, max_val=NROW - P)
                if old(T, 4):
                    sp.wait_ge(moe["pe_xT"], T - 4 + 1)
                    alone(sp)
                    sp.wait_ge(moe["dve_in"], T - 4 + 1)
                    alone(sp)
                sp.dma_start(xin[:, p, :], routed[bass.ds(row, P), :]).then_inc(s_in[p], 16)

            for T in range(4):
                tile_load(T, T)
            with sp.Fori(1, NT // 4) as j:
                for u in range(4):
                    tile_load(4 * j + u, u)
            for T in range(NT // 4 * 4, NT):
                tile_load(T, T % 4)

            def last_load(b, q):
                if old(b, 4):
                    sp.wait_ge(LA.sem, LA.at(b - 4, "sum"))
                    alone(sp)
                sp.dma_start(got[:, q, :, :, :], expert_out[bass.ds(b * 2 * S, 2 * S), :].rearrange(
                    "(t p k) d -> p t k d", t=QB, p=P)).then_inc(s_got[q], 16)

            sp.wait_ge(s_rows, 1)
            alone(sp)
            for b in range(4):
                last_load(b, b)
            with sp.Fori(1, NB // 4) as j:
                for q in range(4):
                    last_load(4 * j + q, q)

        @block.gpsimd
        def _(pool):
            pool.memset(pad_rows[:, :, :], 0.0)
            pool.memset(neg_half[:, :], -0.5)
            pool.memset(qaug_b[:, :], 0.0).then_inc(SU["pool"].sem, 1)
            pool.memset(KST[:, :, :, :], 0.0)
            pool.memset(VA[:, :, :, :, :], 0.0).then_inc(SU["pool"].sem, 1)
            pool.wait_ge(SU["pool"].sem, SU["pool"].at(0, "kst"))
            pool.memset(VA[:, :, :, :, DH:DH + 1], 1.0).then_inc(SU["pool"].sem, 1)

            def rstd(stage, name, dve, src, dst, b):
                pool.wait_ge(dve[0].sem, dve[0].at(b, dve[1]))
                pool.tensor_tensor(dst, src, neg_half[:, :], ALU.pow).then_inc(stage.sem, 1)

            def front(b, p, now):
                if now == WHEN["rstd1"]:
                    rstd(FR["pool"], "rs1", (FR["dve"], "ve"), ve[:, :], rs[:, :], b)
                if now == WHEN["xg"]:
                    pool.wait_ge(s_mb[p], 8 * (b - p) + 16)
                    pool.wait_ge(s_x[p], 8 * (b - p) + 16)
                    if old(b, 1):
                        pool.wait_ge(FR["dve"].sem, FR["dve"].at(b - 1, "x1"))
                    pool.tensor_tensor(xg[:, :, :], X[:, p, :, :], bc(MB[:, p, M_CBGA * P:(M_CBGA + 1) * P], 1, QB),
                                       ALU.add).then_inc(FR["pool"].sem, 1)
                if now == WHEN["rstd2"]:
                    rstd(FR["pool"], "rs2", (FR["dve"], "ve2"), ve[:, :], rs[:, :], b)
                if now == WHEN["rstd3"]:
                    rstd(QK["pool"], "rs3", (QK["dve"], "vs"), ve[:, :], rs[:, :], b)

            def attn_head(a, p, h):
                pool.wait_ge(AT["act"].sem, AT["act"].at(a, f"e{h}"))
                alone(pool)
                d = PT[:, h % 4, :].rearrange("p (x q) -> p x q", x=3)[:, 0:3:2, :]
                pool.affine_select(out=d, in_=d, compare_op=ALU.is_ge, fill=0.0, base=0,
                                   pattern=[[0, 2], [1, P]], channel_multiplier=-1).then_inc(AT["pool"].sem, 1)

            def tail(t, p, now):
                if now == WHEN["base"]:
                    pool.wait_ge(s_gt[p], 8 * (t - p) + 16)
                    pool.wait_ge(TL["dve"].sem, TL["dve"].at(t, "h3"))
                    pool.tensor_tensor(gh[:, :, :], h3[:, :, :], bc(GB[:, p, :], 1, QB),
                                       ALU.mult).then_inc(TL["pool"].sem, 1)
                    pool.wait_ge(TL["pool"].sem, TL["pool"].at(t, "gh"))
                    pool.wait_ge(FR["act"].sem, FR["act"].at(t, "keep"))
                    pool.tensor_tensor(base[:, bass.ds(t * QB, QB), :], gh[:, :, :], base[:, bass.ds(t * QB, QB), :],
                                       ALU.add).then_inc(TL["pool"].sem, 1)
                if now == WHEN["rstd4"]:
                    rstd(TL["pool"], "rs", (TL["dve"], "vs"), ve2[:, :], rs2[:, :], t)

            def scatter(z, p, i, k):
                pool.wait_ge(TL["act"].sem, TL["act"].at(z, "twin"))
                pool.wait_ge(TL["dve"].sem, TL["dve"].at(z, "posi"))
                alone(pool)
                pool.indirect_dma_start(
                    routed[:, :], bass.IndirectOffsetOnAxis(ap=posi[:, p, 2 * i + k:2 * i + k + 1], axis=0),
                    xn2[:, p, i, k, :], None).then_inc(s_sc[p], 16)

            def step(b, p, now):
                for h in heads_at(now):
                    attn_head(b, p, h)
                for n, when in enumerate(WHEN["scatters"]):
                    if now == when:
                        scatter(b, p, *divmod(n, 2))
                tail(b, p, now)
                front(b, p, now)

            run_periods(pool, step)

            for p in range(2):
                pool.wait_ge(s_sc[p], 64 * NB // 2)
            pool.sem_inc(s_tab, 1)
            pool.wait_ge(s_tab, 3)

            def tile_store(T, p):
                pool.wait_ge(moe["dve_eo"], T + 1)
                alone(pool)
                pool.indirect_dma_start(expert_out[:, :], bass.IndirectOffsetOnAxis(ap=dest[:, p:p + 1], axis=0),
                                        eo[:, p, :], None).then_inc(s_st[p], 16)

            with pool.Fori(0, NT // 4) as j:
                for u in range(4):
                    tile_store(4 * j + u, u)
            for T in range(NT // 4 * 4, NT):
                tile_store(T, T % 4)
            for u in range(4):
                pool.wait_ge(s_st[u], 16 * len(range(u, NT, 4)))
            pool.sem_inc(s_rows, 1)

        @block.scalar
        def _(act):
            A, B, C = FR["act"], AT["act"], TL["act"]
            wg_v, wu_v = wg.rearrange("e d h -> d e h"), wu.rearrange("e d h -> d e h")
            ex = experts[:, :].rearrange("p (e n) -> p e n", e=NE)
            act.wait_ge(s_mod, 16 * 3)
            act.activation(c_e[:, :], c_T[:, :], ACT.Exp, scale=-1.0).then_inc(SU["act"].sem, 1)
            act.wait_ge(s_w, 16 * N_W)
            act.activation(decay[:, :], cols[:, 0:1], ACT.Exp, scale=-1.0).then_inc(SU["act"].sem, 1)
            act.wait_ge(SU["dve"].sem, SU["dve"].at(0, "carry"))

            def front(b, p, now):
                if now == WHEN["h"]:
                    act.wait_ge(FR["pe"].sem, FR["pe"].at(b, "nT"))
                    act.activation(hT[:, :], PF[0][:, 0:S], ACT.Identity, scale=modc[:, p, 0:1],
                                   bias=modc[:, p, 1:2]).then_inc(A.sem, 1)
                if now == WHEN["bx"]:
                    act.wait_ge(FR["pe"].sem, FR["pe"].at(b, "bx"))
                    if old(b, 1):
                        act.wait_ge(FR["dve"].sem, FR["dve"].at(b - 1, "scan"))
                    act.activation(bx[:, :], PF[1][:, 0:S], ACT.Identity, bias=cols[:, 1:2]).then_inc(A.sem, 1)
                if now == WHEN["keep"]:
                    act.wait_ge(FR["dve"].sem, FR["dve"].at(b, "x1"))
                    act.activation(base[:, bass.ds(b * QB, QB), :], x1[:, :, :], ACT.Copy).then_inc(A.sem, 1)
                if now == WHEN["squares"]:
                    act.wait_ge(FR["dve"].sem, FR["dve"].at(b, "h2"))
                    for i in range(QB):
                        r = act.activation(sq[:, i, :], H2[:, bass.ds(b * QB + i, 1), :].rearrange("p a d -> p (a d)"), ACT.Square, accum_out=ss[:, i:i + 1])
                    r.then_inc(QK["act"].sem, 1)
                if now == WHEN["xT"]:
                    act.wait_ge(QK["pe"].sem, QK["pe"].at(b, "xnT"))
                    if old(b, 1):
                        act.wait_ge(VS["pe"].sem, VS["pe"].at(b - 1, "v"))
                    act.activation(xnT[:, :], PF[1][:, 0:S], ACT.Copy, scale=cols[:, 2:3]).then_inc(QK["act"].sem, 1)
                if now == WHEN["part0"]:
                    act.wait_ge(QK["dve"].sem, QK["dve"].at(b, "qk"))
                    if old(b, 1):
                        act.wait_ge(s_stw, 96 * b)
                    act.activation(part[:, 0, :, :], qk[:, :, :], ACT.Copy).then_inc(QK["act"].sem, 1)
                if now == WHEN["part1"]:
                    act.wait_ge(QK["dve"].sem, QK["dve"].at(b, "r1"))
                    act.activation(part[:, 1, :, :], qk[:, :, :], ACT.Copy).then_inc(QK["act"].sem, 1)

            def load_experts(e):
                act.dma_start(ex[:, e, 0:HID], wg_v[:, e, :]).then_inc(s_exp, 16)
                act.dma_start(ex[:, e, HID:2 * HID], wu_v[:, e, :]).then_inc(s_exp, 16)
                act.dma_start(ex[:, e, 2 * HID:].rearrange("p (c d) -> p c d", c=HC),
                              wd[e].rearrange("(c p) d -> p c d", p=P)).then_inc(s_exp, 16)

            def values(b, p):
                act.wait_ge(VS["pe"].sem, VS["pe"].at(b, "v"))
                act.activation(vs[:, :, :], PF[0][:, 0:S].rearrange("p (t d) -> p t d", t=QB), ACT.Copy).then_inc(VS["act"].sem, 1)

            def value_heads(b, p):
                act.wait_ge(VS["act"].sem, VS["act"].at(b, "v"))
                if isinstance(b, int) and b == 0:
                    act.wait_ge(SU["pool"].sem, SU["pool"].at(0, "ones"))
                if old(b, 2):
                    act.wait_ge(AT["pe"].sem, AT["pe"].at(b - 2, f"pv{H - 1}"))
                for i in range(QB):
                    r = act.activation(VA[:, p, i, :, 0:DH], vs[:, i, :].rearrange("p (h d) -> p h d", h=H), ACT.Copy)
                r.then_inc(VS["act"].sem, 1)

            def attn_max(a, p):
                act.wait_ge(MA["pe"].sem, MA["pe"].at(a, "nmT"))
                if old(a, 1):
                    act.wait_ge(s_nm, 96 * a)
                act.activation(nmT[:, :], PA_b[0:3 * H, 0:S], ACT.Copy).then_inc(MA["act"].sem, 1)

            def attn_head(a, p, h):
                act.wait_ge(AT["pe"].sem, AT["pe"].at(a, f"s{h}"))
                if h >= 4:
                    act.wait_ge(AT["pe"].sem, AT["pe"].at(a, f"pv{h - 4}"))
                elif old(a, 1):
                    act.wait_ge(AT["pe"].sem, AT["pe"].at(a - 1, f"pv{H - 4 + h}"))
                act.activation(PT[:, h % 4, :], PS[h % 2][:, 0:3 * P], ACT.Exp, scale=SCALE).then_inc(B.sem, 1)

            def tail(t, p, now):
                if now == WHEN["o_copy"]:
                    act.wait_ge(AT["pe"].sem, AT["pe"].at(t, f"pv{H - 1}"))
                    for i in range(2):
                        r = act.activation(OT[:, 2 * i:2 * i + 2, :], PO[i][:, :], ACT.Copy)
                    r.then_inc(C.sem, 1)
                if now == WHEN["onT"]:
                    act.wait_ge(TL["pe"].sem, TL["pe"].at(t, "onT"))
                    act.activation(ONT[:, :], PO[0][:, 0:S], ACT.Copy).then_inc(C.sem, 1)
                if now == WHEN["squares2"]:
                    act.wait_ge(TL["dve"].sem, TL["dve"].at(t, "h3"))
                    for i in range(QB):
                        r = act.activation(sq2[:, i, :], h3[:, i, :], ACT.Square, accum_out=ss2[:, i:i + 1])
                    r.then_inc(C.sem, 1)
                if now == WHEN["x2T"]:
                    act.wait_ge(TL["pe"].sem, TL["pe"].at(t, "xT"))
                    act.activation(xn2T[:, :], PA[1][:, 0:S], ACT.Copy).then_inc(C.sem, 1)
                    act.wait_ge(TL["dve"].sem, TL["dve"].at(t, "xn"))
                    act.activation(xn2[:, p, :, 1, 0:P], xn2[:, p, :, 0, 0:P], ACT.Copy).then_inc(C.sem, 1)
                if now == WHEN["exp_d"]:
                    act.wait_ge(TL["dve"].sem, TL["dve"].at(t, "dl"))
                    act.activation(el[:, :], dl[:, :], ACT.Exp).then_inc(C.sem, 1)

            def step(b, p, now):
                if now == WHEN["v"]:
                    values(b, p)
                if now == WHEN["v_heads"]:
                    value_heads(b, p)
                    if isinstance(b, int) and b < 4:
                        load_experts(2 * b)
                        load_experts(2 * b + 1)
                if now == WHEN["max_T"]:
                    attn_max(b, p)
                for h in heads_at(now):
                    attn_head(b, p, h)
                tail(b, p, now)
                front(b, p, now)

            run_periods(act, step)
            act.wait_ge(TL["dve"].sem, TL["dve"].at(NB - 1, "h3"))
            act.dma_start(gates[:, :, :], mod_rows[:, M_GB * P:].partition_broadcast(P)).then_inc(s_gb, 16)
            act.wait_ge(s_idx, 1)
            alone(act)
            pad_experts(act, range(NE // 2, NE))
            act.activation(warm[:, :], neg_half[:, 0:1], ACT.Silu)

            def tile(T, u, xt=True, gu=True, tr=True, dn=True):
                p = u % 2
                if xt:
                    act.wait_ge(moe["pe_xT"], T + 1 + 1)
                    if old(T, 1):
                        act.wait_ge(moe["pe_gu"], T)
                    act.activation(xT[:, 1 - p, :], PO[0][:, 0:P], ACT.Copy).then_inc(moe["act_xT"], 1)
                if gu:
                    act.wait_ge(moe["pe_gu"], T + 1)
                    if old(T, 2):
                        act.wait_ge(moe["dve_hm"], T - 1)
                    act.activation(sg[:, p, :], PA[p][:, 0:HID], ACT.Silu).then_inc(moe["act_sg"], 1)

            run_tiles(act, tile)

            def last_store(b, p):
                act.wait_ge(LA.sem, LA.at(b, "out"))
                alone(act)
                act.dma_start(out[bass.ds(b, 1), :, :].rearrange("a (t p) d -> p (a t) d", p=P), res[:, p, :, :]).then_inc(s_out[p], 16)

            with act.Fori(0, NB // 2) as j:
                last_store(2 * j, 0)
                last_store(2 * j + 1, 1)
            for p in range(2):
                act.wait_ge(s_out[p], 16 * NB // 2)

        @block.vector
        def _(dve):
            D = SU["dve"]

            def link(ins, stage=D):
                return ins.then_inc(stage.sem, 1)

            def setup_done(name):
                dve.wait_ge(D.sem, D.at(0, name))

            dve.wait_ge(s_cst, 16)
            dve.memset(ones_f[:, :], 1.0)
            dve.memset(nmp[:, :, :, :], 0.0)
            dve.tensor_copy(ident_b[:, :], ident)
            dve.tensor_copy(upper_b[:, :], cst[:, C_UP:C_UP + P])
            dve.tensor_copy(mask_b[:, :, :], bc(cst[:, C_MASK:C_MASK + P], 1, 4))
            dve.memset(ones_b[:, :], 1.0)
            dve.tensor_copy(carry[:, :], cst[:, C_OFF:C_OFF + NE])
            dve.tensor_copy(kaug_b[:, 0:S], cst[:, C_KAUG:C_KAUG + 1].to_broadcast([P, S]))
            dve.memset(kaug_b[:, S:2 * S], 0.0)
            dve.wait_ge(SU["pool"].sem, SU["pool"].at(0, "pads"))
            link(dve.tensor_copy(pad_rows_i[:, :, DST], cst[:, C_JUNK:C_JUNK + 2 * NE]))
            dve.wait_ge(s_mod, 16 * 3)
            dve.wait_ge(SU["act"].sem, SU["act"].at(0, "exp_c"))
            link(dve.tensor_scalar_add(c_e[:, :], c_e[:, :], 1.0))
            setup_done("ec")
            link(dve.reciprocal(c_e[:, :], c_e[:, :]))
            setup_done("rc")
            link(dve.tensor_tensor(silu_T[:, :], c_T[:, :], c_e[:, :], ALU.mult))
            dve.wait_ge(SU["pe"].sem, SU["pe"].at(0, "modT"))
            dve.tensor_copy(mod_T[:, 0, :], PF[1][:, 0:NB])
            link(dve.tensor_scalar_add(mod_T[:, 1, :], PF[1][:, NB:2 * NB], 1.0))
            dve.wait_ge(SU["pe"].sem, SU["pe"].at(0, "modr"))
            dve.tensor_copy(mod_r[:, 0:2 * P], PA[0][0:NB, 0:2 * P])
            link(dve.tensor_copy(mod_r[:, 2 * P:4 * P], PA[1][0:NB, 0:2 * P]))
            setup_done("modr")
            both = mod_r[:, :].rearrange("b (x d) -> b x d", x=4)[:, 0:4:3, :]
            rows = row_s[:, :].rearrange("b (x d) -> b x d", x=5)
            link(dve.tensor_scalar(sgn[:, :, :], both, 0.0, 2.0, ALU.is_ge, ALU.mult))
            setup_done("sgn2")
            link(dve.tensor_scalar(sgn[:, :, :], sgn[:, :, :], 1.0, None, ALU.subtract))
            setup_done("sgn")
            link(dve.tensor_tensor(rows[:, 0:5:4, :], both, sgn[:, :, :], ALU.mult))
            setup_done("abs")
            link(dve.scalar_tensor_tensor(out=rows[:, 0:5:4, :], in0=rows[:, 0:5:4, :], scalar=0.25, in1=sgn[:, :, :],
                                          op0=ALU.max, op1=ALU.mult))
            setup_done("guard")
            dve.tensor_tensor(rows[:, M_CBGA, :], rows[:, M_GA, :], cb_r[:, :], ALU.mult)
            dve.tensor_scalar_add(rows[:, M_CB1, :], mod_r[:, 2 * P:3 * P], 1.0)
            link(dve.tensor_copy(rows[:, M_SB, :], mod_r[:, P:2 * P]))
            dve.wait_ge(s_w, 16 * N_W)
            dve.wait_ge(SU["pe"].sem, SU["pe"].at(0, "bwcw"))
            dve.tensor_copy(bwT[:, :], PF[0][:, 0:P])
            link(dve.tensor_copy(cwT[:, :], PF[0][:, P:2 * P]))
            for i in range(2):
                src = wqkv[:, i, :].rearrange("p (h x d) -> p h x d", h=H, x=2)
                dst = w_rot[:, i, :].rearrange("p (h x d) -> p h x d", h=H, x=2)
                dve.tensor_scalar(dst[:, :, 0, :], src[:, :, 1, :], -1.0, None, ALU.mult)
                r = dve.tensor_copy(dst[:, :, 1, :], src[:, :, 0, :])
            link(r)
            dve.wait_ge(SU["act"].sem, SU["act"].at(0, "exp_a"))
            link(dve.tensor_scalar_add(decay[:, :], decay[:, :], 1.0))
            setup_done("ea")
            link(dve.reciprocal(decay[:, :], decay[:, :]))
            setup_done("decay")
            link(dve.tensor_copy(decay_b[:, :], decay[:, :].to_broadcast([P, S])))
            link(dve.memset(tiny[:, :], 0.0))
            setup_done("carry")

            F, G, B, C = FR["dve"], QK["dve"], MA["dve"], TL["dve"]

            def layernorm_stats(b, src, stage, names):
                for i in range(QB):
                    r = dve.bn_stats(st[:, i, :], src(i))
                link(r, F)
                dve.wait_ge(F.sem, F.at(b, names[0]))
                alone(dve)
                for i in range(QB):
                    r = dve.bn_aggr(mv[:, i, :], st[:, i, :])
                link(r, F)
                dve.wait_ge(F.sem, F.at(b, names[1]))
                link(dve.tensor_scalar_add(ve[:, :], mv[:, :, 1], LN_EPS), F)

            def normalise(dst, src):
                for i in range(QB):
                    r = dve.tensor_scalar(dst[:, i, :], src(i), mv[:, i, 0:1], rs[:, i:i + 1],
                                          ALU.subtract, ALU.mult)
                link(r, F)

            def front(b, p, now):
                if now == WHEN["stats"]:
                    dve.wait_ge(s_x[p], 8 * (b - p) + 16)
                    if old(b, 1):
                        dve.wait_ge(QK["pool"].sem, QK["pool"].at(b - 1, "rs3"))
                    if old(b, 2):
                        dve.wait_ge(FR["act"].sem, FR["act"].at(b - 2, "hT"))
                    dve.tensor_copy(modc[:, p, 0:1], mod_T[:, 1, bass.ds(b, 1)])
                    dve.tensor_copy(modc[:, p, 1:2], mod_T[:, 0, bass.ds(b, 1)])
                    layernorm_stats(b, lambda i: X[:, p, i, :], F, ("st", "mv"))
                if now == WHEN["norm1"]:
                    dve.wait_ge(FR["pool"].sem, FR["pool"].at(b, "rs1"))
                    if old(b, 1):
                        dve.wait_ge(QK["pe"].sem, QK["pe"].at(b - 1, "xnT"))
                    normalise(nrm, lambda i: X[:, p, i, :])
                if now == WHEN["scan"]:
                    dve.wait_ge(FR["act"].sem, FR["act"].at(b, "bx"))
                    if old(b, 1):
                        dve.wait_ge(FR["pe"].sem, FR["pe"].at(b - 1, "y"))
                    link(dve.tensor_tensor_scan(hs[:, :], decay_b[:, :], bx[:, :], 0.0, ALU.mult, ALU.add), F)
                if now == WHEN["x1"]:
                    dve.wait_ge(FR["pe"].sem, FR["pe"].at(b, "y"))
                    dve.wait_ge(s_mb[p], 8 * (b - p) + 16)
                    link(dve.tensor_tensor(tmp[:, :, :], PF[0][:, 0:S].rearrange("p (t d) -> p t d", t=QB),
                                           bc(MB[:, p, 0:P], 1, QB), ALU.mult), F)
                    dve.wait_ge(F.sem, F.at(b, "ty"))
                    dve.wait_ge(FR["pool"].sem, FR["pool"].at(b, "xg"))
                    if old(b, 1):
                        dve.wait_ge(FR["act"].sem, FR["act"].at(b - 1, "keep"))
                    link(dve.tensor_tensor(x1[:, :, :], tmp[:, :, :], xg[:, :, :], ALU.add), F)
                    dve.wait_ge(F.sem, F.at(b, "x1"))
                    layernorm_stats(b, lambda i: x1[:, i, :], F, ("st2", "mv2"))
                if now == WHEN["norm2"]:
                    dve.wait_ge(FR["pool"].sem, FR["pool"].at(b, "rs2"))
                    dve.wait_ge(FR["pe"].sem, FR["pe"].at(b, "nT"))
                    normalise(nrm, lambda i: x1[:, i, :])
                if now == WHEN["h2"]:
                    dve.wait_ge(F.sem, F.at(b, "n2"))
                    link(dve.tensor_tensor(H2[:, bass.ds(b * QB, QB), :], nrm[:, :, :], bc(MB[:, p, M_CB1 * P:(M_CB1 + 1) * P], 1, QB),
                                           ALU.mult), F)
                    dve.wait_ge(F.sem, F.at(b, "h2a"))
                    link(dve.tensor_tensor(H2[:, bass.ds(b * QB, QB), :], H2[:, bass.ds(b * QB, QB), :], bc(MB[:, p, M_SB * P:(M_SB + 1) * P], 1, QB),
                                           ALU.add), F)
                if now == WHEN["mean3"]:
                    dve.wait_ge(QK["act"].sem, QK["act"].at(b, "ss"))
                    link(dve.tensor_scalar(ve[:, :], ss[:, :], 1.0 / P, RMS_EPS, ALU.mult, ALU.add), G)
                if now == WHEN["norm3"]:
                    dve.wait_ge(QK["pool"].sem, QK["pool"].at(b, "rs3"))
                    for i in range(QB):
                        r = dve.tensor_scalar(nrm[:, i, :], H2[:, bass.ds(b * QB + i, 1), :].rearrange("p a d -> p (a d)"), rs[:, i:i + 1], None, ALU.mult)
                    link(r, G)
                if now == WHEN["rope"]:
                    dve.wait_ge(QK["pe"].sem, QK["pe"].at(b, "qk"))
                    two = lambda t: t[:, :].rearrange("p (x k) -> p x k", x=2)
                    link(dve.tensor_tensor(r_c[:, :, :], two(PF[0]), bc(cst[:, C_COS:C_COS + S], 1, 2), ALU.mult), G)
                    link(dve.tensor_tensor(r_s[:, :, :], two(PF[1]), bc(cst[:, C_SIN:C_SIN + S], 1, 2), ALU.mult), G)
                    dve.wait_ge(G.sem, G.at(b, "rs"))
                    link(dve.tensor_tensor(qk[:, :, :], r_c[:, :, :], r_s[:, :, :], ALU.add), G)
                if now == WHEN["rest1"]:
                    dve.wait_ge(QK["act"].sem, QK["act"].at(b, "ph"))
                    link(dve.tensor_tensor(qk[:, :, :], qk[:, :, :], part[:, 0, :, :], ALU.subtract), G)
                if now == WHEN["part2"]:
                    dve.wait_ge(QK["act"].sem, QK["act"].at(b, "pm"))
                    link(dve.tensor_tensor(part[:, 2, :, :], qk[:, :, :], part[:, 1, :, :], ALU.subtract), G)

            def attn_unit(a, p, u):
                g, k = divmod(u, 3)
                dve.wait_ge(MA["pe"].sem, MA["pe"].at(a, f"a{u}"))
                if k == 0:
                    dst, src = MX[:, 0, 4 * g:4 * g + 4], PA[u % 2][:, :].rearrange("p (h k) -> p h k", h=4)
                else:
                    h = 4 * g + 2 * (k - 1)
                    dst, src = MX[:, 1, h:h + 2], PA[u % 2][:, :].rearrange("p (h k) -> p h k", h=2)
                link(dve.tensor_reduce(dst, src, op=ALU.max, axis=AX_X), B)

            def attn_max(a, p):
                dve.wait_ge(B.sem, B.at(a, "m11"))
                if old(a, 1):
                    dve.wait_ge(MA["pe"].sem, MA["pe"].at(a - 1, "nmT"))
                link(dve.tensor_scalar(nmp[:, :, 0, :], MX[:, :, :], -1.0, None, ALU.mult), B)
                dve.wait_ge(B.sem, B.at(a, "nh"))
                link(dve.scalar_tensor_tensor(out=rem[:, :, :], in0=MX[:, :, :], scalar=-1.0, in1=nmp[:, :, 0, :],
                                              op0=ALU.mult, op1=ALU.subtract), B)
                dve.wait_ge(B.sem, B.at(a, "rem"))
                link(dve.tensor_copy(nmp[:, :, 1, :], rem[:, :, :]), B)
                dve.wait_ge(B.sem, B.at(a, "nm"))
                link(dve.tensor_tensor(rem[:, :, :], rem[:, :, :], nmp[:, :, 1, :], ALU.subtract), B)
                dve.wait_ge(B.sem, B.at(a, "rem2"))
                link(dve.tensor_copy(nmp[:, :, 2, :], rem[:, :, :]), B)

            def tail(t, p, now):
                def chain(ins, name):
                    link(ins, C)
                    dve.wait_ge(C.sem, C.at(t, name))

                if now == WHEN["divide"]:
                    dve.wait_ge(TL["pe"].sem, TL["pe"].at(t, "oT"))
                    heads = [PO[i][:, :].rearrange("p (h r) -> p h r", r=32) for i in range(QB)]
                    for i in range(QB):
                        r = dve.reciprocal(rc[:, i, :], heads[i][:, :, DH])
                    chain(r, "rc")
                    for i in range(QB):
                        r = dve.tensor_tensor(ON[:, i, :].rearrange("p (h d) -> p h d", h=H), heads[i][:, :, 0:DH],
                                              bc(rc[:, i, :], 2, DH), ALU.mult)
                    link(r, C)
                if now == WHEN["h3"]:
                    dve.wait_ge(TL["pe"].sem, TL["pe"].at(t, "wo"))
                    link(dve.tensor_tensor(h3[:, :, :], PO[1][:, 0:S].rearrange("p (t d) -> p t d", t=QB),
                                           H2[:, bass.ds(t * QB, QB), :], ALU.add), C)
                if now == WHEN["mean4"]:
                    dve.wait_ge(TL["act"].sem, TL["act"].at(t, "ss"))
                    link(dve.tensor_scalar(ve2[:, :], ss2[:, :], 1.0 / P, RMS_EPS, ALU.mult, ALU.add), C)
                if now == WHEN["x2"]:
                    dve.wait_ge(TL["pool"].sem, TL["pool"].at(t, "rs"))
                    if old(t, 2):
                        dve.wait_ge(s_sc[p], 32 * (t - p))
                    for i in range(QB):
                        r = dve.scalar_tensor_tensor(out=xn2[:, p, i, 0, 0:P], in0=h3[:, i, :], scalar=rs2[:, i:i + 1],
                                                     in1=g2_b[:, :], op0=ALU.mult, op1=ALU.mult)
                    link(r, C)
                if now == WHEN["top2"]:
                    dve.wait_ge(TL["pe"].sem, TL["pe"].at(t, "lg"))
                    chain(dve.tensor_copy(lg[:, :, :], PA[1][:, 0:QB * NE].rearrange("p (t e) -> p t e", t=QB)), "lg")
                    alone(dve)
                    for i in range(QB):
                        r = dve.max(mx8[:, i, :], lg[:, i, :])
                    chain(r, "mx")
                    alone(dve)
                    for i in range(QB):
                        r = dve.max_index(ix8[:, i, :], mx8[:, i, :], lg[:, i, :])
                    chain(r, "ix")
                    chain(dve.tensor_copy(ixf[:, :, :], ix8[:, :, 0:2]), "ixf")
                    chain(dve.tensor_tensor(oh[:, :, :, :], bc(bc(cst[:, C_IOTA:C_IOTA + NE], 1, 2), 1, QB),
                                            bc(ixf[:, :, :], 3, NE), ALU.is_equal), "oh")
                    link(dve.tensor_tensor(ohs[:, :, :], oh[:, :, 0, :], oh[:, :, 1, :], ALU.add), C)
                    link(dve.tensor_tensor(dl[:, :], mx8[:, :, 1], mx8[:, :, 0], ALU.subtract), C)
                if now == WHEN["weights"]:
                    dve.wait_ge(TL["act"].sem, TL["act"].at(t, "el"))
                    chain(dve.tensor_scalar_add(e1[:, :], el[:, :], 1.0), "e1")
                    chain(dve.reciprocal(w12[:, :, 0], e1[:, :]), "w1")
                    chain(dve.tensor_tensor(w12[:, :, 1], w12[:, :, 0], el[:, :], ALU.mult), "w2")
                    dve.tensor_copy(xn2[:, p, :, :, WT], w12[:, :, :])
                    dve.tensor_copy(xn2_i[:, p, :, :, DST],
                                    cst[:, bass.ds(C_DST + t * 4, 4)].rearrange("p (t k) -> p t k", t=QB))
                if now == WHEN["rows"]:
                    dve.wait_ge(TL["pe"].sem, TL["pe"].at(t, "rank"))
                    rk = PA[1][:, 0:3 * NE].rearrange("p (t e) -> p t e", t=3)
                    chain(dve.tensor_tensor(pall[:, :, :], rk[:, 0:QB, :], bc(carry[:, :], 1, QB), ALU.add), "pall")
                    chain(dve.tensor_tensor(carry[:, :], rk[:, QB, :], carry[:, :], ALU.add), "carry")
                    chain(dve.tensor_tensor(prod[:, :, :, :], oh[:, :, :, :], bc(pall[:, :, :], 2, 2), ALU.mult), "prod")
                    chain(dve.tensor_reduce(posf[:, :, :], prod[:, :, :, :], op=ALU.add, axis=AX_X), "posf")
                    link(dve.tensor_copy(posi[:, p, :], posf[:, :, :].rearrange("p t k -> p (t k)")), C)

            def step(b, p, now):
                for u in units_at(now):
                    attn_unit(b, p, u)
                if now == WHEN["max_parts"]:
                    attn_max(b, p)
                tail(b, p, now)
                front(b, p, now)

            run_periods(dve, step)

            R = RT

            def step(ins, name):
                ins.then_inc(R.sem, 1)
                dve.wait_ge(R.sem, R.at(0, name))

            dve.wait_ge(C.sem, C.at(NB - 1, "posi"))
            dve.tensor_copy(endi[:, :], carry[:, :]).then_inc(s_idx, 1)
            step(dve.tensor_tensor(cnt[:, :], carry[:, :], cst[:, C_OFF:C_OFF + NE], ALU.subtract), "cnt")
            step(dve.tensor_scalar(cnt[:, :], cnt[:, :], P / 2 - 0.5, 1.0 / P, ALU.add, ALU.mult), "cnt2")
            step(dve.tensor_copy(cnti[:, :], cnt[:, :]), "cnti")
            step(dve.tensor_copy(cnt[:, :], cnti[:, :]), "nt")
            step(dve.tensor_tensor_scan(cum[:, :], ones_f[:, :], cnt[:, :], 0.0, ALU.mult, ALU.add), "cum")
            tiles = cst[0:1, C_TILE:C_TILE + NT]
            step(dve.tensor_tensor(past[:, :, :], bc(tiles, 2, NE), bc(cum[0:1, :], 1, NT), ALU.is_ge), "past")
            step(dve.tensor_reduce(eidx[:, :], past[:, :, :], op=ALU.add, axis=AX_X), "eidx")
            step(dve.tensor_tensor(past[:, :, :], past[:, :, :], bc(cnt[0:1, :], 1, NT), ALU.mult), "pastn")
            step(dve.tensor_reduce(first[:, :], past[:, :, :], op=ALU.add, axis=AX_X), "first")
            step(dve.tensor_tensor(first[:, :], tiles, first[:, :], ALU.subtract), "inside")
            step(dve.tensor_scalar(first[:, :], first[:, :], float(P), None, ALU.mult), "jrow")
            step(dve.scalar_tensor_tensor(out=first[:, :], in0=eidx[:, :], scalar=float(REG), in1=first[:, :],
                                          op0=ALU.mult, op1=ALU.add), "row")
            step(dve.tensor_scalar(eidx[:, :], eidx[:, :], NE - 1.0, float(EW), ALU.min, ALU.mult), "col")
            dve.tensor_copy(tab[:, 0, :], first[:, :]).then_inc(s_tab, 1)
            dve.tensor_copy(tab[:, 1, :], eidx[:, :]).then_inc(s_tab, 1)

            def tile(T, u, xt=True, gu=True, tr=True, dn=True):
                p = u % 2
                if gu:
                    dve.wait_ge(moe["act_sg"], T + 1)
                    if old(T, 2):
                        dve.wait_ge(moe["pe_tr"], T - 2 + 1)
                    dve.tensor_tensor(hm[:, p, :], PS[p][:, 0:HID], sg[:, p, :], ALU.mult).then_inc(moe["dve_hm"], 1)
                if tr:
                    dve.wait_ge(moe["pe_tr"], T - 1 + 1)
                    if old(T, 3):
                        dve.wait_ge(moe["pe_dn"], T - 2)
                    dve.tensor_copy(hmT[:, 1 - p, :], PF[1 - p][:, 0:HID]).then_inc(moe["dve_hT"], 1)
                if dn:
                    v = (u + 2) % 4
                    dve.wait_ge(moe["pe_dn"], T - 2 + 1)
                    if old(T, 6):
                        dve.wait_ge(s_st[v], 4 * (T - 2 - v))
                    dve.tensor_copy(dest[:, v:v + 1], in_dest[:, v:v + 1])
                    dve.tensor_scalar(eo[:, v, :], PO[1][:, 0:P], in_w[:, v:v + 1], None,
                                      ALU.mult).then_inc(moe["dve_eo"], 1)
                if xt:
                    v = (u + 1) % 4
                    dve.wait_ge(s_in[v], 4 * (T + 1 - v) + 16)
                    dve.tensor_copy(in_w[:, v:v + 1], xin[:, v, WT:WT + 1])
                    dve.tensor_copy(in_dest[:, v:v + 1], xin_i[:, v, DST:DST + 1]).then_inc(moe["dve_in"], 1)

            run_tiles(dve, tile)

            L = LA

            def last(b, q):
                p = q % 2

                def step(ins, name):
                    ins.then_inc(L.sem, 1)
                    dve.wait_ge(L.sem, L.at(b, name))

                dve.wait_ge(s_got[q], 4 * (b - q) + 16)
                if old(b, 2):
                    dve.wait_ge(s_out[p], 8 * (b - p))
                step(dve.tensor_tensor(res[:, p, :, :], got[:, q, :, 0, :], got[:, q, :, 1, :], ALU.add), "sum")
                step(dve.tensor_tensor(res[:, p, :, :], res[:, p, :, :], gates[:, bass.ds(b, 1), :].to_broadcast([P, QB, P]),
                                       ALU.mult), "g")
                dve.tensor_tensor(res[:, p, :, :], res[:, p, :, :], base[:, bass.ds(b * QB, QB), :], ALU.add).then_inc(L.sem, 1)

            dve.wait_ge(s_gb, 16)
            for b in range(4):
                last(b, b)
            with dve.Fori(1, NB // 4) as j:
                for q in range(4):
                    last(4 * j + q, q)

        @block.tensor
        def _(pe):
            mm = nc.tensor.matmul
            transpose = nc.tensor.transpose
            pe.wait_ge(s_cst, 16)
            pe.wait_ge(s_mod, 16 * 3)
            pe.wait_ge(SU["dve"].sem, SU["dve"].at(0, "silu"))
            for i in range(2):
                r = mm(PF[1][:, i * NB:(i + 1) * NB], wmod_s[:, i * P:(i + 1) * P], silu_T[:, :], start=True, stop=True)
            r.then_inc(SU["pe"].sem, 1)
            for i in range(2):
                r = mm(PA[i][0:NB, 0:2 * P], silu_T[:, :], wmod_s[:, (i + 1) * 2 * P:(i + 2) * 2 * P], start=True, stop=True)
            r.then_inc(SU["pe"].sem, 1)
            pe.wait_ge(s_w, 16 * N_W)
            transpose(PF[0][:, 0:P], w_in[:, 0, :], ident)
            transpose(PF[0][:, P:2 * P], w_in[:, 1, :], ident).then_inc(SU["pe"].sem, 1)
            pe.wait_ge(SU["dve"].sem, SU["dve"].at(0, "carry"))
            pe.wait_ge(SU["pool"].sem, SU["pool"].at(0, "ones"))
            A, B, C = FR["pe"], AT["pe"], TL["pe"]

            def front(b, p, now):
                if now == WHEN["T1"]:
                    pe.wait_ge(FR["dve"].sem, FR["dve"].at(b, "n1"))
                    if old(b, 1):
                        pe.wait_ge(VS["act"].sem, VS["act"].at(b - 1, "v"))
                    for i in range(QB):
                        r = transpose(PF[0][:, i * P:(i + 1) * P], nrm[:, i, :], ident)
                    r.then_inc(A.sem, 1)
                if now == WHEN["bx_mm"]:
                    pe.wait_ge(FR["act"].sem, FR["act"].at(b, "hT"))
                    if old(b, 1):
                        pe.wait_ge(QK["dve"].sem, QK["dve"].at(b - 1, "rs"))
                    mm(PF[1][:, 0:S], bwT[:, :], hT[:, :], start=True, stop=True).then_inc(A.sem, 1)
                if now == WHEN["y"]:
                    pe.wait_ge(FR["dve"].sem, FR["dve"].at(b, "scan"))
                    for i in range(QB):
                        r = mm(PF[0][:, i * P:(i + 1) * P], hs[:, i * P:(i + 1) * P], cwT[:, :], start=True, stop=True)
                    r.then_inc(A.sem, 1)
                if now == WHEN["T3"]:
                    pe.wait_ge(QK["dve"].sem, QK["dve"].at(b, "xn"))
                    for i in range(QB):
                        r = transpose(PF[1][:, i * P:(i + 1) * P], nrm[:, i, :], ident)
                    r.then_inc(QK["pe"].sem, 1)
                if now == WHEN["qk"]:
                    pe.wait_ge(QK["act"].sem, QK["act"].at(b, "xnT"))
                    for i in range(2):
                        mm(PF[0][:, i * S:(i + 1) * S], wqkv[:, i, :], xnT[:, :], start=True, stop=True)
                        r = mm(PF[1][:, i * S:(i + 1) * S], w_rot[:, i, :], xnT[:, :], start=True, stop=True)
                    r.then_inc(QK["pe"].sem, 1)

            def values(b, p):
                pe.wait_ge(QK["dve"].sem, QK["dve"].at(b, "rc"))
                for i in range(QB):
                    r = mm(PF[0][:, i * P:(i + 1) * P], xnT[:, i * P:(i + 1) * P], wqkv[:, 2, :], start=True, stop=True)
                r.then_inc(VS["pe"].sem, 1)

            def attn_unit(a, p, u):
                g, k = divmod(u, 3)
                if u == 0:
                    pe.wait_ge(s_stk[p][0], 24 * (a - p) + 48)
                    if old(a, 1):
                        pe.wait_ge(MA["act"].sem, MA["act"].at(a - 1, "nmT"))
                if u == 6:
                    pe.wait_ge(s_stk[p][1], 24 * (a - p) + 48)
                if u == 1 and old(a, LEAD + 1):
                    pe.wait_ge(TL["dve"].sem, TL["dve"].at(a - LEAD - 1, "carry"))
                if u >= 2:
                    pe.wait_ge(MA["dve"].sem, MA["dve"].at(a, f"m{u - 2}"))
                elif old(a, 1):
                    pe.wait_ge(MA["dve"].sem, MA["dve"].at(a - 1, f"m{10 + u}"))
                bank = PA[u % 2]
                if k == 0:
                    heads, n = range(4 * g, 4 * g + 4), P
                else:
                    heads, n = range(4 * g + 2 * (k - 1), 4 * g + 2 * k), S
                q0 = 0 if k == 0 else P
                for i, h in enumerate(heads):
                    mm(bank[:, i * n:(i + 1) * n], QST[:, p, h // 2, q0:q0 + P], KST[:, p, h, 0:n],
                       start=(i == 0), stop=False, skip_group_check=True)
                diag = bank[:, :].rearrange("p (h k) -> p h k", k=n)[:, :, n - P:n]
                mm(diag, ident_b[:, :], mask_b[:, 0:len(heads), :], start=False, stop=True,
                   skip_group_check=True).then_inc(MA["pe"].sem, 1)

            def attn_max(a, p):
                pe.wait_ge(MA["dve"].sem, MA["dve"].at(a, "nl"))
                for i in range(QB):
                    r = transpose(PA_b[:, i * P:(i + 1) * P], nmp[:, i, :, :].rearrange("p x h -> p (x h)"), ident_b[:, :])
                r.then_inc(MA["pe"].sem, 1)

            def attn_scores(a, p, h):
                if h == 0:
                    pe.wait_ge(s_nm, 96 * a + 96)
                if h >= 2:
                    pe.wait_ge(AT["act"].sem, AT["act"].at(a, f"e{h - 2}"))
                elif old(a, 1):
                    pe.wait_ge(AT["act"].sem, AT["act"].at(a - 1, f"e{H - 2 + h}"))
                bank = PS[h % 2]
                mm(bank[:, 0:S], KST[:, p, h, 0:P], QST[:, p, h // 2, :], start=True, stop=True)
                mm(bank[:, S:S + P], KST[:, p, h, P:S], QST[:, p, h // 2, P:S], start=True, stop=True).then_inc(B.sem, 1)

            def attn_pv(a, p, h):
                pe.wait_ge(AT["pool"].sem, AT["pool"].at(a, f"c{h}"))
                if h == 0 and old(a, 1):
                    pe.wait_ge(TL["dve"].sem, TL["dve"].at(a - 1, "h3"))
                g, j = divmod(h, 4)
                o = PO[g // 2][32 * j:32 * j + 32, (g % 2) * S:(g % 2) * S + S]
                mm(o, VA[:, p, 0, h, :], PT[:, h % 4, 0:S], start=True, stop=False)
                mm(o[:, P:S], VA[:, p, 1, h, :], PT[:, h % 4, S:3 * P], start=False, stop=True).then_inc(B.sem, 1)

            def tail(t, p, now):
                if now == WHEN["oT"]:
                    pe.wait_ge(TL["act"].sem, TL["act"].at(t, "OT"))
                    for i in range(QB):
                        for g in range(4):
                            r = transpose(PO[i][:, g * P:(g + 1) * P], OT[:, g, i * P:(i + 1) * P], ident)
                    r.then_inc(C.sem, 1)
                if now == WHEN["T_on"]:
                    pe.wait_ge(TL["dve"].sem, TL["dve"].at(t, "on"))
                    for i in range(QB):
                        r = transpose(PO[0][:, i * P:(i + 1) * P], ON[:, i, :], ident)
                    r.then_inc(C.sem, 1)
                if now == WHEN["wo"]:
                    pe.wait_ge(TL["act"].sem, TL["act"].at(t, "onT"))
                    for i in range(QB):
                        r = mm(PO[1][:, i * P:(i + 1) * P], ONT[:, i * P:(i + 1) * P], wo_s[:, :], start=True, stop=True)
                    r.then_inc(C.sem, 1)
                if now == WHEN["T_x2"]:
                    pe.wait_ge(TL["dve"].sem, TL["dve"].at(t, "xn"))
                    if not isinstance(t, int) or t + LEAD < NB:
                        pe.wait_ge(MA["dve"].sem, MA["dve"].at(t + LEAD, "m11"))
                    for i in range(QB):
                        r = transpose(PA[1][:, i * P:(i + 1) * P], xn2[:, p, i, 0, 0:P], ident)
                    r.then_inc(C.sem, 1)
                if now == WHEN["logits"]:
                    pe.wait_ge(TL["act"].sem, TL["act"].at(t, "xT"))
                    for i in range(QB):
                        r = mm(PA[1][:, i * NE:(i + 1) * NE], xn2T[:, i * P:(i + 1) * P], wr_s[:, :], start=True, stop=True)
                    r.then_inc(C.sem, 1)
                if now == WHEN["rank"]:
                    pe.wait_ge(TL["dve"].sem, TL["dve"].at(t, "ohs"))
                    for i, (o, terms) in enumerate((
                            (0, ((upper_b, 0),)), (1, ((ones_b, 0), (upper_b, 1))), (2, ((ones_b, 0), (ones_b, 1))))):
                        for k, (w, blk) in enumerate(terms):
                            r = mm(PA[1][:, o * NE:(o + 1) * NE], w[:, :], ohs[:, blk, :], start=(k == 0),
                                   stop=(k == len(terms) - 1))
                    r.then_inc(C.sem, 1)

            def step(b, p, now):
                if now == WHEN["v"]:
                    values(b, p)
                for u in units_at(now):
                    attn_unit(b, p, u)
                if now == WHEN["max_T"]:
                    attn_max(b, p)
                for h in heads_at(now):
                    attn_scores(b, p, h)
                for h in heads_at(now - PV_LATER):
                    attn_pv(b, p, h)
                tail(b, p, now)
                front(b, p, now)

            run_periods(pe, step)
            pe.wait_ge(s_tab, 3)
            pe.wait_ge(s_exp, 16 * 3 * NE)
            cols = {}

            def column(T):
                return pe.value_load(tab[0:1, 1, bass.ds(T, 1)], min_val=0, max_val=(NE - 1) * EW)

            def tile(T, u, xt=True, gu=True, tr=True, dn=True):
                p = u % 2
                if gu:
                    col = cols[u] = column(T)
                if xt:
                    v = (u + 1) % 4
                    pe.wait_ge(s_in[v], 4 * (T + 1 - v) + 16)
                    if old(T, 0):
                        pe.wait_ge(moe["act_xT"], T + 1)
                    transpose(PO[0][:, 0:P], xin[:, v, 0:P], ident).then_inc(moe["pe_xT"], 1)
                if gu:
                    pe.wait_ge(moe["act_xT"], T + 1)
                    if old(T, 2):
                        pe.wait_ge(moe["dve_hm"], T - 2 + 1)
                    mm(PA[p][:, 0:HID], xT[:, p, :], experts[:, bass.ds(col, HID)], start=True, stop=True)
                    mm(PS[p][:, 0:HID], xT[:, p, :], experts[:, bass.ds(col + HID, HID)], start=True, stop=True).then_inc(moe["pe_gu"], 1)
                if tr:
                    pe.wait_ge(moe["dve_hm"], T - 1 + 1)
                    if old(T, 3):
                        pe.wait_ge(moe["dve_hT"], T - 2)
                    for c_ in range(HC):
                        r = transpose(PF[1 - p][:, c_ * P:(c_ + 1) * P], hm[:, 1 - p, c_ * P:(c_ + 1) * P], ident)
                    r.then_inc(moe["pe_tr"], 1)
                if dn:
                    pcol = cols[u - 2] if u >= 2 else column(T - 2)
                    pe.wait_ge(moe["dve_hT"], T - 2 + 1)
                    if old(T, 3):
                        pe.wait_ge(moe["dve_eo"], T - 3 + 1)
                    for c_ in range(HC):
                        r = mm(PO[1][:, 0:P], hmT[:, p, c_ * P:(c_ + 1) * P],
                               experts[:, bass.ds(pcol + 2 * HID + c_ * P, P)], start=(c_ == 0), stop=(c_ == HC - 1))
                    r.then_inc(moe["pe_dn"], 1)

            run_tiles(pe, tile)


_INS = ['L0_attn_x', 'L0_attn_log_A', 'L0_attn_B_w', 'L0_attn_B_b', 'L0_attn_C_w', 'L0_attn_C_b', 'L0_ffn_wq',
        'L0_ffn_wk', 'L0_ffn_wv', 'L0_ffn_wo', 'L0_ffn_w_router', 'L0_ffn_wg', 'L0_ffn_wu', 'L0_ffn_wd',
        'L0_ffn_g1', 'L0_ffn_g2', 'L0_c', 'L0_wmod']


def kernel(**inputs):
    import concourse.bacc as _bacc
    from concourse.bass_utils import run_bass_kernel_spmd as _run

    nc = _bacc.Bacc("TRN2", target_bir_lowering=False, num_devices=1)
    arrays, args = {}, []
    for name in _INS:
        a = np.ascontiguousarray(inputs[name])
        arrays[name + "_dram"] = a
        args.append(nc.dram_tensor(name + "_dram", a.shape, mybir.dt.from_np(a.dtype), kind="ExternalInput").ap())
    arrays["consts_dram"] = constants()
    args.append(nc.dram_tensor("consts_dram", [P, C_N], F32, kind="ExternalInput").ap())
    args.append(nc.dram_tensor("out_dram", [NB, S, P], F32, kind="ExternalOutput").ap())
    build(nc, *args)
    r = _run(nc, [arrays], core_ids=[0])
    return r.results[0]["out_dram"]
```
